# Optimizing a Trainium2 kernel written in Bass

```python
import numpy as np
import jax
import jax.numpy as jnp

def _softmax(x, axis=-1):
    return jax.nn.softmax(x, axis=axis)

def _gelu(x):
    return jax.nn.gelu(x, approximate=True)

def _silu(x):
    return jax.nn.silu(x)

def _sigmoid(x):
    return jax.nn.sigmoid(x)

def _layernorm(x, axis=-1, eps=1e-05):
    m = jnp.mean(x, axis=axis, keepdims=True)
    v = jnp.var(x, axis=axis, keepdims=True)
    return (x - m) / jnp.sqrt(v + eps)

def _scatter_add(tgt, idx, src, axis=0):
    return tgt.at[idx].add(src)

def _segment_sum(src, seg, n):
    return jax.ops.segment_sum(src, seg, n)
kernel_name = 'mk_perceiver_d2_seqx_r4_fdfb02'

def setup_inputs(seed: int=0):
    np.random.seed(seed)
    _w = jnp.asarray

    def _rec_inputs():
        import jax
        import jax.numpy as jnp
        _rk = jax.random.key(seed)
        x = 7.22e-05 + 1 * jax.random.normal(jax.random.fold_in(_rk, 1), (2, 256, 256), jnp.float32)
        _lenS = 256 - jax.random.randint(jax.random.fold_in(_rk, 7), (2,), 0, max(1, 256 // 4) + 1, jnp.int32)
        _lenS2 = 4096 - jax.random.randint(jax.random.fold_in(_rk, 8), (2,), 0, max(1, 4096 // 4) + 1, jnp.int32)
        _ctx_1024P = jax.random.normal(jax.random.fold_in(_rk, 11), (2, 16, 256), jnp.float32)
        _ctx_1024c = jax.random.dirichlet(jax.random.fold_in(_rk, 511), 0.3 * jnp.ones((16,), jnp.float32), (2, 4096))
        _ctx_1024t = jnp.einsum('bsk,bkd->bsd', _ctx_1024c, _ctx_1024P)
        _ctx_1024t = _ctx_1024t * jax.lax.rsqrt(jnp.mean(jnp.square(_ctx_1024t)) + 1e-12) * 0.953939
        ctx_1024 = 4.13588e-05 + 0.999923 * (_ctx_1024t + 0.3 * jax.random.normal(jax.random.fold_in(_rk, 611), (2, 4096, 256), jnp.float32))
        _validS = jnp.arange(256)[None, :] < _lenS[:, None]
        _validS2 = jnp.arange(4096)[None, :] < _lenS2[:, None]
        _causal = jnp.tril(jnp.ones((256, 256), dtype=bool))
        mask_1x1xSxS2_if1 = jnp.where(jnp.ones((1, 1, 256, 4096), dtype=bool), 1, 0).astype(jnp.int32)
        mask_SxS2_ff0 = jnp.where(jnp.ones((256, 4096), dtype=bool), 0.0, -1000000000.0).astype(jnp.float32)
        return (x, ctx_1024, mask_1x1xSxS2_if1, mask_SxS2_ff0)
    x, ctx_1024, mask_1x1xSxS2_if1, mask_SxS2_ff0 = _rec_inputs()

    def _L0_xattn_setup():
        import jax, jax.numpy as jnp
        import numpy as np
        B, S, E, H = (4, 512, 256, 16)
        D = E // H
        key = jax.random.key(seed)
        ks = jax.random.split(key, 12)
        scale = 1.0 / np.sqrt(E)
        return {'q_vec': jax.random.normal(ks[0], (B, S, E), jnp.float32), 'k_vec': jax.random.normal(ks[1], (B, S, E), jnp.float32), 'v_vec': jax.random.normal(ks[2], (B, S, E), jnp.float32), 'mask_input': jnp.ones((1, 1, S, S), jnp.int32), 'Wq': jax.random.normal(ks[3], (E, E), jnp.float32) * scale, 'bq': jnp.zeros((E,), jnp.float32), 'Wk': jax.random.normal(ks[4], (E, E), jnp.float32) * scale, 'bk': jnp.zeros((E,), jnp.float32), 'Wv': jax.random.normal(ks[5], (E, E), jnp.float32) * scale, 'bv': jnp.zeros((E,), jnp.float32), 'Wo': jax.random.normal(ks[6], (E, E), jnp.float32) * scale, 'bo': jnp.zeros((E,), jnp.float32)}
    _L0_xattn_all = _L0_xattn_setup()
    _L0_xattn_in = {k: v for k, v in _L0_xattn_all.items() if k in ('Wq', 'bq', 'Wk', 'bk', 'Wv', 'bv', 'Wo', 'bo')}
    del _L0_xattn_all

    def _L0_attn_setup():
        import jax, jax.numpy as jnp
        import numpy as np
        B, L, D = (4, 1024, 256)
        DS, EXP, DC = (16, 2, 4)
        DI = EXP * D
        K_SYM = max(3, 2 * DC + 1)

        def _linear(x, w, b):
            return jnp.einsum('blc,oc->blo', x, w) + b

        def _dwconv(x, kernel, bias, pad_l, pad_r):
            y = jax.lax.conv_general_dilated(x.transpose(0, 2, 1), kernel, window_strides=(1,), padding=[(pad_l, pad_r)], dimension_numbers=('NCH', 'OIH', 'NCH'), feature_group_count=x.shape[-1])
            return y.transpose(0, 2, 1) + bias

        def _rmsnorm(x, w, eps=1e-06):
            scale = jax.lax.rsqrt(jnp.mean(x * x, axis=-1, keepdims=True) + eps)
            return w * x * scale
        key = jax.random.key(seed)
        ks = jax.random.split(key, 12)

        def n(k, shape, s=0.02):
            return jax.random.normal(k, shape, jnp.float32) * s
        return {'x': jax.random.normal(ks[0], (B, L, D), jnp.float32), 'norm_w': jnp.ones((D,), jnp.float32), 'in_w': n(ks[1], (2 * DI, D)), 'in_b': jnp.zeros((2 * DI,), jnp.float32), 'dwa_k': n(ks[2], (DI, 1, DC)), 'dwa_b': jnp.zeros((DI,), jnp.float32), 'A': n(ks[3], (DI, DS)), 'Bm': n(ks[4], (DS, DI)), 'sym_k': n(ks[5], (DI, 1, K_SYM)), 'sym_b': jnp.zeros((DI,), jnp.float32), 'pw_w': n(ks[6], (DI, DI)), 'pw_b': jnp.zeros((DI,), jnp.float32), 'ha_w': n(ks[7], (DI // 2, DI)), 'ha_b': jnp.zeros((DI // 2,), jnp.float32), 'hb_w': n(ks[8], (DI // 2, DI)), 'hb_b': jnp.zeros((DI // 2,), jnp.float32), 'fuse_w': n(ks[9], (DI, DI)), 'fuse_b': jnp.zeros((DI,), jnp.float32), 'out_w': n(ks[10], (D, DI)), 'out_b': jnp.zeros((D,), jnp.float32)}
    _L0_attn_all = _L0_attn_setup()
    _L0_attn_in = {k: v for k, v in _L0_attn_all.items() if k in ('norm_w', 'in_w', 'in_b', 'dwa_k', 'dwa_b', 'A', 'Bm', 'sym_k', 'sym_b', 'pw_w', 'pw_b', 'ha_w', 'ha_b', 'hb_w', 'hb_b', 'fuse_w', 'fuse_b', 'out_w', 'out_b')}
    del _L0_attn_all

    def _L0_ffn_setup():
        import jax, jax.numpy as jnp
        import numpy as np
        LN_EPS = 1e-05

        def layernorm(x, g, b):
            mu = jnp.mean(x, axis=-1, keepdims=True)
            var = jnp.mean((x - mu) ** 2, axis=-1, keepdims=True)
            return (x - mu) * jax.lax.rsqrt(var + LN_EPS) * g + b

        def act_quant_fake(x):
            scale = 127.0 / jnp.clip(jnp.max(jnp.abs(x), axis=-1, keepdims=True), 1e-05)
            return jnp.clip(jnp.round(x * scale), -128.0, 127.0) / scale

        def weight_quant_fake(w):
            scale = 1.0 / jnp.clip(jnp.mean(jnp.abs(w)), 1e-05)
            return jnp.clip(jnp.round(w * scale), -1.0, 1.0) / scale

        def bitlinear(x, w, b):
            dqx = act_quant_fake(x)
            dqw = weight_quant_fake(w)
            return jnp.einsum('btd,hd->bth', dqx, dqw) + b
        key = jax.random.key(seed)
        ks = jax.random.split(key, 5)
        B, T, D, H = (8, 1024, 256, 1024)
        return {'x': jax.random.normal(ks[0], (B, T, D), dtype=jnp.float32), 'ln1_g': jnp.ones((D,), jnp.float32), 'ln1_b': jnp.zeros((D,), jnp.float32), 'w1': jax.random.normal(ks[1], (H, D), dtype=jnp.float32) * (1.0 / np.sqrt(D)), 'b1': jax.random.normal(ks[2], (H,), dtype=jnp.float32) * 0.02, 'ln2_g': jnp.ones((H,), jnp.float32), 'ln2_b': jnp.zeros((H,), jnp.float32), 'w2': jax.random.normal(ks[3], (D, H), dtype=jnp.float32) * (1.0 / np.sqrt(H)), 'b2': jax.random.normal(ks[4], (D,), jnp.float32) * 0.02}
    _L0_ffn_all = _L0_ffn_setup()
    _L0_ffn_in = {k: v for k, v in _L0_ffn_all.items() if k in ('ln1_g', 'ln1_b', 'w1', 'b1', 'ln2_g', 'ln2_b', 'w2', 'b2')}
    del _L0_ffn_all

    def _L1_xattn_setup():
        import jax, jax.numpy as jnp
        import numpy as np
        B, S, D = (8, 512, 256)
        SCALE = float(np.sqrt(D))
        key = jax.random.key(seed)
        ks = jax.random.split(key, 9)
        inv = 1.0 / np.sqrt(D)
        return {'q': jax.random.normal(ks[0], (B, S, D), dtype=jnp.float32), 'k': jax.random.normal(ks[1], (B, S, D), dtype=jnp.float32), 'v': jax.random.normal(ks[2], (B, S, D), dtype=jnp.float32), 'att_mask': jnp.zeros((S, S), dtype=jnp.float32), 'Wq': jax.random.uniform(ks[3], (D, D), jnp.float32, -inv, inv), 'bq': jax.random.uniform(ks[4], (D,), jnp.float32, -inv, inv), 'Wk': jax.random.uniform(ks[5], (D, D), jnp.float32, -inv, inv), 'bk': jax.random.uniform(ks[6], (D,), jnp.float32, -inv, inv), 'Wv': jax.random.uniform(ks[7], (D, D), jnp.float32, -inv, inv), 'bv': jax.random.uniform(ks[8], (D,), jnp.float32, -inv, inv)}
    _L1_xattn_all = _L1_xattn_setup()
    _L1_xattn_in = {k: v for k, v in _L1_xattn_all.items() if k in ('Wq', 'bq', 'Wk', 'bk', 'Wv', 'bv')}
    del _L1_xattn_all

    def _L1_attn_setup():
        import jax, jax.numpy as jnp
        import numpy as np
        B, L, D = (1, 1024, 256)
        N_AR, N_DIFF, D_HEAD = (8, 8, 64)
        H = N_AR + N_DIFF
        ROPE_BASE = 10000.0

        def rotate_half(x):
            x1, x2 = jnp.split(x, 2, axis=-1)
            return jnp.concatenate([-x2, x1], axis=-1)

        def rope_cos_sin(seq_len, d_head):
            inv_freq = 1.0 / ROPE_BASE ** (jnp.arange(0, d_head, 2, dtype=jnp.float32) / d_head)
            t = jnp.arange(seq_len, dtype=jnp.float32)
            freqs = t[:, None] * inv_freq[None, :]
            emb = jnp.concatenate([freqs, freqs], axis=-1)
            return (jnp.cos(emb), jnp.sin(emb))

        def _attend(q, k, v, mask):
            scale = D_HEAD ** (-0.5)
            scores = jnp.einsum('bhqd,bhkd->bhqk', q, k) * scale + mask
            attn = jax.nn.softmax(scores.astype(jnp.float32), axis=-1).astype(q.dtype)
            return jnp.einsum('bhqk,bhkd->bhqd', attn, v)
        key = jax.random.key(seed)
        ks = jax.random.split(key, 5)
        return {'hidden_states': jax.random.normal(ks[0], (B, L, D), dtype=jnp.float32), 'Wq': jax.random.normal(ks[1], (D, H * D_HEAD), dtype=jnp.float32) * 0.02, 'Wk': jax.random.normal(ks[2], (D, H * D_HEAD), dtype=jnp.float32) * 0.02, 'Wv': jax.random.normal(ks[3], (D, H * D_HEAD), dtype=jnp.float32) * 0.02, 'Wo': jax.random.normal(ks[4], (H * D_HEAD, D), dtype=jnp.float32) * 0.02}
    _L1_attn_all = _L1_attn_setup()
    _L1_attn_in = {k: v for k, v in _L1_attn_all.items() if k in ('Wq', 'Wk', 'Wv', 'Wo')}
    del _L1_attn_all

    def _L1_ffn_setup():
        import jax, jax.numpy as jnp
        import numpy as np
        import math
        B, S, H = (8, 1024, 256)
        E, I, K = (8, 512, 2)
        CAP_FACTOR = 1.0

        def _router(x, expert_embeddings):
            dot = jnp.einsum('bsh,eh->bse', x, expert_embeddings)
            n = dot.shape[0] * dot.shape[1]
            dot2 = dot.reshape(n, E)
            vals, idx = jax.lax.top_k(dot2, K)
            rows = jnp.arange(n)[:, None]
            masked = jnp.full_like(dot2, -jnp.inf).at[rows, idx].set(vals)
            return jax.nn.softmax(masked, axis=-1)
        key = jax.random.key(seed)
        k1, k2, k3, k4 = jax.random.split(key, 4)

        def kaiming(k, shape):
            bound = math.sqrt(3.0 / shape[-1])
            return jax.random.uniform(k, shape, jnp.float32, -bound, bound)
        x = jax.random.normal(k1, (B, S, H), jnp.float32)
        expert_embeddings = kaiming(k2, (E, H))
        first_linear = kaiming(k3, (E, I, H))
        second_linear = kaiming(k4, (E, H, I))
        return {'x': x, 'expert_embeddings': expert_embeddings, 'first_linear': first_linear, 'second_linear': second_linear}
    _L1_ffn_all = _L1_ffn_setup()
    _L1_ffn_in = {k: v for k, v in _L1_ffn_all.items() if k in ('expert_embeddings', 'first_linear', 'second_linear')}
    del _L1_ffn_all
    return {'x': x, 'ctx_1024': ctx_1024, 'mask_1x1xSxS2_if1': mask_1x1xSxS2_if1, 'mask_SxS2_ff0': mask_SxS2_ff0, 'L0_xattn_Wq': _L0_xattn_in['Wq'], 'L0_xattn_bq': _L0_xattn_in['bq'], 'L0_xattn_Wk': _L0_xattn_in['Wk'], 'L0_xattn_bk': _L0_xattn_in['bk'], 'L0_xattn_Wv': _L0_xattn_in['Wv'], 'L0_xattn_bv': _L0_xattn_in['bv'], 'L0_xattn_Wo': _L0_xattn_in['Wo'], 'L0_xattn_bo': _L0_xattn_in['bo'], 'L0_attn_norm_w': _L0_attn_in['norm_w'], 'L0_attn_in_w': _L0_attn_in['in_w'], 'L0_attn_in_b': _L0_attn_in['in_b'], 'L0_attn_dwa_k': _L0_attn_in['dwa_k'], 'L0_attn_dwa_b': _L0_attn_in['dwa_b'], 'L0_attn_A': _L0_attn_in['A'], 'L0_attn_Bm': _L0_attn_in['Bm'], 'L0_attn_sym_k': _L0_attn_in['sym_k'], 'L0_attn_sym_b': _L0_attn_in['sym_b'], 'L0_attn_pw_w': _L0_attn_in['pw_w'], 'L0_attn_pw_b': _L0_attn_in['pw_b'], 'L0_attn_ha_w': _L0_attn_in['ha_w'], 'L0_attn_ha_b': _L0_attn_in['ha_b'], 'L0_attn_hb_w': _L0_attn_in['hb_w'], 'L0_attn_hb_b': _L0_attn_in['hb_b'], 'L0_attn_fuse_w': _L0_attn_in['fuse_w'], 'L0_attn_fuse_b': _L0_attn_in['fuse_b'], 'L0_attn_out_w': _L0_attn_in['out_w'], 'L0_attn_out_b': _L0_attn_in['out_b'], 'L0_ffn_ln1_g': _L0_ffn_in['ln1_g'], 'L0_ffn_ln1_b': _L0_ffn_in['ln1_b'], 'L0_ffn_w1': _L0_ffn_in['w1'], 'L0_ffn_b1': _L0_ffn_in['b1'], 'L0_ffn_ln2_g': _L0_ffn_in['ln2_g'], 'L0_ffn_ln2_b': _L0_ffn_in['ln2_b'], 'L0_ffn_w2': _L0_ffn_in['w2'], 'L0_ffn_b2': _L0_ffn_in['b2'], 'L1_xattn_Wq': _L1_xattn_in['Wq'], 'L1_xattn_bq': _L1_xattn_in['bq'], 'L1_xattn_Wk': _L1_xattn_in['Wk'], 'L1_xattn_bk': _L1_xattn_in['bk'], 'L1_xattn_Wv': _L1_xattn_in['Wv'], 'L1_xattn_bv': _L1_xattn_in['bv'], 'L1_attn_Wq': _L1_attn_in['Wq'], 'L1_attn_Wk': _L1_attn_in['Wk'], 'L1_attn_Wv': _L1_attn_in['Wv'], 'L1_attn_Wo': _L1_attn_in['Wo'], 'L1_ffn_expert_embeddings': _L1_ffn_in['expert_embeddings'], 'L1_ffn_first_linear': _L1_ffn_in['first_linear'], 'L1_ffn_second_linear': _L1_ffn_in['second_linear']}

def reference(x, ctx_1024, mask_1x1xSxS2_if1, mask_SxS2_ff0, L0_xattn_Wq, L0_xattn_bq, L0_xattn_Wk, L0_xattn_bk, L0_xattn_Wv, L0_xattn_bv, L0_xattn_Wo, L0_xattn_bo, L0_attn_norm_w, L0_attn_in_w, L0_attn_in_b, L0_attn_dwa_k, L0_attn_dwa_b, L0_attn_A, L0_attn_Bm, L0_attn_sym_k, L0_attn_sym_b, L0_attn_pw_w, L0_attn_pw_b, L0_attn_ha_w, L0_attn_ha_b, L0_attn_hb_w, L0_attn_hb_b, L0_attn_fuse_w, L0_attn_fuse_b, L0_attn_out_w, L0_attn_out_b, L0_ffn_ln1_g, L0_ffn_ln1_b, L0_ffn_w1, L0_ffn_b1, L0_ffn_ln2_g, L0_ffn_ln2_b, L0_ffn_w2, L0_ffn_b2, L1_xattn_Wq, L1_xattn_bq, L1_xattn_Wk, L1_xattn_bk, L1_xattn_Wv, L1_xattn_bv, L1_attn_Wq, L1_attn_Wk, L1_attn_Wv, L1_attn_Wo, L1_ffn_expert_embeddings, L1_ffn_first_linear, L1_ffn_second_linear):
    import jax
    import jax.numpy as jnp

    def _L0_xattn_ref(q_vec, k_vec, v_vec, mask_input, Wq, bq, Wk, bk, Wv, bv, Wo, bo):
        import jax, jax.numpy as jnp
        import numpy as np
        B, S, E, H = (4, 512, 256, 16)
        D = E // H

        def proj(x, W, b):
            y = jnp.einsum('bse,fe->bsf', x, W) + b
            return y.reshape(x.shape[0], -1, H, D).transpose(0, 2, 1, 3)
        q = proj(q_vec, Wq, bq)
        k = proj(k_vec, Wk, bk)
        v = proj(v_vec, Wv, bv)
        energy = jnp.einsum('bhqd,bhkd->bhqk', q, k) / jnp.sqrt(jnp.float32(D))
        energy = jnp.where(mask_input == 0, jnp.float32(-1000000000.0), energy)
        attn = jax.nn.softmax(energy, axis=-1)
        context = jnp.einsum('bhqk,bhkd->bhqd', attn, v)
        context = context.transpose(0, 2, 1, 3).reshape(q_vec.shape[0], -1, E)
        return jnp.einsum('bse,fe->bsf', context, Wo) + bo

    def _L0_attn_ref(x, norm_w, in_w, in_b, dwa_k, dwa_b, A, Bm, sym_k, sym_b, pw_w, pw_b, ha_w, ha_b, hb_w, hb_b, fuse_w, fuse_b, out_w, out_b):
        import jax, jax.numpy as jnp
        import numpy as np
        B, L, D = (4, 1024, 256)
        DS, EXP, DC = (16, 2, 4)
        DI = EXP * D
        K_SYM = max(3, 2 * DC + 1)

        def _linear(x, w, b):
            return jnp.einsum('blc,oc->blo', x, w) + b

        def _dwconv(x, kernel, bias, pad_l, pad_r):
            y = jax.lax.conv_general_dilated(x.transpose(0, 2, 1), kernel, window_strides=(1,), padding=[(pad_l, pad_r)], dimension_numbers=('NCH', 'OIH', 'NCH'), feature_group_count=x.shape[-1])
            return y.transpose(0, 2, 1) + bias

        def _rmsnorm(x, w, eps=1e-06):
            scale = jax.lax.rsqrt(jnp.mean(x * x, axis=-1, keepdims=True) + eps)
            return w * x * scale
        residual = x
        h = _rmsnorm(x, norm_w)
        h = _linear(h, in_w, in_b)
        gate, val = (h[..., :DI], h[..., DI:])
        gate = jax.nn.sigmoid(gate)
        a = _dwconv(val, dwa_k, dwa_b, 1, 2)
        a = jnp.einsum('bld,ds->bls', a, A)
        a = jnp.einsum('bls,sd->bld', a, Bm)
        b = _dwconv(val, sym_k, sym_b, K_SYM // 2, K_SYM // 2)
        b = jax.nn.silu(b)
        b = _linear(b, pw_w, pw_b)
        a = _linear(a, ha_w, ha_b)
        b = _linear(b, hb_w, hb_b)
        y = jnp.concatenate([a, b], axis=-1)
        y = _linear(y, fuse_w, fuse_b)
        y = gate * y
        y = _linear(y, out_w, out_b)
        return residual + y

    def _L0_ffn_ref(x, ln1_g, ln1_b, w1, b1, ln2_g, ln2_b, w2, b2):
        import jax, jax.numpy as jnp
        import numpy as np
        LN_EPS = 1e-05

        def layernorm(x, g, b):
            mu = jnp.mean(x, axis=-1, keepdims=True)
            var = jnp.mean((x - mu) ** 2, axis=-1, keepdims=True)
            return (x - mu) * jax.lax.rsqrt(var + LN_EPS) * g + b

        def act_quant_fake(x):
            scale = 127.0 / jnp.clip(jnp.max(jnp.abs(x), axis=-1, keepdims=True), 1e-05)
            return jnp.clip(jnp.round(x * scale), -128.0, 127.0) / scale

        def weight_quant_fake(w):
            scale = 1.0 / jnp.clip(jnp.mean(jnp.abs(w)), 1e-05)
            return jnp.clip(jnp.round(w * scale), -1.0, 1.0) / scale

        def bitlinear(x, w, b):
            dqx = act_quant_fake(x)
            dqw = weight_quant_fake(w)
            return jnp.einsum('btd,hd->bth', dqx, dqw) + b
        h = layernorm(x, ln1_g, ln1_b)
        h = bitlinear(h, w1, b1)
        h = jax.nn.gelu(h, approximate=False)
        h = layernorm(h, ln2_g, ln2_b)
        h = bitlinear(h, w2, b2)
        return h

    def _L1_xattn_ref(q, k, v, att_mask, Wq, bq, Wk, bk, Wv, bv):
        import jax, jax.numpy as jnp
        import numpy as np
        B, S, D = (8, 512, 256)
        SCALE = float(np.sqrt(D))
        wq = jnp.einsum('bsd,ed->bse', q, Wq) + bq
        wk = jnp.einsum('bsd,ed->bse', k, Wk) + bk
        wv = jnp.einsum('bsd,ed->bse', v, Wv) + bv
        att_score = jnp.einsum('bqd,bkd->bqk', wq, wk) / SCALE + att_mask
        att_weight = jax.nn.softmax(att_score, axis=-1)
        return jnp.einsum('bqk,bkd->bqd', att_weight, wv)

    def _L1_attn_ref(hidden_states, Wq, Wk, Wv, Wo):
        import jax, jax.numpy as jnp
        import numpy as np
        B, L, D = (1, 1024, 256)
        N_AR, N_DIFF, D_HEAD = (8, 8, 64)
        H = N_AR + N_DIFF
        ROPE_BASE = 10000.0

        def rotate_half(x):
            x1, x2 = jnp.split(x, 2, axis=-1)
            return jnp.concatenate([-x2, x1], axis=-1)

        def rope_cos_sin(seq_len, d_head):
            inv_freq = 1.0 / ROPE_BASE ** (jnp.arange(0, d_head, 2, dtype=jnp.float32) / d_head)
            t = jnp.arange(seq_len, dtype=jnp.float32)
            freqs = t[:, None] * inv_freq[None, :]
            emb = jnp.concatenate([freqs, freqs], axis=-1)
            return (jnp.cos(emb), jnp.sin(emb))

        def _attend(q, k, v, mask):
            scale = D_HEAD ** (-0.5)
            scores = jnp.einsum('bhqd,bhkd->bhqk', q, k) * scale + mask
            attn = jax.nn.softmax(scores.astype(jnp.float32), axis=-1).astype(q.dtype)
            return jnp.einsum('bhqk,bhkd->bhqd', attn, v)
        b, l, _ = hidden_states.shape

        def heads(x, W):
            return (x @ W).reshape(b, l, H, D_HEAD).transpose(0, 2, 1, 3)
        q = heads(hidden_states, Wq)
        k = heads(hidden_states, Wk)
        v = heads(hidden_states, Wv)
        cos, sin = rope_cos_sin(l, D_HEAD)
        q = q * cos + rotate_half(q) * sin
        k = k * cos + rotate_half(k) * sin
        neg_inf = jnp.finfo(jnp.float32).min
        causal = jnp.where(jnp.tril(jnp.ones((l, l), dtype=bool)), 0.0, -jnp.inf).astype(jnp.float32)
        out_ar = _attend(q[:, :N_AR], k[:, :N_AR], v[:, :N_AR], causal)
        out_diff = _attend(q[:, N_AR:], k[:, N_AR:], v[:, N_AR:], jnp.zeros((l, l), jnp.float32))
        out = jnp.concatenate([out_ar, out_diff], axis=1)
        out = out.transpose(0, 2, 1, 3).reshape(b, l, H * D_HEAD)
        return out @ Wo

    def _L1_ffn_ref(x, expert_embeddings, first_linear, second_linear):
        import jax, jax.numpy as jnp
        import numpy as np
        import math
        B, S, H = (8, 1024, 256)
        E, I, K = (8, 512, 2)
        CAP_FACTOR = 1.0

        def _router(x, expert_embeddings):
            dot = jnp.einsum('bsh,eh->bse', x, expert_embeddings)
            n = dot.shape[0] * dot.shape[1]
            dot2 = dot.reshape(n, E)
            vals, idx = jax.lax.top_k(dot2, K)
            rows = jnp.arange(n)[:, None]
            masked = jnp.full_like(dot2, -jnp.inf).at[rows, idx].set(vals)
            return jax.nn.softmax(masked, axis=-1)
        batch, seq, hidden = x.shape
        n_tokens = batch * seq
        expert_capacity = math.ceil(n_tokens / E * CAP_FACTOR)
        weights = _router(x, expert_embeddings)
        ones = (weights > 0).astype(weights.dtype)
        cap_ones = jnp.where(jnp.cumsum(ones, axis=0) <= expert_capacity, ones, 0.0)
        caw = weights * cap_ones
        vals, idx = jax.lax.top_k(caw.T, expert_capacity)
        index = idx.reshape(-1)
        x_flat = x.reshape(n_tokens, hidden)
        tokens = x_flat[index].reshape(E, expert_capacity, hidden)
        inter = jax.nn.relu(jnp.einsum('ech,eih->eci', tokens, first_linear))
        out = jnp.einsum('eci,ehi->ech', inter, second_linear)
        out = out * vals[:, :, None]
        final = jnp.zeros((n_tokens, hidden), x.dtype).at[index].add(out.reshape(-1, hidden))
        return final.reshape(x.shape)
    x = x + _L0_xattn_ref(_layernorm(x, axis=-1), ctx_1024, ctx_1024, mask_1x1xSxS2_if1, L0_xattn_Wq, L0_xattn_bq, L0_xattn_Wk, L0_xattn_bk, L0_xattn_Wv, L0_xattn_bv, L0_xattn_Wo, L0_xattn_bo)
    x = x + _L0_attn_ref(_layernorm(x, axis=-1), L0_attn_norm_w, L0_attn_in_w, L0_attn_in_b, L0_attn_dwa_k, L0_attn_dwa_b, L0_attn_A, L0_attn_Bm, L0_attn_sym_k, L0_attn_sym_b, L0_attn_pw_w, L0_attn_pw_b, L0_attn_ha_w, L0_attn_ha_b, L0_attn_hb_w, L0_attn_hb_b, L0_attn_fuse_w, L0_attn_fuse_b, L0_attn_out_w, L0_attn_out_b)
    x = x + _L0_ffn_ref(_layernorm(x, axis=-1), L0_ffn_ln1_g, L0_ffn_ln1_b, L0_ffn_w1, L0_ffn_b1, L0_ffn_ln2_g, L0_ffn_ln2_b, L0_ffn_w2, L0_ffn_b2)
    x = x + _L1_xattn_ref(_layernorm(x, axis=-1), ctx_1024, ctx_1024, mask_SxS2_ff0, L1_xattn_Wq, L1_xattn_bq, L1_xattn_Wk, L1_xattn_bk, L1_xattn_Wv, L1_xattn_bv)
    x = x + _L1_attn_ref(_layernorm(x, axis=-1), L1_attn_Wq, L1_attn_Wk, L1_attn_Wv, L1_attn_Wo)
    x = x + _L1_ffn_ref(_layernorm(x, axis=-1), L1_ffn_expert_embeddings, L1_ffn_first_linear, L1_ffn_second_linear)
    return x

_drawn_inputs = setup_inputs


def setup_inputs(seed=0):
    import zlib

    import numpy as np

    out = dict(_drawn_inputs(seed))
    spreads = {'mask_SxS2_ff0': (0.0, 2.0),
     'L0_xattn_bq': (0.0, 0.284),
     'L0_xattn_bk': (0.0, 2.0),
     'L0_xattn_bv': (0.0, 0.1),
     'L0_xattn_bo': (0.0, 0.1),
     'L0_attn_norm_w': (1.0, 0.6),
     'L0_attn_in_b': (0.0, 0.577),
     'L0_attn_dwa_b': (0.0, 0.8),
     'L0_attn_sym_b': (0.0, 0.8),
     'L0_attn_pw_b': (0.0, 0.57),
     'L0_attn_ha_b': (0.0, 0.432),
     'L0_attn_hb_b': (0.0, 0.469),
     'L0_attn_fuse_b': (0.0, 0.929),
     'L0_attn_out_b': (0.0, 0.298),
     'L0_ffn_ln1_g': (1.0, 0.2),
     'L0_ffn_ln1_b': (0.0, 0.335),
     'L0_ffn_ln2_g': (1.0, 0.2),
     'L0_ffn_ln2_b': (0.0, 0.394)}
    factors = {'L0_attn_in_w': 4.45,
     'L0_attn_dwa_k': 8.0,
     'L0_attn_A': 8.0,
     'L0_attn_Bm': 8.0,
     'L0_attn_sym_k': 8.0,
     'L0_attn_pw_w': 8.0,
     'L0_attn_ha_w': 8.0,
     'L0_attn_hb_w': 6.718,
     'L0_attn_fuse_w': 3.796,
     'L0_ffn_b1': 9.876,
     'L0_ffn_b2': 9.796,
     'L1_xattn_bq': 64.0,
     'L1_xattn_bk': 64.0,
     'L1_xattn_bv': 2.771,
     'L1_attn_Wq': 8.0,
     'L1_attn_Wk': 8.0,
     'L1_xattn_Wq': 7.024,
     'L1_xattn_Wk': 6.136}
    for name, (base, spread) in spreads.items():
        noise = np.random.default_rng([zlib.crc32(name.encode()), seed]).standard_normal(out[name].shape)
        drawn = base * np.exp(spread * noise) if base else spread * noise
        out[name] = jnp.asarray(drawn.astype(out[name].dtype))
    for name, factor in factors.items():
        out[name] = (out[name] * factor).astype(out[name].dtype)
    return out
```

```python
from contextlib import ExitStack

import numpy as np

import concourse.bass as bass
from concourse import mybir

F32 = mybir.dt.float32
BF16 = mybir.dt.bfloat16
I32 = mybir.dt.int32
ALU = mybir.AluOpType
ACT = mybir.ActivationFunctionType
AX = mybir.AxisListType

P = 128
B, S, S2, D = 2, 256, 4096, 256
T = B * S
TT = T // P
CT = D // P
H, DH = 16, 16
G = 4
GPB = H // G
NG = B * GPB
KC = S2 // P
CH = 512
NCH = S2 // CH
ROWS = 6 * DH
KROWS = ROWS + 3
VW = DH + 1
MASKED = -(2.0 ** 100)
K_PARTS = (0, 0, 0, 1, 1, 2)
Q_PARTS = (0, 1, 2, 0, 1, 0)

DI = 512
IT = DI // P
DS = 16
TAPS_A, LEFT_A = 4, 1
TAPS_B, LEFT_B = 9, 4
PAD = S + 8
FF = 1024
FT = FF // P
HM, DM = 16, 64
HALF = HM * DM // 2
E, EI, CAP = 8, 512, T // 8
ROUND = 1.5 * 2.0 ** 23

COLS = {"bq": 2, "bk": 2, "in_b": 8, "dwa_b": 4, "sym_b": 4, "pw_b": 4, "ha_b": 2, "hb_b": 2,
        "fuse_b": 4, "norm_w": 2, "dwa_k": 16, "sym_k": 36, "bq1": 2, "bk1": 2}
ROW_NAMES = {"bo": 256, "out_b": 256, "g1": 256, "b1": 256, "w1b": 1024, "g2": 1024, "b2": 1024,
             "w2b": 256, "bv": 256, "bv1": 256}
CONSTS = {"upper": P, "slots": CAP, "experts": E, "cos": 2 * DM, "sin": 2 * DM, "causal": 2 * S}


def offsets(sizes):
    at, out = 0, {}
    for name, n in sizes.items():
        out[name] = at
        at += n
    return out, at


COL_AT, N_COLS = offsets(COLS)
ROW_AT, N_ROWS = offsets(ROW_NAMES)
CONST_AT, N_CONSTS = offsets(CONSTS)
N_FFN_ROWS = ROW_AT["bv"]


def build(nc, t):
    ctx = ExitStack()
    with ctx:
        arena = ctx.enter_context(nc.sbuf_tensor("arena", [P, 53120], F32))
        psum = ctx.enter_context(nc.psum_tensor("psum", [P, 8, 512], F32))

        def sem(name):
            return ctx.enter_context(nc.semaphore(name))

        def f32(at, n):
            return arena[:, at:at + n]

        def b16(at, n):
            return arena[:, at:at + n // 2].bitcast(BF16)

        KST = [b16(8192 * i, 16384).rearrange("p (j n) -> p j n", j=G) for i in range(3)]
        V_AT = 24576
        V = f32(V_AT, KC * H * VW).rearrange("p (k h e) -> p k h e", k=KC, h=H)
        V_flat = f32(V_AT, KC * H * VW + 16)
        MASKB = b16(33296, 8192).rearrange("p (t n) -> p t n", t=2)
        QST = b16(37392, 8192).rearrange("p (h n) -> p h n", h=H)
        PR = [f32(41488 + 1024 * i, 1024) for i in range(2)]
        CTX = [f32(43536 + 1024 * i, 1024).rearrange("p (c n) -> p c n", c=CT) for i in range(2)]
        K32 = [f32(45584 + 512 * i, 512) for i in range(2)]
        KPT = [b16(46608 + 768 * i, 1536).rearrange("p (r n) -> p r n", r=3) for i in range(2)]
        X = f32(48144, 1024).rearrange("p (t c) -> p t c", t=TT)
        PVS = f32(49168, 256)
        CTXN = f32(49424, 1024).rearrange("p (t c) -> p t c", t=TT)
        at = 50448
        IDENT = f32(at, 128); at += 128
        IDENTB = b16(at, 128); at += 64
        COLT = f32(at, N_COLS); at += N_COLS
        BV = f32(at, 256); at += 256
        MX = [f32(at + 64 * i, 64) for i in range(2)]; at += 128
        M8 = f32(at, 8); at += 8
        MR = f32(at, 8); at += 8
        MPART = b16(at, 24).rearrange("p (m r) -> p m r", r=3); at += 12
        RINV = f32(at, 8).rearrange("p (t j) -> p t j", t=2); at += 8
        BN = f32(at, 48); at += 48
        MV = f32(at, 8); at += 8
        SD = f32(at, 8); at += 8
        FLAGF = f32(at, 4); at += 4
        VS = [f32(at + 84 * i, 84) for i in range(4)]; at += 336
        FLAG = arena[0:1, at:at + 1].bitcast(I32); at += 1
        ONES = f32(at, 128); at += 128
        AW = f32(at, IT * DS).rearrange("p (t s) -> p t s", t=IT); at += IT * DS
        assert at <= 52096, at
        MASKI = arena[:, 16384:16384 + 8192].bitcast(I32).rearrange("p (t n) -> p t n", t=2)
        HN = f32(41488, 1024).rearrange("p (t c) -> p t c", t=TT)
        HT = f32(42512, 1024).rearrange("p (c n) -> p c n", c=CT)
        WQ = f32(8192, 512).rearrange("p (c f) -> p c f", c=CT)
        WK = f32(52096, 512).rearrange("p (c f) -> p c f", c=CT)
        WV = f32(52608, 512).rearrange("p (c f) -> p c f", c=CT)

        def col(name, i):
            return COLT[:, COL_AT[name] + i:COL_AT[name] + i + 1]

        def ST(i):
            return psum[:, 2 * i:2 * i + 2, :]

        def SP_(i):
            return psum[:, 4 + i, :]

        PV = psum[:, 6, 0:256]
        PX = psum[:, 7, :]

        ROWS_T = f32(0, N_FFN_ROWS)

        def row(name):
            return ROWS_T[:, ROW_AT[name]:ROW_AT[name] + ROW_NAMES[name]]

        WO = f32(4352, 512).rearrange("p (c f) -> p c f", c=CT)
        WOUT = f32(4864, 1024).rearrange("p (t f) -> p t f", t=IT)
        TW1 = b16(5888, 2048).rearrange("p (c f) -> p c f", c=CT)
        TW2 = b16(6912, 2048).rearrange("p (t f) -> p t f", t=FT)
        WIN = f32(16384, 2048).rearrange("p (c f) -> p c f", c=CT)
        WPW = f32(18432, 2048).rearrange("p (t f) -> p t f", t=IT)
        WHA = f32(20480, 1024).rearrange("p (t f) -> p t f", t=IT)
        WHB = f32(21504, 1024).rearrange("p (t f) -> p t f", t=IT)
        WFU = f32(22528, 2048).rearrange("p (t f) -> p t f", t=IT)
        W1RAW = f32(43536, 2048)
        W2RAW = f32(45584, 2048)
        BM = f32(47632, 512)
        HL = f32(24576, 1024).rearrange("p (t c) -> p t c", t=TT)
        HS = f32(25600, 1024).rearrange("p (t c) -> p t c", t=TT)
        HTC = f32(26624, 1024).rearrange("p (c n) -> p c n", c=CT)
        GATE = f32(27648, 2048).rearrange("p (m n) -> p m n", m=IT)
        VAL = f32(29696, IT * B * PAD).rearrange("p (m b n) -> p m b n", m=IT, b=B)
        AWK = f32(31808, IT * TAPS_A * 32).rearrange("p (m k s) -> p m k s", m=IT, k=TAPS_A)
        CB = f32(33856, 2048).rearrange("p (m n) -> p m n", m=IT)
        SB = f32(35904, 2048).rearrange("p (m n) -> p m n", m=IT)
        PWO = f32(37952, 2048).rearrange("p (m n) -> p m n", m=IT)
        AS = f32(40000, 512)
        AB = f32(40512, 2048).rearrange("p (m n) -> p m n", m=IT)
        YC = f32(31808, 2048).rearrange("p (m n) -> p m n", m=IT)
        YG = CB
        HQ = b16(25600, 1024).rearrange("p (t c) -> p t c", t=TT)
        HQT = b16(26112, 1024).rearrange("p (c n) -> p c n", c=CT)
        UH = f32(26624, 4096).rearrange("p (t f) -> p t f", t=TT)
        QH = b16(30720, 4096).rearrange("p (t f) -> p t f", t=TT)
        QHT = b16(32768, 4096).rearrange("p (k n) -> p k n", k=FT)
        CTXT = [f32(8192, 8192).rearrange("p (c n) -> p c n", c=CT), f32(0, 8192).rearrange("p (c n) -> p c n", c=CT)]
        CTXK = [f32(16384, 8192).rearrange("p (k c) -> p k c", k=KC), f32(8192, 8192).rearrange("p (k c) -> p k c", k=KC)]
        PE1 = [f32(24576 + 4096 * i, 4096) for i in range(2)]
        QE = f32(32768, 1024).rearrange("p (c n) -> p c n", c=CT)
        QC = f32(33792, 1024).rearrange("p (c n) -> p c n", c=CT)
        MRING = [f32(34816 + 2048 * i, 2048) for i in range(2)]
        PT1 = f32(38912, 4096)
        WQ1 = f32(43536, 512).rearrange("p (c f) -> p c f", c=CT)
        WK1 = f32(44048, 512).rearrange("p (c f) -> p c f", c=CT)
        WV1 = f32(44560, 512).rearrange("p (c f) -> p c f", c=CT)
        HTE = f32(45072, 1024).rearrange("p (c n) -> p c n", c=CT)
        AO = f32(46096, 1024).rearrange("p (t c) -> p t c", t=TT)
        HLE = CTXN
        WQKV = [f32(16384 + 2048 * i, 2048).rearrange("p (c f) -> p c f", c=CT) for i in range(3)]
        WOM = f32(22528, 2048).rearrange("p (k f) -> p k f", k=8)
        VTM = f32(24576, 4096).rearrange("p (t f) -> p t f", t=TT)
        QTM = f32(28672, 4096).rearrange("p (t f) -> p t f", t=TT)
        OTM = QTM
        QT = f32(32768, 4096).rearrange("p (k n) -> p k n", k=8)
        OT = QT
        KT = f32(36864, 4096).rearrange("p (k n) -> p k n", k=8)
        PM = [f32(40960 + 512 * i, 512).rearrange("p (t n) -> p t n", t=2) for i in range(2)]
        PTM = [f32(41984 + 512 * i, 512).rearrange("p (k n) -> p k n", k=2) for i in range(2)]
        T2 = [f32(45072 + 512 * i, 512).rearrange("p (h d) -> p h d", h=8) for i in range(2)]
        HTF = f32(43536, 1024).rearrange("p (c n) -> p c n", c=CT)
        CONST = f32(47120, N_CONSTS)

        def const(name):
            return CONST[:, CONST_AT[name]:CONST_AT[name] + CONSTS[name]]

        W1E = f32(0, 8192).rearrange("p (c e i) -> p c e i", c=CT, e=E)
        W2E = f32(8192, 8192).rearrange("p (t e h) -> p t e h", t=IT, e=E)
        EMB = f32(44560, 16).rearrange("p (c e) -> p c e", c=CT)
        SEL = f32(24576, 2048).rearrange("p (t e s) -> p t e s", t=TT, e=E)
        SELW = f32(26624, 2048).rearrange("p (t e s) -> p t e s", t=TT, e=E)
        SELT = f32(28672, 2048).rearrange("p (k n) -> p k n", k=4)
        XG = f32(30720, 1024).rearrange("p (c n) -> p c n", c=CT)
        INTER = f32(31744, 2048).rearrange("p (t n) -> p t n", t=IT)
        OE = f32(33792, 1024).rearrange("p (k c) -> p k c", k=4)
        R = [f32(34816 + 32 * i, 32).rearrange("p (t e) -> p t e", e=E) for i in range(12)]
        R1 = [f32(35200 + 4 * i, 4) for i in range(8)]
        assert 47120 + N_CONSTS <= 48144
        at = 52096
        AMAX = f32(at, 4); at += 4
        QSC = f32(at, 4); at += 4
        OSC = f32(at, 4); at += 4
        MS = f32(at, 4); at += 4
        CQ = f32(at, 4); at += 4
        EMX = f32(at, 32); at += 32
        EM = f32(at, 4); at += 4
        ET = f32(at, 4); at += 4
        ENB = f32(at, 4); at += 4
        ESUM = f32(at, 4); at += 4
        ERI = f32(at, 4); at += 4
        FMX = f32(at, 64); at += 64
        FNB = f32(at, 64); at += 64
        FSUM = f32(at, 64); at += 64
        FRI = f32(at, 64); at += 64
        WSUM = f32(at, 2); at += 2
        WMEAN = f32(at, 2); at += 2
        WSC = f32(at, 2); at += 2
        ABIAS = f32(at, 1); at += 1
        assert at <= 53120

        kparts = nc.dram_tensor("kparts", [B, 3, D, S2], BF16, kind="Internal").ap()
        qparts = nc.dram_tensor("qparts", [3, D, T], BF16, kind="Internal").ap()

        x_loaded = sem("x_loaded")
        cols_loaded = sem("cols_loaded")
        wq_loaded = sem("wq_loaded")
        wkv_loaded = sem("wkv_loaded")
        mask_loaded = sem("mask_loaded")
        ident_built = sem("ident_built")
        ones_built = sem("ones_built")
        kones_built = sem("kones_built")
        mask_counted = sem("mask_counted")
        mask_flagged = sem("mask_flagged")
        mask_step = sem("mask_step")
        ln_step = sem("ln_step")
        ln_var = sem("ln_var")
        ln_sd = sem("ln_sd")
        h_ready = sem("h_ready")
        ht_psum = sem("ht_psum")
        ht_ready = sem("ht_ready")
        q_psum = sem("q_psum")
        q_split = sem("q_split")
        q_ready = sem("q_ready")
        q_stored = sem("q_stored")
        q_stacked = sem("q_stacked")
        ctx_loaded = [sem(f"ctx_loaded{i}") for i in range(2)]
        k_psum = sem("k_psum")
        k_copied = sem("k_copied")
        k_rest = sem("k_rest")
        k_middle = sem("k_middle")
        k_low = sem("k_low")
        k_stored = [sem(f"k_stored{i}") for i in range(2)]
        v_psum = sem("v_psum")
        v_copied = sem("v_copied")
        k_stacked = [sem(f"k_stacked{i}") for i in range(3)]
        s_ready = sem("s_ready")
        s_maxed = sem("s_maxed")
        m_step = sem("m_step")
        m_split = sem("m_split")
        m_turned = sem("m_turned")
        m_stacked_a = sem("m_stacked_a")
        m_stacked_v = sem("m_stacked_v")
        st_ready = sem("st_ready")
        exp_ready = sem("exp_ready")
        pv_done = sem("pv_done")
        pv_copied = sem("pv_copied")
        pv_turned = sem("pv_turned")
        norm_step = sem("norm_step")
        v_staged = sem("v_staged")
        out_stored = sem("out_stored")
        SIGNALS = """
            aw_loaded bm_loaded raw_loaded mix_loaded rows_loaded wo_loaded bv1_loaded l1w_loaded
            ctxt_loaded0 ctxt_loaded1 ctxk_loaded0 ctxk_loaded1 mask1_loaded0 mask1_loaded1
            qkv_loaded wom_loaded const_loaded emb_loaded w1e_loaded w2e_loaded
            w_summed w_total w_quantised
            b_out x_ready sq_ready
            c_padded c_in c_in_copied c_a_weights c_conv_b c_sigmoid c_silu c_a c_a_copied c_ab
            c_ab_copied c_ha c_ha_copied c_pw c_pw_copied c_hb c_hb_copied c_fuse c_gated c_out
            d_quant d_turned d_turned_copied d_up d_hidden d_gelu d_quant2 d_turned2
            d_turned2_copied d_down
            e_q e_q_copied e_qc e_qc_copied e_cq e_cq_copied e_scores e_masked e_bias e_exp
            e_turned e_turned_a e_turned_v e_att e_normed e_out
            f_qkv f_roped f_rope_part f_v_copied f_turned f_turned_copied f_scores f_masked f_bias f_exp
            f_pt f_pt_copied f_pv f_normed f_ot f_ot_copied f_out
            g_logits g_chosen g_cum g_sel g_selw g_xg g_xg_copied g_up g_up_copied g_down
            g_down_copied g_selt g_selt_copied g_out step_v
        """.split()
        on = {name: sem(name) for name in SIGNALS}

        def by_part_of(ap):
            return ap.rearrange("(c p) n -> p c n", p=P)

        block = ctx.enter_context(nc.Block())

        @block.sync
        def _(sp):
            sp.dma_start(X, t["x"].rearrange("(t p) c -> p t c", p=P)).then_inc(x_loaded, 16)
            sp.dma_start(COLT, t["cols"]).then_inc(cols_loaded, 16)
            sp.dma_start(AW, t["A"].rearrange("(t p) s -> p t s", p=P)).then_inc(on["aw_loaded"], 16)
            sp.dma_start(BV, t["rows"][:, ROW_AT["bv"]:ROW_AT["bv"] + 256].broadcast_to((P, 256)))\
              .then_inc(cols_loaded, 16)
            sp.dma_start(WQ, t["wqT"].rearrange("(c p) f -> p c f", p=P)).then_inc(wq_loaded, 16)
            sp.dma_start(WK, t["wkT"].rearrange("(c p) f -> p c f", p=P)).then_inc(wkv_loaded, 16)
            sp.dma_start(WV, t["wvT"].rearrange("(c p) f -> p c f", p=P)).then_inc(wkv_loaded, 16)
            sp.dma_start(MASKI, t["mask"].rearrange("(t p) n -> p t n", p=P)).then_inc(mask_loaded, 16)

            def load_ctx(b, ch, slot):
                sp.dma_start(CTX[slot], t["ctxT"][b].rearrange("(c p) n -> p c n", p=P)
                             [:, :, bass.ds(ch * CH, CH)]).then_inc(ctx_loaded[slot], 16)

            def store_k(b, ch, f):
                piece = 16 * b + 2 * ch + f
                sp.wait_ge(k_low, piece + 1)
                sp.dma_start(kparts[b, :, f * P:(f + 1) * P, bass.ds(ch * CH, CH)]
                             .rearrange("r p n -> p r n"), KPT[f]).then_inc(k_stored[f], 16)

            def store_q():
                for f in range(CT):
                    sp.wait_ge(q_ready, f + 1)
                    sp.dma_start(qparts[:, f * P:(f + 1) * P, :].rearrange("r p n -> p r n"), KPT[f])\
                      .then_inc(q_stored, 16)
                sp.wait_ge(q_stored, 16 * CT)
                for r in range(6):
                    sp.dma_start(QST[DH * r:DH * (r + 1), :, :],
                                 qparts[Q_PARTS[r]].rearrange("(h d) n -> d h n", d=DH)).then_inc(q_stacked, 16)

            def load_stack(gg):
                b, g, slot = gg // GPB, gg % GPB, gg % 3
                for r in range(6):
                    src = kparts[b, K_PARTS[r], g * G * DH:(g + 1) * G * DH, :]
                    sp.dma_start(KST[slot][DH * r:DH * (r + 1), :, :],
                                 src.rearrange("(j d) n -> d j n", d=DH)).then_inc(k_stacked[slot], 16)

            load_ctx(0, 0, 0)
            load_ctx(0, 1, 1)
            store_q()
            for b in range(B):
                def chunk_pair(i, more):
                    for u in range(2):
                        for f in range(CT):
                            store_k(b, 2 * i + u, f)
                        if b == 0:
                            sp.wait_ge(v_psum, 8 * i + (4 * u + 4))
                        if more:
                            load_ctx(b, 2 * i + (u + 2), u)
                with sp.Fori(0, NCH // 2 - 1) as i:
                    chunk_pair(i, True)
                chunk_pair(NCH // 2 - 1, False)
                if b == 0:
                    load_ctx(1, 0, 0)
                    load_ctx(1, 1, 1)
                for f in range(CT):
                    sp.wait_ge(k_stored[f], 16 * 8 * (b + 1))
                if b == 0:
                    load_stack(0)
                    sp.wait_ge(q_psum, CT)
                    load_stack(1)
                    sp.wait_ge(mask_step, 2)
                    load_stack(2)
            load_ctx(1, 0, 0)
            load_ctx(1, 1, 1)
            sp.wait_ge(st_ready, KC)
            load_stack(3)
            sp.wait_ge(st_ready, 2 * KC)
            load_stack(4)
            sp.wait_ge(st_ready, 3 * KC)
            load_stack(5)
            with sp.Fori(0, NCH // 2 - 1) as i:
                for u in range(2):
                    sp.wait_ge(v_psum, KC + 8 * i + 4 * u + 4)
                    load_ctx(1, 2 * i + u + 2, u)
            sp.wait_ge(st_ready, 4 * KC)
            load_stack(6)
            sp.wait_ge(st_ready, 5 * KC)
            load_stack(7)

            def load(dst, src, name):
                sp.dma_start(dst, src).then_inc(on[name], 16)

            def by_part(name):
                return t[name].rearrange("(c p) f -> p c f", p=P)

            sp.wait_ge(v_psum, 2 * KC)
            load(W1RAW.rearrange("p (c f) -> p c f", c=CT), by_part("w1T"), "raw_loaded")
            load(W2RAW.rearrange("p (c f) -> p c f", c=FT), by_part("w2T"), "raw_loaded")
            for copy in range(P // DS):
                load(BM[copy * DS:(copy + 1) * DS, :], t["Bm"], "bm_loaded")
            sp.wait_ge(st_ready, 6 * KC)
            for dst, name in ((WIN, "winT"), (WPW, "wpwT"), (WHA, "whaT"), (WHB, "whbT"), (WFU, "wfuT")):
                load(dst, by_part(name), "mix_loaded")
            sp.wait_ge(st_ready, 7 * KC)
            load(WO, by_part("woT"), "wo_loaded")
            load(WOUT, by_part("woutT"), "wo_loaded")
            load(ROWS_T, t["rows"][:, 0:N_FFN_ROWS].broadcast_to((P, N_FFN_ROWS)), "rows_loaded")
            sp.wait_ge(st_ready, 8 * KC)
            load(CTXT[0], by_part_of(t["ctxT"][0]), "ctxt_loaded0")
            sp.wait_ge(norm_step, 3 * NG)
            load(BV, t["rows"][:, ROW_AT["bv1"]:ROW_AT["bv1"] + 256].broadcast_to((P, 256)), "bv1_loaded")
            sp.wait_ge(on["w_quantised"], 6)
            load(WQ1, by_part("wq1T"), "l1w_loaded")
            load(WK1, by_part("wk1"), "l1w_loaded")
            load(WV1, by_part("wv1T"), "l1w_loaded")
            sp.wait_ge(on["c_ab"], 4)
            load(CONST, t["consts"], "const_loaded")
            sp.wait_ge(on["c_fuse"], 4)
            load(CTXK[0], t["ctx"][0].rearrange("(k p) c -> p k c", p=P), "ctxk_loaded0")
            sp.wait_ge(on["c_out"], 4)

            def load_mask(n):
                unit, half = n // 2, n % 2
                if n >= 2:
                    sp.wait_ge(on["e_masked"], 4 * (n - 1))
                qt = unit % 2
                load(MRING[half], t["mask1"][qt * P:(qt + 1) * P, half * 2048:(half + 1) * 2048],
                     f"mask1_loaded{half}")

            load_mask(0)
            load_mask(1)
            sp.wait_ge(on["x_ready"], 3 * TT)
            load(CTXT[1], by_part_of(t["ctxT"][1]), "ctxt_loaded1")
            for n in range(2, 4):
                load_mask(n)
            sp.wait_ge(on["e_scores"], 16)
            load(CTXK[1], t["ctx"][1].rearrange("(k p) c -> p k c", p=P), "ctxk_loaded1")
            for n in range(4, 6):
                load_mask(n)
            sp.wait_ge(on["e_att"], 2)
            for dst, name in zip(WQKV, ("wqm", "wkm", "wvm")):
                load(dst, by_part(name), "qkv_loaded")
            load(WOM, by_part("wom"), "wom_loaded")
            for n in range(6, 8):
                load_mask(n)
            sp.wait_ge(on["e_scores"], 32)
            for k in range(CT):
                load(W1E[:, k], t["w1e"][:, k * P:(k + 1) * P, :].rearrange("e p i -> p e i"), "w1e_loaded")
            sp.wait_ge(on["e_att"], 4)
            for k in range(IT):
                load(W2E[:, k], t["w2e"][:, k * P:(k + 1) * P, :].rearrange("e p h -> p e h"), "w2e_loaded")
            sp.wait_ge(on["e_out"], 4)
            load(EMB, by_part("embT"), "emb_loaded")
            sp.wait_ge(on["x_ready"], 6 * TT)
            sp.dma_start(t["out"].rearrange("(t p) c -> p t c", p=P), X).then_inc(out_stored, 16)
            sp.wait_ge(out_stored, 16)

        @block.gpsimd
        def _(pool):
            nc.gpsimd.memset(IDENT, 0.0).then_inc(ident_built, 1)
            nc.gpsimd.memset(IDENTB, 0.0).then_inc(ident_built, 1)
            nc.gpsimd.memset(ONES, 1.0).then_inc(ones_built, 1)
            pool.wait_ge(ident_built, 2)
            for m in (IDENT, IDENTB):
                nc.gpsimd.affine_select(out=m, in_=m, compare_op=ALU.not_equal, fill=1.0, base=0,
                                        pattern=[[-1, P]], channel_multiplier=1).then_inc(ident_built, 1)
            nc.gpsimd.memset(V[:, :, :, DH:VW], 1.0).then_inc(ones_built, 1)
            nc.gpsimd.memset(V_flat[:, KC * H * VW:KC * H * VW + 16], 0.0).then_inc(ones_built, 1)
            two_ones = float(np.array([0x3F803F80], np.uint32).view(np.float32)[0])
            pool.wait_ge(ones_built, 3)
            nc.gpsimd.memset(arena[ROWS:KROWS, 0:8192], two_ones).then_inc(kones_built, 1)
            pool.wait_ge(kones_built, 1)

            def low_part(piece, f):
                pool.wait_ge(k_middle, piece + 1)
                nc.gpsimd.tensor_tensor(KPT[f][:, 2, :], K32[f], KPT[f][:, 1, :], ALU.subtract)\
                  .then_inc(k_low, 1)

            with pool.Fori(0, NCH) as i:
                for f in range(CT):
                    low_part(2 * i + f, f)
            pool.wait_ge(k_low, 2 * NCH)
            pool.wait_ge(q_psum, CT)
            nc.gpsimd.memset(arena[ROWS:KROWS, 8192:16384], two_ones).then_inc(kones_built, 1)
            pool.wait_ge(kones_built, 2)
            pool.wait_ge(mask_step, 2)
            nc.gpsimd.memset(arena[ROWS:KROWS, 16384:24576], two_ones).then_inc(kones_built, 1)
            pool.wait_ge(kones_built, 3)
            with pool.Fori(0, NCH) as i:
                for f in range(CT):
                    low_part(2 * i + f + 16, f)
            for gg in range(NG):
                g, n0 = gg % GPB, KC * gg
                pool.wait_ge(v_copied, KC * (gg // GPB + 1))

                def stage_values(i, first):
                    for u in range(8):
                        if not first or n0 + u >= 4:
                            pool.wait_ge(pv_done, 8 * i + (n0 + u - 3))
                        nc.gpsimd.tensor_copy(VS[u % 4], V_flat[:, bass.ds(i * (8 * H * VW) + (u * H * VW + g * G * VW), 84)])\
                          .then_inc(v_staged, 1)
                stage_values(0, True)
                with pool.Fori(1, KC // 8) as i:
                    stage_values(i, False)

            pool.wait_ge(pv_done, NG * KC)
            pool.wait_ge(v_staged, NG * KC)
            nc.gpsimd.memset(VAL[:, :, :, 0:4], 0.0).then_inc(on["c_padded"], 1)
            nc.gpsimd.memset(VAL[:, :, :, S + 4:PAD], 0.0).then_inc(on["c_padded"], 1)
            pool.wait_ge(on["c_padded"], 2)

            nc.gpsimd.memset(AWK, 0.0).then_inc(on["c_a_weights"], 1)
            nc.gpsimd.memset(ABIAS, 0.0).then_inc(on["c_a_weights"], 1)
            pool.wait_ge(on["c_a_weights"], 2)
            pool.wait_ge(on["aw_loaded"], 16)
            for m in range(IT):
                for k in range(TAPS_A):
                    nc.gpsimd.tensor_scalar(AWK[:, m, k, 0:DS], AW[:, m, :], col("dwa_k", TAPS_A * m + k), None,
                                            ALU.mult).then_inc(on["c_a_weights"], 1)

            for piece in range(16):
                pool.wait_ge(on["f_rope_part"], 3 * (piece + 1))
                i, half = piece % 8 // 2, piece % 2
                out = QTM[:, i, half * HALF:(half + 1) * HALF].rearrange("p (h d) -> p h d", h=8)
                nc.gpsimd.tensor_tensor(out, out, T2[piece % 2], ALU.add).then_inc(on["f_roped"], 1)

        @block.scalar
        def _(act):
            act.wait_ge(ln_var, 1)
            nc.scalar.activation(SD[:, 0:4], SD[:, 4:8], ACT.Sqrt).then_inc(ln_sd, 1)
            for c in range(CT):
                act.wait_ge(ht_psum, c + 1)
                nc.scalar.activation(HT[:, c, :], psum[:, 6 + c, :], ACT.Copy).then_inc(ht_ready, 1)

            def copy_k(piece, f, reuse):
                act.wait_ge(k_psum, piece + 1)
                if reuse is not None:
                    act.wait_ge(k_stored[f], reuse)
                bias = COLT[:, COL_AT["bk"] + f:COL_AT["bk"] + f + 1]
                nc.scalar.activation(K32[f], psum[:, f, :], ACT.Identity, bias=bias).then_inc(k_copied, 1)
                nc.scalar.activation(KPT[f][:, 0, :], psum[:, f, :], ACT.Identity, bias=bias).then_inc(k_copied, 1)

            def v_tile(done, kc, bank):
                act.wait_ge(v_psum, done + 1)
                nc.scalar.activation(V[:, bass.ds(kc, 1), :, 0:DH],
                                     psum[:, bank, 0:256].rearrange("p (o h d) -> p o h d", o=1, h=H),
                                     ACT.Copy).then_inc(v_copied, 1)

            act.wait_ge(cols_loaded, 32)
            act.wait_ge(q_stored, 16 * CT)
            with act.Fori(0, NCH) as i:
                for f in range(CT):
                    copy_k(2 * i + f, f, 16 * i)
                for v in range(4):
                    v_tile(4 * i + v, 4 * i + v, 2 + v % 2)
            with act.Fori(0, NCH) as i:
                for f in range(CT):
                    copy_k(2 * i + f + 16, f, 16 * i + 16 * NCH)

            def stack_max(gg):
                b, g = gg // GPB, gg % GPB
                act.wait_ge(m_turned, gg + 1)
                nc.scalar.activation(QST[ROWS:KROWS, G * g:G * g + 2, b * S:(b + 1) * S],
                                     psum[ROWS:KROWS, 2, :].rearrange("p (j n) -> p j n", j=2),
                                     ACT.Copy).then_inc(m_stacked_a, 1)

            for gg in range(NG):
                if gg == GPB:
                    act.wait_ge(v_staged, GPB * KC)
                    with act.Fori(0, KC // 4) as i:
                        for v in range(4):
                            v_tile(4 * i + v + KC, 4 * i + v, v)
                stack_max(gg)
                n0 = KC * gg

                def exps(i, first):
                    for u in range(8):
                        act.wait_ge(st_ready, 8 * i + (n0 + u + 1))
                        if not first or n0 + u >= 2:
                            act.wait_ge(pv_done, 8 * i + (n0 + u - 1))
                        nc.scalar.activation(PR[u % 2], ST(u % 2).rearrange("p b n -> p (b n)"), ACT.Exp)\
                          .then_inc(exp_ready, 1)
                exps(0, True)
                with act.Fori(1, KC // 8) as i:
                    exps(i, False)
                act.wait_ge(pv_done, n0 + KC)
                if gg:
                    act.wait_ge(pv_turned, gg)
                nc.scalar.activation(PVS, PV, ACT.Copy).then_inc(pv_copied, 1)


            sqrts = [1]

            def root():
                sqrts[0] += 1
                act.wait_ge(ln_var, sqrts[0])
                nc.scalar.activation(SD[:, 0:4], SD[:, 4:8], ACT.Sqrt).then_inc(ln_sd, 1)

            turns = [1]

            def copy_turned(dst, scale=None):
                for c in range(CT):
                    act.wait_ge(ht_psum, CT * turns[0] + c + 1)
                    if scale is None:
                        nc.scalar.activation(dst[:, c, :], psum[:, 6 + c, :], ACT.Copy).then_inc(ht_ready, 1)
                    else:
                        nc.scalar.activation(dst[:, c, :], psum[:, 6 + c, :], ACT.Identity,
                                             scale=col(scale, c)).then_inc(ht_ready, 1)
                turns[0] += 1

            def signal(ins, name):
                ins.then_inc(on[name], 1)

            copy_turned(HTC)
            root()
            root()
            copy_turned(HTC, "norm_w")
            act.wait_ge(on["c_padded"], 2)
            for j in range(8):
                act.wait_ge(on["c_in"], j + 1)
                if j < IT:
                    signal(nc.scalar.activation(VAL[:, j, :, 4:S + 4],
                                                psum[:, j, :].rearrange("p (b n) -> p b n", b=B), ACT.Identity,
                                                bias=col("in_b", IT + j)), "c_in_copied")
                else:
                    signal(nc.scalar.activation(GATE[:, j - IT, :], psum[:, j, :], ACT.Sigmoid,
                                                bias=col("in_b", j - IT)), "c_in_copied")
            act.wait_ge(on["c_a"], 1)
            signal(nc.scalar.activation(ABIAS[0:DS, :], psum[0:DS, 1, 0:1], ACT.Copy), "c_a_copied")
            act.wait_ge(on["c_a_copied"], 1)
            act.wait_ge(on["c_a"], 2)
            signal(nc.scalar.activation(AS, psum[:, 0, :], ACT.Identity, bias=ABIAS), "c_a_copied")
            for m in range(IT):
                act.wait_ge(on["c_ab"], m + 1)
                signal(nc.scalar.activation(AB[:, m, :], psum[:, 1 + m, :], ACT.Copy), "c_ab_copied")
            for m in range(IT):
                act.wait_ge(on["c_conv_b"], IT * (TAPS_B - 1) + m + 1)
                signal(nc.scalar.activation(SB[:, m, :], CB[:, m, :], ACT.Sigmoid), "c_sigmoid")
            for m in range(2):
                act.wait_ge(on["c_ha"], m + 1)
                signal(nc.scalar.activation(YC[:, m, :], psum[:, 5 + m, :], ACT.Identity,
                                            bias=col("ha_b", m)), "c_ha_copied")
            for m in range(IT):
                act.wait_ge(on["c_pw"], m + 1)
                signal(nc.scalar.activation(PWO[:, m, :], psum[:, m, :], ACT.Identity,
                                            bias=col("pw_b", m)), "c_pw_copied")
            for m in range(2):
                act.wait_ge(on["c_hb"], m + 1)
                signal(nc.scalar.activation(YC[:, 2 + m, :], psum[:, 4 + m, :], ACT.Identity,
                                            bias=col("hb_b", m)), "c_hb_copied")
            root()
            root()
            for c in range(CT):
                act.wait_ge(on["d_turned"], c + 1)
                signal(nc.scalar.activation(HQT[:, c, :], psum[:, 6 + c, 0:256].bitcast(BF16), ACT.Copy),
                       "d_turned_copied")
            for n in range(8):
                act.wait_ge(on["d_hidden"], n + 1)
                part = UH[:, n // 2, n % 2 * 512:(n % 2 + 1) * 512]
                signal(nc.scalar.activation(part, part, ACT.Gelu), "d_gelu")
            root()
            for k in range(FT):
                act.wait_ge(on["d_turned2"], k + 1)
                signal(nc.scalar.activation(QHT[:, k, :], psum[:, k, 0:256].bitcast(BF16), ACT.Copy),
                       "d_turned2_copied")
            root()
            copy_turned(HTE)
            for f in range(CT):
                act.wait_ge(on["e_q"], f + 1)
                signal(nc.scalar.activation(QE[:, f, :], psum[:, f, :], ACT.Identity, bias=col("bq1", f)),
                       "e_q_copied")
            for c in range(CT):
                act.wait_ge(on["e_qc"], c + 1)
                signal(nc.scalar.activation(QC[:, c, :], psum[:, 2 + c, :], ACT.Copy, scale=D ** -0.5),
                       "e_qc_copied")
            for w in range(4):
                act.wait_ge(on["e_bias"], w + 1)
                signal(nc.scalar.activation(PE1[w % 2], PE1[w % 2], ACT.Exp, bias=ENB[:, w:w + 1],
                                            accum_out=ESUM[:, w:w + 1]), "e_exp")
                for n in range(0, 8, 2):
                    act.wait_ge(on["e_turned"], 8 * w + n + 1)
                    if w:
                        act.wait_ge(on["e_att"], w)
                    signal(nc.scalar.activation(PT1[:, n * 512:(n + 1) * 512], psum[:, 4, :], ACT.Copy),
                           "e_turned_a")
            copy_turned(HTE)
            root()
            copy_turned(HTF)
            for n in range(16):
                act.wait_ge(on["f_turned"], n + 1)
                dst = QT if n < 8 else KT
                signal(nc.scalar.activation(dst[:, n % 8, :], psum[:, n % 8, :], ACT.Copy), "f_turned_copied")
            for n in range(8):
                act.wait_ge(on["f_qkv"], 16 + n + 1)
                signal(nc.scalar.activation(VTM[:, n // 2, n % 2 * HALF:(n % 2 + 1) * HALF], psum[:, n, :],
                                            ACT.Copy), "f_v_copied")
            for n in range(32):
                act.wait_ge(on["f_bias"], n + 1)
                if n >= 2:
                    act.wait_ge(on["f_pt"], n - 1)
                src = PM[n % 2] if n % HM < 8 else psum[:, n % 2, :].rearrange("p (t n) -> p t n", t=2)
                for qt in range(2):
                    signal(nc.scalar.activation(PM[n % 2][:, qt, :], src[:, qt, :], ACT.Exp, scale=DM ** -0.5,
                                                bias=FNB[:, 2 * n + qt:2 * n + qt + 1],
                                                accum_out=FSUM[:, 2 * n + qt:2 * n + qt + 1]), "f_exp")
            for k in range(8):
                act.wait_ge(on["f_ot"], k + 1)
                signal(nc.scalar.activation(OT[:, k, :], psum[:, k, :], ACT.Copy), "f_ot_copied")
            root()
            copy_turned(HTF)
            act.wait_ge(on["g_logits"], 2)
            signal(nc.scalar.activation(R1[3], R1[2], ACT.Exp), "g_logits")
            for c in range(CT):
                act.wait_ge(on["g_xg"], c + 1)
                signal(nc.scalar.activation(XG[:, c, :], psum[:, 2 + c, :], ACT.Copy), "g_xg_copied")
            for m in range(IT):
                act.wait_ge(on["g_up"], m + 1)
                signal(nc.scalar.activation(INTER[:, m, :], psum[:, 4 + m, :], ACT.Relu), "g_up_copied")
            for k in range(4):
                act.wait_ge(on["g_down"], k + 1)
                signal(nc.scalar.activation(OE[:, k, :], psum[:, k, 0:256], ACT.Copy), "g_down_copied")

        @block.vector
        def _(dve):
            dve.wait_ge(x_loaded, 16)
            for i in range(TT):
                nc.vector.bn_stats(BN[:, 6 * i:6 * i + 6], X[:, i, :]).then_inc(ln_step, 1)
            dve.wait_ge(ln_step, TT)
            for i in range(TT):
                nc.vector.bn_aggr(MV[:, 2 * i:2 * i + 2], BN[:, 6 * i:6 * i + 6]).then_inc(ln_step, 1)
            dve.wait_ge(ln_step, 2 * TT)
            mean = MV.rearrange("p (t two) -> p t two", two=2)
            nc.vector.tensor_scalar(SD[:, 4:8], mean[:, :, 1], 1e-5, None, ALU.add).then_inc(ln_var, 1)
            dve.wait_ge(ln_sd, 1)
            nc.vector.reciprocal(SD[:, 4:8], SD[:, 0:4]).then_inc(ln_step, 1)
            dve.wait_ge(ln_step, 2 * TT + 1)
            for i in range(TT):
                nc.vector.tensor_scalar(HN[:, i, :], X[:, i, :], MV[:, 2 * i:2 * i + 1], SD[:, 4 + i:5 + i],
                                        ALU.subtract, ALU.mult).then_inc(h_ready, 1)
            dve.wait_ge(mask_loaded, 16)
            for i in range(2):
                nc.vector.tensor_scalar(MASKB[:, i, :], MASKI[:, i, :], 0.0, MASKED, ALU.is_equal, ALU.mult)\
                  .then_inc(mask_step, 1)
            dve.wait_ge(mask_step, 2)
            nc.vector.tensor_reduce(FLAGF[:, 0:1], MASKB, AX.XY, ALU.min).then_inc(mask_step, 1)
            dve.wait_ge(mask_step, 3)
            nc.vector.tensor_scalar(FLAGF[:, 1:2], FLAGF[:, 0:1], 0.0, None, ALU.is_lt).then_inc(mask_step, 1)
            dve.wait_ge(mask_counted, 1)
            nc.vector.tensor_scalar(FLAG, psum[0:1, 5, 0:1], 0.0, None, ALU.is_gt).then_inc(mask_flagged, 1)
            dve.wait_ge(cols_loaded, 32)
            for f in range(CT):
                n = 4 * f
                dve.wait_ge(q_psum, f + 1)
                nc.vector.tensor_scalar(K32[f], psum[:, f, :], COLT[:, COL_AT["bq"] + f:COL_AT["bq"] + f + 1],
                                        DH ** -0.5, ALU.add, ALU.mult).then_inc(q_split, 1)
                dve.wait_ge(q_split, n + 1)
                nc.vector.tensor_copy(KPT[f][:, 0, :], K32[f]).then_inc(q_split, 1)
                dve.wait_ge(q_split, n + 2)
                nc.vector.tensor_tensor(K32[f], K32[f], KPT[f][:, 0, :], ALU.subtract).then_inc(q_split, 1)
                dve.wait_ge(q_split, n + 3)
                nc.vector.tensor_copy(KPT[f][:, 1, :], K32[f]).then_inc(q_split, 1)
                dve.wait_ge(q_split, n + 4)
                nc.vector.tensor_tensor(KPT[f][:, 2, :], K32[f], KPT[f][:, 1, :], ALU.subtract)\
                  .then_inc(q_ready, 1)

            def split_k(piece, f):
                dve.wait_ge(k_copied, 2 * piece + 2)
                nc.vector.tensor_tensor(K32[f], K32[f], KPT[f][:, 0, :], ALU.subtract).then_inc(k_rest, 1)
                dve.wait_ge(k_rest, piece + 1)
                nc.vector.tensor_copy(KPT[f][:, 1, :], K32[f]).then_inc(k_middle, 1)

            def maxes(n, col, row, mx):
                for c in range(8):
                    dve.wait_ge(s_ready, n + (c + 1))
                    nc.vector.tensor_reduce(mx[:, bass.ds(col + c, 1)], SP_(c % 2), AX.X, ALU.max)\
                      .then_inc(s_maxed, 1)

            with dve.Fori(0, NCH) as i:
                for f in range(CT):
                    split_k(2 * i + f, f)
            with dve.Fori(0, NCH) as i:
                for f in range(CT):
                    split_k(2 * i + f + 16, f)
                maxes(8 * i, 8 * i, None, MX[0])

            def split_max(gg):
                n = 4 * gg
                dve.wait_ge(s_maxed, 64 * (gg + 1))
                nc.vector.tensor_reduce(M8, MX[gg % 2].rearrange("p (m c) -> p m c", c=8), AX.X, ALU.max)\
                  .then_inc(m_step, 1)
                if gg:
                    dve.wait_ge(m_turned, gg)
                dve.wait_ge(m_step, n + 1)
                nc.vector.tensor_scalar(MPART[:, :, 0], M8, -1.0, None, ALU.mult).then_inc(m_step, 1)
                dve.wait_ge(m_step, n + 2)
                nc.vector.scalar_tensor_tensor(out=MR, in0=M8, scalar=-1.0, in1=MPART[:, :, 0],
                                               op0=ALU.mult, op1=ALU.subtract).then_inc(m_step, 1)
                dve.wait_ge(m_step, n + 3)
                nc.vector.tensor_copy(MPART[:, :, 1], MR).then_inc(m_step, 1)
                dve.wait_ge(m_step, n + 4)
                nc.vector.tensor_tensor(MPART[:, :, 2], MR, MPART[:, :, 1], ALU.subtract).then_inc(m_split, 1)
                b, g = gg // GPB, gg % GPB
                dve.wait_ge(m_turned, gg + 1)
                nc.vector.tensor_copy(QST[ROWS:KROWS, G * g + 2:G * g + 4, b * S:(b + 1) * S],
                                      psum[ROWS:KROWS, 3, :].rearrange("p (j n) -> p j n", j=2))\
                  .then_inc(m_stacked_v, 1)

            def normalise(gg):
                b, g = gg // GPB, gg % GPB
                n = 3 * gg
                dve.wait_ge(pv_turned, gg + 1)
                turned = PX[:, 0:256].rearrange("p (t j e) -> p t j e", t=2, j=G)
                nc.vector.reciprocal(RINV, turned[:, :, :, DH]).then_inc(norm_step, 1)
                dve.wait_ge(norm_step, n + 1)
                out = CTXN[:, 2 * b:2 * b + 2, G * DH * g:G * DH * (g + 1)].rearrange("p t (j d) -> p t j d", j=G)
                nc.vector.tensor_tensor(out, turned[:, :, :, 0:DH],
                                        RINV.unsqueeze(3).broadcast_to((P, 2, G, DH)), ALU.mult)\
                  .then_inc(norm_step, 1)
                dve.wait_ge(norm_step, n + 2)
                flat = CTXN[:, 2 * b:2 * b + 2, G * DH * g:G * DH * (g + 1)]
                bv = BV[:, G * DH * g:G * DH * (g + 1)].unsqueeze(1).broadcast_to((P, 2, G * DH))
                nc.vector.tensor_tensor(flat, flat, bv, ALU.add).then_inc(norm_step, 1)

            for gg in range(NG):
                split_max(gg)
                if gg + 1 < NG:
                    mx = MX[(gg + 1) % 2]
                    n = 64 * (gg + 1)
                    maxes(n, 0, None, mx)
                    if gg:
                        normalise(gg - 1)
                    maxes(n + 8, 8, None, mx)
                    with dve.Fori(1, KC // 8) as i:
                        maxes(16 * i + n, 16 * i, None, mx)
                        maxes(16 * i + (n + 8), 16 * i + 8, None, mx)
                else:
                    normalise(gg - 1)
            normalise(NG - 1)


            steps = [0]

            def mark(ins):
                ins.then_inc(on["step_v"], 1)
                steps[0] += 1

            def done():
                dve.wait_ge(on["step_v"], steps[0])

            roots = [1]

            def root():
                roots[0] += 1
                dve.wait_ge(ln_sd, roots[0])
                mark(nc.vector.reciprocal(SD[:, 4:8], SD[:, 0:4]))
                done()

            def statistics(src, n, width):
                for i in range(TT):
                    for j in range(n):
                        mark(nc.vector.bn_stats(BN[:, 6 * (n * i + j):6 * (n * i + j + 1)],
                                                src[:, i, j * width:(j + 1) * width]))
                done()
                for i in range(TT):
                    mark(nc.vector.bn_aggr(MV[:, 2 * i:2 * i + 2], BN[:, 6 * n * i:6 * n * (i + 1)]))
                done()
                nc.vector.tensor_scalar(SD[:, 4:8], mean[:, :, 1], 1e-5, None, ALU.add).then_inc(ln_var, 1)
                root()

            def centred(dst, src, i):
                return nc.vector.tensor_scalar(dst[:, i, :], src[:, i, :], MV[:, 2 * i:2 * i + 1],
                                               SD[:, 4 + i:5 + i], ALU.subtract, ALU.mult)

            def x_ready(ins):
                ins.then_inc(on["x_ready"], 1)

            dve.wait_ge(on["raw_loaded"], 32)
            for n, w in enumerate((W1RAW, W2RAW)):
                nc.vector.tensor_reduce(WSUM[:, n:n + 1], w, AX.X, ALU.add, apply_absolute_value=True)\
                  .then_inc(on["w_summed"], 1)
            dve.wait_ge(on["b_out"], 1)
            for i in range(TT):
                dve.wait_ge(on["b_out"], i + 1)
                x_ready(nc.vector.tensor_tensor(X[:, i, :], X[:, i, :], psum[:, i, 0:256], ALU.add))
            dve.wait_ge(on["x_ready"], TT)
            statistics(X, 1, D)
            for i in range(TT):
                mark(centred(HL, X, i))
            done()
            for i in range(TT):
                mark(nc.vector.tensor_tensor_reduce(HS[:, i, :], HL[:, i, :], HL[:, i, :], 1.0, 0.0,
                                                    ALU.mult, ALU.add, MS[:, i:i + 1]))
            done()
            nc.vector.tensor_scalar(SD[:, 4:8], MS, 1.0 / D, 1e-6, ALU.mult, ALU.add).then_inc(ln_var, 1)
            root()
            for i in range(TT):
                nc.vector.tensor_scalar(HS[:, i, :], HL[:, i, :], SD[:, 4 + i:5 + i], None, ALU.mult)\
                  .then_inc(h_ready, 1)
            for i in range(TT):
                mark(nc.vector.tensor_tensor(X[:, i, :], X[:, i, :], HL[:, i, :], ALU.add))
            dve.wait_ge(on["w_total"], 1)
            mark(nc.vector.tensor_scalar(WMEAN, psum[:, 4, 0:2], 1.0 / (D * FF), 1e-5, ALU.mult, ALU.max))
            done()
            mark(nc.vector.reciprocal(WSC, WMEAN))
            done()
            for n, (w, tw) in enumerate(((W1RAW, TW1), (W2RAW, TW2))):
                flat = tw.rearrange("p a b -> p (a b)")
                signal = on["w_quantised"]
                nc.vector.tensor_scalar(w, w, WSC[:, n:n + 1], ROUND, ALU.mult, ALU.add).then_inc(signal, 1)
                dve.wait_ge(signal, 3 * n + 1)
                nc.vector.tensor_scalar(w, w, ROUND, 1.0, ALU.subtract, ALU.min).then_inc(signal, 1)
                dve.wait_ge(signal, 3 * n + 2)
                nc.vector.tensor_scalar(flat, w, -1.0, None, ALU.max).then_inc(signal, 1)
            for k in range(TAPS_B):
                for m in range(IT):
                    tap = col("sym_k", TAPS_B * m + k)
                    src = VAL[:, m, :, 4 + k - LEFT_B:4 + k - LEFT_B + S]
                    out = CB[:, m, :].rearrange("p (b n) -> p b n", b=B)
                    if k == 0:
                        dve.wait_ge(on["c_in_copied"], m + 1)
                        nc.vector.tensor_scalar(out, src, tap, col("sym_b", m), ALU.mult, ALU.add)\
                          .then_inc(on["c_conv_b"], 1)
                    else:
                        dve.wait_ge(on["c_conv_b"], IT * (k - 1) + m + 1)
                        nc.vector.scalar_tensor_tensor(out=out, in0=src, scalar=tap, in1=out,
                                                       op0=ALU.mult, op1=ALU.add)\
                          .then_inc(on["c_conv_b"], 1)
            for m in range(IT):
                dve.wait_ge(on["c_sigmoid"], m + 1)
                nc.vector.tensor_tensor(SB[:, m, :], SB[:, m, :], CB[:, m, :], ALU.mult).then_inc(on["c_silu"], 1)
            for m in range(IT):
                dve.wait_ge(on["c_fuse"], m + 1)
                nc.vector.scalar_tensor_tensor(out=YG[:, m, :], in0=psum[:, m, :], scalar=col("fuse_b", m),
                                               in1=GATE[:, m, :], op0=ALU.add, op1=ALU.mult)\
                  .then_inc(on["c_gated"], 1)
            for i in range(TT):
                dve.wait_ge(on["c_out"], i + 1)
                x_ready(nc.vector.tensor_tensor(X[:, i, :], X[:, i, :], psum[:, 4 + i, 0:256], ALU.add))
            dve.wait_ge(on["x_ready"], 2 * TT)

            def quantise(src, dst, ready, per_row):
                mark(nc.vector.tensor_reduce(AMAX, src, AX.X, ALU.max, apply_absolute_value=True))
                done()
                mark(nc.vector.tensor_scalar(AMAX, AMAX, 1e-5, None, ALU.max))
                done()
                mark(nc.vector.reciprocal(QSC, AMAX))
                done()
                mark(nc.vector.tensor_scalar(QSC, QSC, 127.0, None, ALU.mult))
                mark(nc.vector.tensor_scalar(OSC, AMAX, per_row, 1.0 / 127.0, ALU.mult, ALU.mult))
                done()
                for i in range(TT):
                    mark(nc.vector.tensor_scalar(src[:, i, :], src[:, i, :], QSC[:, i:i + 1], ROUND,
                                                 ALU.mult, ALU.add))
                    done()
                    mark(nc.vector.tensor_scalar(dst[:, i, :], src[:, i, :], ROUND, 127.0, ALU.subtract, ALU.min))
                    done()
                    nc.vector.tensor_scalar(dst[:, i, :], dst[:, i, :], -128.0, None, ALU.max)\
                      .then_inc(on[ready], 1)

            def scaled(src, i, g, b):
                mark(nc.vector.tensor_tensor(src[:, i, :], src[:, i, :], row(g), ALU.mult))
                done()
                mark(nc.vector.tensor_tensor(src[:, i, :], src[:, i, :], row(b), ALU.add))

            statistics(X, 1, D)
            for i in range(TT):
                mark(centred(HL, X, i))
            done()
            statistics(HL, 1, D)
            dve.wait_ge(on["rows_loaded"], 16)
            for i in range(TT):
                mark(centred(HL, HL, i))
                done()
                scaled(HL, i, "g1", "b1")
            done()
            quantise(HL, HQ, "d_quant", WMEAN[:, 0:1])
            for n in range(8):
                i, half = n // 2, n % 2
                dve.wait_ge(on["d_up"], n + 1)
                nc.vector.scalar_tensor_tensor(out=UH[:, i, half * 512:(half + 1) * 512], in0=psum[:, n, :],
                                               scalar=OSC[:, i:i + 1], in1=row("w1b")[:, half * 512:(half + 1) * 512],
                                               op0=ALU.mult, op1=ALU.add).then_inc(on["d_hidden"], 1)
            dve.wait_ge(on["d_gelu"], 8)
            statistics(UH, 2, 512)
            for i in range(TT):
                mark(centred(UH, UH, i))
                done()
                scaled(UH, i, "g2", "b2")
            done()
            quantise(UH, QH, "d_quant2", WMEAN[:, 1:2])
            for i in range(TT):
                mark(nc.vector.tensor_tensor(X[:, i, :], X[:, i, :], row("w2b"), ALU.add))
            done()
            for i in range(TT):
                dve.wait_ge(on["d_down"], i + 1)
                x_ready(nc.vector.scalar_tensor_tensor(out=X[:, i, :], in0=psum[:, i, 0:256], scalar=OSC[:, i:i + 1],
                                                       in1=X[:, i, :], op0=ALU.mult, op1=ALU.add))
            dve.wait_ge(on["x_ready"], 3 * TT)

            statistics(X, 1, D)
            for i in range(TT):
                centred(HLE, X, i).then_inc(h_ready, 1)
            dve.wait_ge(on["e_cq"], 1)
            nc.vector.tensor_scalar(CQ, psum[:, 4, 0:4], D ** -0.5, None, ALU.mult).then_inc(on["e_cq_copied"], 1)
            dve.wait_ge(on["e_cq_copied"], 1)

            def mask_scores(w):
                for n in range(8):
                    half = n // 4
                    if n % 4 == 0:
                        dve.wait_ge(on[f"mask1_loaded{half}"], 16 * (w + 1))
                    dve.wait_ge(on["e_scores"], 8 * w + n + 1)
                    if w >= 2:
                        dve.wait_ge(on["e_turned"], 8 * (w - 1))
                    nc.vector.tensor_tensor_reduce(PE1[w % 2][:, n * 512:(n + 1) * 512], psum[:, n % 4, :],
                                                   MRING[half][:, n % 4 * 512:(n % 4 + 1) * 512], 1.0, -3.0e38,
                                                   ALU.add, ALU.max, EMX[:, 8 * w + n:8 * w + n + 1])\
                      .then_inc(on["e_masked"], 1)
                dve.wait_ge(on["e_masked"], 8 * (w + 1))
                one = slice(w, w + 1)
                mark(nc.vector.tensor_reduce(EM[:, one], EMX[:, 8 * w:8 * w + 8], AX.X, ALU.max))
                done()
                mark(nc.vector.tensor_tensor(ET[:, one], EM[:, one], CQ[:, one], ALU.add))
                done()
                nc.vector.tensor_tensor(ENB[:, one], CQ[:, one], ET[:, one], ALU.subtract).then_inc(on["e_bias"], 1)

            def copy_exps(w):
                for n in range(1, 8, 2):
                    dve.wait_ge(on["e_turned"], 8 * w + n + 1)
                    if w:
                        dve.wait_ge(on["e_att"], w)
                    nc.vector.tensor_copy(PT1[:, n * 512:(n + 1) * 512], psum[:, 5, :]).then_inc(on["e_turned_v"], 1)

            def norm_att(w):
                dve.wait_ge(on["e_exp"], w + 1)
                mark(nc.vector.reciprocal(ERI[:, w:w + 1], ESUM[:, w:w + 1]))
                done()
                dve.wait_ge(on["e_att"], w + 1)
                nc.vector.tensor_scalar(AO[:, w, :], psum[:, 6, 0:256], ERI[:, w:w + 1], None, ALU.mult)\
                  .then_inc(on["e_normed"], 1)

            mask_scores(0)
            for w in range(4):
                if w < 3:
                    mask_scores(w + 1)
                copy_exps(w)
                norm_att(w)
            for i in range(TT):
                dve.wait_ge(on["e_out"], i + 1)
                x_ready(nc.vector.tensor_tensor(X[:, i, :], X[:, i, :], psum[:, i, 0:256], ALU.add))
            dve.wait_ge(on["x_ready"], 4 * TT)

            statistics(X, 1, D)
            for i in range(TT):
                centred(HLE, X, i).then_inc(h_ready, 1)
            dve.wait_ge(on["const_loaded"], 16)
            cos = const("cos").rearrange("p (t d) -> p t d", t=2)
            sin = const("sin").rearrange("p (t d) -> p t d", t=2)
            for piece in range(16):
                which, i, half = piece // 8, piece % 8 // 2, piece % 2
                dve.wait_ge(on["f_qkv"], piece + 1)
                if which:
                    dve.wait_ge(on["f_turned"], 8)
                if piece >= 2:
                    dve.wait_ge(on["f_roped"], piece - 1)
                src = psum[:, piece % 8, :].rearrange("p (h d) -> p h d", h=8)
                out = QTM[:, i, half * HALF:(half + 1) * HALF].rearrange("p (h d) -> p h d", h=8)
                c = cos[:, i % 2, :].unsqueeze(1).broadcast_to((P, 8, DM))
                lo = sin[:, i % 2, 0:DM // 2].unsqueeze(1).broadcast_to((P, 8, DM // 2))
                hi = sin[:, i % 2, DM // 2:DM].unsqueeze(1).broadcast_to((P, 8, DM // 2))
                part = on["f_rope_part"]
                nc.vector.tensor_tensor(T2[piece % 2][:, :, 0:DM // 2], src[:, :, DM // 2:DM], lo, ALU.mult)\
                  .then_inc(part, 1)
                nc.vector.tensor_tensor(T2[piece % 2][:, :, DM // 2:DM], src[:, :, 0:DM // 2], hi, ALU.mult)\
                  .then_inc(part, 1)
                nc.vector.tensor_tensor(out, src, c, ALU.mult).then_inc(part, 1)
            causal = const("causal").rearrange("p (t n) -> p t n", t=2)

            def row_maxima(n):
                dve.wait_ge(on["f_scores"], n + 1)
                src = psum[:, n % 2, :].rearrange("p (t n) -> p t n", t=2)
                if n % HM < 8:
                    if n >= 2:
                        dve.wait_ge(on["f_pt"], n - 1)
                    for qt in range(2):
                        mark(nc.vector.tensor_tensor_reduce(PM[n % 2][:, qt, :], src[:, qt, :], causal[:, qt, :],
                                                            1.0, -3.0e38, ALU.add, ALU.max,
                                                            FMX[:, 2 * n + qt:2 * n + qt + 1]))
                else:
                    mark(nc.vector.tensor_reduce(FMX[:, 2 * n:2 * n + 2], src, AX.X, ALU.max))
                done()
                nc.vector.tensor_scalar(FNB[:, 2 * n:2 * n + 2], FMX[:, 2 * n:2 * n + 2], -(DM ** -0.5), None,
                                        ALU.mult).then_inc(on["f_bias"], 1)

            def copy_turned_exps(n):
                dve.wait_ge(on["f_pt"], n + 1)
                if n >= 2:
                    dve.wait_ge(on["f_pv"], n - 1)
                nc.vector.tensor_copy(PTM[n % 2], psum[:, 2 + n % 2, :].rearrange("p (k n) -> p k n", k=2))\
                  .then_inc(on["f_pt_copied"], 1)

            def norm_heads(o):
                b, half = o // 2, o % 2
                dve.wait_ge(on["f_exp"], 16 * (o + 1))
                cols = slice(16 * o, 16 * (o + 1))
                mark(nc.vector.reciprocal(FRI[:, cols], FSUM[:, cols]))
                done()
                dve.wait_ge(on["f_pv"], 8 * (o + 1))
                ri = FRI[:, cols].rearrange("p (h t) -> p h t", t=2)
                for qt in range(2):
                    out = OTM[:, 2 * b + qt, half * HALF:(half + 1) * HALF].rearrange("p (h d) -> p h d", h=8)
                    nc.vector.tensor_tensor(out, psum[:, 4 + 2 * half + qt, :].rearrange("p (h d) -> p h d", h=8),
                                            ri[:, :, qt].unsqueeze(2).broadcast_to((P, 8, DM)), ALU.mult)\
                      .then_inc(on["f_normed"], 1)

            dve.wait_ge(on["f_turned_copied"], 16)
            row_maxima(0)
            for n in range(32):
                if n < 31:
                    row_maxima(n + 1)
                copy_turned_exps(n)
                if n % 8 == 1 and n > 8:
                    norm_heads(n // 8 - 1)
            norm_heads(3)
            for i in range(TT):
                dve.wait_ge(on["f_out"], i + 1)
                x_ready(nc.vector.tensor_tensor(X[:, i, :], X[:, i, :], psum[:, i, 0:256], ALU.add))
            dve.wait_ge(on["x_ready"], 5 * TT)

            statistics(X, 1, D)
            for i in range(TT):
                centred(HLE, X, i).then_inc(h_ready, 1)
            dve.wait_ge(on["g_logits"], 1)
            logits, hot1, hot2, weights, chosen, slot, pick = R[0], R[1], R[2], R[3], R[4], R[5], R[6]
            best1, best2, gap, egap, den, share1, share2 = R1[0], R1[1], R1[2], R1[3], R1[4], R1[5], R1[6]
            less8 = const("experts").unsqueeze(1).broadcast_to((P, TT, E))

            def over_e(ap):
                return ap.unsqueeze(2).broadcast_to((P, TT, E))

            mark(nc.vector.tensor_copy(logits, psum[:, 0, 0:TT * E].rearrange("p (t e) -> p t e", t=TT)))
            done()
            for best, hot in ((best1, hot1), (best2, hot2)):
                mark(nc.vector.tensor_reduce(best, logits, AX.X, ALU.max))
                done()
                mark(nc.vector.tensor_tensor(pick, logits, over_e(best), ALU.is_equal))
                done()
                mark(nc.vector.tensor_tensor(pick, pick, less8, ALU.mult))
                done()
                mark(nc.vector.tensor_reduce(R1[7], pick, AX.X, ALU.min))
                done()
                mark(nc.vector.tensor_tensor(hot, less8, over_e(R1[7]), ALU.is_equal))
                done()
                if best is best1:
                    mark(nc.vector.scalar_tensor_tensor(out=logits, in0=hot, scalar=-3.0e38, in1=logits,
                                                        op0=ALU.mult, op1=ALU.add))
                    done()
            nc.vector.tensor_tensor(gap, best2, best1, ALU.subtract).then_inc(on["g_logits"], 1)
            dve.wait_ge(on["g_logits"], 3)
            mark(nc.vector.tensor_scalar(den, egap, 1.0, None, ALU.add))
            done()
            mark(nc.vector.reciprocal(share1, den))
            done()
            mark(nc.vector.tensor_tensor(share2, egap, share1, ALU.mult))
            done()
            mark(nc.vector.tensor_tensor(hot1, hot1, over_e(share1), ALU.mult))
            mark(nc.vector.tensor_tensor(hot2, hot2, over_e(share2), ALU.mult))
            done()
            mark(nc.vector.tensor_tensor(weights, hot1, hot2, ALU.add))
            done()
            nc.vector.tensor_scalar(chosen, weights, 0.0, None, ALU.is_gt).then_inc(on["g_chosen"], 1)
            dve.wait_ge(on["g_cum"], 1)
            cum = psum[:, 1, 0:TT * E].rearrange("p (t e) -> p t e", t=TT)
            mark(nc.vector.scalar_tensor_tensor(out=slot, in0=cum, scalar=float(CAP), in1=chosen,
                                                op0=ALU.is_le, op1=ALU.mult))
            done()
            mark(nc.vector.tensor_tensor(slot, slot, cum, ALU.mult))
            done()
            for i in range(TT):
                nc.vector.tensor_tensor(SEL[:, i], slot[:, i, :].unsqueeze(2).broadcast_to((P, E, CAP)),
                                        const("slots").unsqueeze(1).broadcast_to((P, E, CAP)), ALU.is_equal)\
                  .then_inc(on["g_sel"], 1)
            for i in range(TT):
                dve.wait_ge(on["g_sel"], i + 1)
                nc.vector.tensor_tensor(SELW[:, i], SEL[:, i],
                                        weights[:, i, :].unsqueeze(2).broadcast_to((P, E, CAP)), ALU.mult)\
                  .then_inc(on["g_selw"], 1)
            for k in range(4):
                dve.wait_ge(on["g_selt"], k + 1)
                nc.vector.tensor_copy(SELT[:, k, :], psum[:, [0, 1, 0, 1][k], :]).then_inc(on["g_selt_copied"], 1)
            for i in range(TT):
                dve.wait_ge(on["g_out"], i + 1)
                x_ready(nc.vector.tensor_tensor(X[:, i, :], X[:, i, :], psum[:, 4 + i, 0:256], ALU.add))

        @block.tensor
        def _(pe):
            pe.wait_ge(ident_built, 4)
            for c in range(CT):
                for i in range(TT):
                    pe.wait_ge(h_ready, i + 1)
                    last = nc.tensor.transpose(psum[:, 6 + c, i * P:(i + 1) * P], HN[:, i, c * P:(c + 1) * P],
                                               IDENT)
                last.then_inc(ht_psum, 1)
            pe.wait_ge(wq_loaded, 16)
            pe.wait_ge(ht_ready, CT)
            for f in range(CT):
                for c in range(CT):
                    last = nc.tensor.matmul(psum[:, f, :], WQ[:, c, f * P:(f + 1) * P], HT[:, c, :],
                                            start=(c == 0), stop=(c == CT - 1))
                last.then_inc(q_psum, 1)
            pe.wait_ge(mask_step, 4)
            pe.wait_ge(ones_built, 3)
            nc.tensor.matmul(psum[0:1, 5, 0:1], FLAGF[:, 1:2], ONES[:, 0:1], start=True, stop=True)\
              .then_inc(mask_counted, 1)
            pe.wait_ge(mask_flagged, 1)
            any_masked = pe.value_load(FLAG, min_val=0, max_val=1)
            pe.wait_ge(wkv_loaded, 32)
            pe.wait_ge(q_ready, CT)

            def project_k(piece, f, slot, first=False):
                if not first:
                    pe.wait_ge(k_copied, 2 * piece - 2)
                for c in range(CT):
                    last = nc.tensor.matmul(psum[:, f, :], WK[:, c, f * P:(f + 1) * P], CTX[slot][:, c, :],
                                            start=(c == 0), stop=(c == CT - 1))
                last.then_inc(k_psum, 1)

            def project_v(tile, v, bank, slot, banks, first=False):
                if not first:
                    pe.wait_ge(v_copied, tile + (1 - banks))
                for c in range(CT):
                    last = nc.tensor.matmul(psum[:, bank, 0:256], CTX[slot][:, c, v * P:(v + 1) * P],
                                            WV[:, c, :], start=(c == 0), stop=(c == CT - 1))
                last.then_inc(v_psum, 1)

            def scores(n, masked, slot, qh, jh, qt, c, b, first=False):
                if not first:
                    pe.wait_ge(s_maxed, n - 1)
                q = QST[0:ROWS, bass.ds(qh, 1), b * S + qt * P:b * S + (qt + 1) * P]
                k = KST[slot][0:ROWS, bass.ds(jh, 1), c * CH:(c + 1) * CH]
                last = nc.tensor.matmul(SP_(c % 2), q, k, start=True, stop=not masked, skip_group_check=True)
                if masked:
                    last = nc.tensor.matmul(SP_(c % 2), IDENTB, MASKB[:, qt, c * CH:(c + 1) * CH],
                                            start=False, stop=True, skip_group_check=True)
                last.then_inc(s_ready, 1)

            def turn_max(gg):
                pe.wait_ge(m_split, gg + 1)
                if gg:
                    pe.wait_ge(exp_ready, KC * gg)
                for m in range(8):
                    last = nc.tensor.matmul(psum[ROWS:KROWS, 2 + m // 4, (m % 4) * P:(m % 4 + 1) * P],
                                            MPART[:, m, :], IDENTB, start=True, stop=True)
                last.then_inc(m_turned, 1)

            def turned_scores(masked, slot, g, b, kc, u):
                for j in range(G):
                    last = nc.tensor.matmul(ST(u % 2)[:, j // 2, (j % 2) * S:(j % 2 + 1) * S],
                                            KST[slot][0:KROWS, j, bass.ds(kc * P, P)],
                                            QST[0:KROWS, G * g + j, b * S:(b + 1) * S],
                                            start=(j % 2 == 0), stop=not masked and j % 2 == 1,
                                            skip_group_check=True)
                if masked:
                    for bank in range(2):
                        for qt in range(2):
                            out = ST(u % 2)[:, bank, :].rearrange("p (j n) -> p j n", j=2)
                            last = nc.tensor.matmul(out[:, :, qt * P:(qt + 1) * P],
                                                    MASKB[:, qt, bass.ds(kc * P, P)],
                                                    IDENTB.unsqueeze(1).broadcast_to((P, 2, P)),
                                                    start=False, stop=qt == 1, skip_group_check=True)
                last.then_inc(st_ready, 1)

            def weigh_values(n, u, start, stop):
                pe.wait_ge(v_staged, n + 1)
                for j in range(G):
                    last = nc.tensor.matmul(PV[32 * j:32 * (j + 1), :],
                                            VS[u % 4][:, j * VW:j * VW + 32],
                                            PR[u % 2][:, j * S:(j + 1) * S], start=start, stop=stop,
                                            skip_group_check=True)
                last.then_inc(pv_done, 1)

            def first_batch():
                def chunk(i, u, first):
                    pe.wait_ge(ctx_loaded[u], 16 * i + 16)
                    for f in range(CT):
                        project_k(4 * i + (2 * u + f), f, u, first and u == 0)
                    for v in range(4):
                        project_v(8 * i + (4 * u + v), v, 2 + v % 2, u, 2, first and 4 * u + v < 2)
                for u in range(2):
                    chunk(0, u, True)
                with pe.Fori(1, NCH // 2) as i:
                    for u in range(2):
                        chunk(i, u, False)

            def second_batch(masked):
                pe.wait_ge(q_stacked, 96)
                def chunk(i, u, first):
                    pe.wait_ge(ctx_loaded[u], 16 * i + 16 * (NCH // 2 + 1))
                    for f in range(CT):
                        project_k(4 * i + (2 * u + f + 16), f, u)
                    if first and u == 0:
                        pe.wait_ge(k_stacked[0], 96)
                    for c in range(8):
                        scores(16 * i + (8 * u + c), masked, 0, i, i, u, c, 0, first and u == 0 and c < 2)
                for u in range(2):
                    chunk(0, u, True)
                with pe.Fori(1, NCH // 2) as i:
                    for u in range(2):
                        chunk(i, u, False)

            def attend(masked):
                second_batch(masked)
                pe.wait_ge(kones_built, 3)
                for gg in range(NG):
                    b, g, slot = gg // GPB, gg % GPB, gg % 3
                    nb, ng, nslot = (gg + 1) // GPB, (gg + 1) % GPB, (gg + 1) % 3
                    n0 = KC * gg
                    if gg == GPB:
                        def chunk(i, u):
                            pe.wait_ge(ctx_loaded[u], 16 * i + 16 * (NCH + 1))
                            for v in range(4):
                                project_v(8 * i + (4 * u + v + KC), v, v, u, 4)
                        pe.wait_ge(exp_ready, KC * gg)
                        pe.wait_ge(v_copied, KC)
                        with pe.Fori(0, NCH // 2) as i:
                            for u in range(2):
                                chunk(i, u)
                        pe.wait_ge(v_copied, 2 * KC)
                    turn_max(gg)
                    if gg + 1 < NG:
                        pe.wait_ge(k_stacked[nslot], 96 * ((gg + 1) // 3 + 1))
                    pe.wait_ge(m_stacked_a, gg + 1)
                    pe.wait_ge(m_stacked_v, gg + 1)

                    def steps(i, first):
                        for u in range(8):
                            if n0 + u >= 2 or not first:
                                pe.wait_ge(exp_ready, 8 * i + (n0 + u - 1))
                            turned_scores(masked, slot, g, b, 8 * i + u, u)
                            if gg + 1 < NG:
                                for c in (2 * u % 8, 2 * u % 8 + 1):
                                    scores(16 * i + (64 * (gg + 1) + 8 * (u // 4) + c), masked, nslot,
                                           G * ng + i, i, u // 4, c, nb)
                            if first and u == 2 and gg:
                                pe.wait_ge(pv_copied, gg)
                                if gg > 1:
                                    pe.wait_ge(norm_step, 3 * (gg - 1))
                                turn_context(gg - 1)
                            if u == 0 and first:
                                continue
                            if u == 1 and first and gg:
                                pe.wait_ge(pv_copied, gg)
                            pe.wait_ge(exp_ready, 8 * i + (n0 + u))
                            weigh_values(8 * i + (n0 + u - 1), (u - 1) % 8, first and u == 1, False)

                    steps(0, True)
                    with pe.Fori(1, KC // 8) as i:
                        steps(i, False)
                    pe.wait_ge(exp_ready, n0 + KC)
                    weigh_values(n0 + KC - 1, KC - 1, False, True)

            def turn_context(gg):
                for qt in range(2):
                    last = nc.tensor.transpose(PX[:, qt * P:(qt + 1) * P], PVS[:, qt * P:(qt + 1) * P], IDENT)
                last.then_inc(pv_turned, 1)

            first_batch()
            with pe.If(any_masked == 1):
                attend(True)
            with pe.Else():
                attend(False)
            pe.wait_ge(pv_copied, NG)
            pe.wait_ge(norm_step, 3 * (NG - 1))
            turn_context(NG - 1)

            turns = [1]

            def turn(src, need, sem_=None):
                pe.wait_ge(ht_ready, CT * turns[0])
                for c in range(CT):
                    for i in range(TT):
                        if c == 0 and sem_ is not None:
                            pe.wait_ge(sem_, need + i + 1)
                        last = nc.tensor.transpose(psum[:, 6 + c, i * P:(i + 1) * P],
                                                   src[:, i, c * P:(c + 1) * P], IDENT)
                    last.then_inc(ht_psum, 1)
                turns[0] += 1

            def turned():
                pe.wait_ge(ht_ready, CT * turns[0])

            def linear(out, weights, xs, m, name, width=P):
                n = len(xs)
                for k in range(n):
                    last = nc.tensor.matmul(out, weights[:, k, m * P:m * P + width], xs[k],
                                            start=(k == 0), stop=(k == n - 1))
                last.then_inc(on[name], 1)

            def linear_rows(out, lhs, weights, bias, name):
                n = len(lhs)
                if bias is not None:
                    nc.tensor.matmul(out, ONES[0:1, :], bias, start=True, stop=False)
                for k in range(n):
                    last = nc.tensor.matmul(out, lhs[k], weights[:, k, :], start=(k == 0 and bias is None),
                                            stop=(k == n - 1))
                last.then_inc(on[name], 1)

            def tok(ap, i):
                return [ap[:, k, i * P:(i + 1) * P] for k in range(ap.shape[1])]

            pe.wait_ge(norm_step, 3 * NG)
            turn(CTXN, 0)
            turned()
            pe.wait_ge(on["wo_loaded"], 32)
            pe.wait_ge(on["rows_loaded"], 16)
            pe.wait_ge(exp_ready, NG * KC)
            for i in range(TT):
                linear_rows(psum[:, i, 0:256], tok(HTC, i), WO, row("bo")[0:1, :], "b_out")
            pe.wait_ge(on["w_summed"], 2)
            nc.tensor.matmul(psum[:, 4, 0:2], ONES, WSUM, start=True, stop=True).then_inc(on["w_total"], 1)
            turn(HS, TT, h_ready)
            turned()
            pe.wait_ge(on["mix_loaded"], 80)
            pe.wait_ge(on["x_ready"], TT)
            for j in range(8):
                if j == 4:
                    pe.wait_ge(on["w_quantised"], 1)
                linear(psum[:, j, :], WIN, [HTC[:, c, :] for c in range(CT)], (j + IT) % 8, "c_in")
            pe.wait_ge(on["c_a_weights"], 2 + IT * TAPS_A)
            pe.wait_ge(on["c_in_copied"], IT)
            for m in range(IT):
                last = nc.tensor.matmul(psum[0:DS, 1, 0:1], AW[:, m, :], col("dwa_b", m), start=(m == 0),
                                        stop=(m == IT - 1))
            last.then_inc(on["c_a"], 1)
            for m in range(IT):
                for k in range(TAPS_A):
                    src = VAL[:, m, :, 4 + k - LEFT_A:4 + k - LEFT_A + S]
                    last = nc.tensor.matmul(psum[32 * k:32 * k + 32, 0, :].rearrange("p (b n) -> p b n", b=B),
                                            AWK[:, m, k, :], src, start=(m == 0), stop=(m == IT - 1),
                                            tile_position=(0, 32 * k))
            last.then_inc(on["c_a"], 1)
            pe.wait_ge(on["c_a_copied"], 2)
            pe.wait_ge(on["bm_loaded"], 16 * P // DS)
            for m in range(IT):
                pe.wait_ge(on["c_in_copied"], m + 2)
                nc.tensor.matmul(psum[:, 1 + m, :], BM[:, m * P:(m + 1) * P], AS, start=True, stop=True)\
                  .then_inc(on["c_ab"], 1)
            pe.wait_ge(on["c_ab_copied"], IT)
            for m in range(2):
                pe.wait_ge(on["c_in_copied"], 6 + m)
                linear(psum[:, 5 + m, :], WHA, [AB[:, k, :] for k in range(IT)], m, "c_ha")
            pe.wait_ge(on["c_silu"], IT)
            for m in range(IT):
                linear(psum[:, m, :], WPW, [SB[:, k, :] for k in range(IT)], m, "c_pw")
            pe.wait_ge(on["c_pw_copied"], IT)
            pe.wait_ge(on["c_ha_copied"], 1)
            for m in range(2):
                linear(psum[:, 4 + m, :], WHB, [PWO[:, k, :] for k in range(IT)], m, "c_hb")
            pe.wait_ge(on["c_ha_copied"], 2)
            pe.wait_ge(on["c_hb_copied"], 2)
            for m in range(IT):
                linear(psum[:, m, :], WFU, [YC[:, k, :] for k in range(IT)], m, "c_fuse")
            pe.wait_ge(on["c_in_copied"], 8)
            pe.wait_ge(on["c_gated"], IT)
            for i in range(TT):
                linear_rows(psum[:, 4 + i, 0:256], tok(YG, i), WOUT, row("out_b")[0:1, :], "c_out")

            pe.wait_ge(on["x_ready"], 2 * TT)
            for c in range(CT):
                for i in range(TT):
                    if c == 0:
                        pe.wait_ge(on["d_quant"], i + 1)
                    last = nc.tensor.transpose(psum[:, 6 + c, i * 64:(i + 1) * 64].bitcast(BF16),
                                               HQ[:, i, c * P:(c + 1) * P], IDENTB)
                last.then_inc(on["d_turned"], 1)
            pe.wait_ge(on["d_turned_copied"], CT)
            pe.wait_ge(on["w_quantised"], 6)
            for n in range(8):
                i, half = n // 2, n % 2
                for c in range(CT):
                    last = nc.tensor.matmul(psum[:, n, :], HQT[:, c, i * P:(i + 1) * P],
                                            TW1[:, c, half * 512:(half + 1) * 512], start=(c == 0), stop=(c == 1))
                last.then_inc(on["d_up"], 1)
            pe.wait_ge(on["d_hidden"], 8)
            pe.wait_ge(on["d_quant2"], TT)
            for k in range(FT):
                for i in range(TT):
                    last = nc.tensor.transpose(psum[:, k, i * 64:(i + 1) * 64].bitcast(BF16),
                                               QH[:, i, k * P:(k + 1) * P], IDENTB)
                last.then_inc(on["d_turned2"], 1)
            pe.wait_ge(on["d_turned2_copied"], FT)
            for i in range(TT):
                linear_rows(psum[:, i, 0:256], tok(QHT, i), TW2, None, "d_down")

            turn(HLE, 2 * TT, h_ready)
            turned()
            pe.wait_ge(on["l1w_loaded"], 48)
            pe.wait_ge(on["x_ready"], 3 * TT)
            hs = [HTE[:, c, :] for c in range(CT)]
            for f in range(CT):
                linear(psum[:, f, :], WQ1, hs, f, "e_q")
            pe.wait_ge(on["e_q_copied"], CT)
            for c in range(CT):
                linear(psum[:, 2 + c, :], WK1, [QE[:, k, :] for k in range(CT)], c, "e_qc")
            for i in range(TT):
                for k in range(CT):
                    last = nc.tensor.matmul(psum[:, 4, i:i + 1], QE[:, k, i * P:(i + 1) * P], col("bk1", k),
                                            start=(k == 0), stop=(k == CT - 1))
            last.then_inc(on["e_cq"], 1)
            pe.wait_ge(on["e_qc_copied"], CT)

            def key_scores(w):
                pe.wait_ge(on[f"ctxt_loaded{w // 2}"], 16)
                for n in range(8):
                    if 8 * w + n >= 4:
                        pe.wait_ge(on["e_masked"], 8 * w + n - 3)
                    for c in range(CT):
                        last = nc.tensor.matmul(psum[:, n % 4, :], QC[:, c, w * P:(w + 1) * P],
                                                CTXT[w // 2][:, c, n * 512:(n + 1) * 512],
                                                start=(c == 0), stop=(c == CT - 1))
                    last.then_inc(on["e_scores"], 1)

            def turn_exps(w):
                pe.wait_ge(on["e_exp"], w + 1)
                if w == 0:
                    pe.wait_ge(on["e_cq_copied"], 1)
                for n in range(8):
                    m = 4 * w + n // 2
                    if m:
                        pe.wait_ge(on["e_turned_a" if n % 2 == 0 else "e_turned_v"], m)
                    for j in range(4):
                        k = 4 * n + j
                        last = nc.tensor.transpose(psum[:, 4 + n % 2, j * P:(j + 1) * P],
                                                   PE1[w % 2][:, k * P:(k + 1) * P], IDENT)
                    last.then_inc(on["e_turned"], 1)

            def weigh_context(w):
                pe.wait_ge(on[f"ctxk_loaded{w // 2}"], 16)
                if w:
                    pe.wait_ge(on["e_normed"], w)
                for k in range(KC):
                    if k % 8 == 0:
                        pe.wait_ge(on["e_turned_a"], 4 * w + k // 8 + 1)
                        pe.wait_ge(on["e_turned_v"], 4 * w + k // 8 + 1)
                    last = nc.tensor.matmul(psum[:, 6, 0:256], PT1[:, k * P:(k + 1) * P], CTXK[w // 2][:, k, :],
                                            start=(k == 0), stop=(k == KC - 1))
                last.then_inc(on["e_att"], 1)

            key_scores(0)
            for w in range(4):
                if w < 3:
                    key_scores(w + 1)
                turn_exps(w)
                weigh_context(w)
            pe.wait_ge(on["e_normed"], 4)
            turn(AO, 0)
            turned()
            pe.wait_ge(on["bv1_loaded"], 16)
            pe.wait_ge(on["e_masked"], 32)
            for i in range(TT):
                linear_rows(psum[:, i, 0:256], tok(HTE, i), WV1, BV[0:1, :], "e_out")

            turn(HLE, 3 * TT, h_ready)
            turned()
            pe.wait_ge(on["qkv_loaded"], 48)

            def project(which, first_wait):
                for n in range(8):
                    i, half = n // 2, n % 2
                    first_wait(n)
                    for c in range(CT):
                        last = nc.tensor.matmul(psum[:, n, :], HTF[:, c, i * P:(i + 1) * P],
                                                WQKV[which][:, c, half * HALF:(half + 1) * HALF],
                                                start=(c == 0), stop=(c == CT - 1))
                    last.then_inc(on["f_qkv"], 1)

            def turn_heads(base, roped):
                pe.wait_ge(on["f_roped"], roped)
                for k in range(8):
                    for i in range(TT):
                        last = nc.tensor.transpose(psum[:, k, i * P:(i + 1) * P], QTM[:, i, k * P:(k + 1) * P],
                                                   IDENT)
                    last.then_inc(on["f_turned"], 1)

            pe.wait_ge(on["x_ready"], 4 * TT)
            project(0, lambda n: None)
            turn_heads(0, 8)
            project(1, lambda n: pe.wait_ge(on["f_turned_copied"], n + 1))
            turn_heads(8, 16)
            project(2, lambda n: pe.wait_ge(on["f_turned_copied"], 8 + n + 1))
            pe.wait_ge(on["f_v_copied"], 8)

            def unit(n):
                b, h = n // HM, n % HM
                return b, h, 64 * (h % 2), h // 2

            def head_scores(n):
                b, h, p0, k = unit(n)
                if n >= 2:
                    pe.wait_ge(on["f_exp"], 2 * (n - 1))
                for qt in range(2):
                    last = nc.tensor.matmul(psum[:, n % 2, qt * S:(qt + 1) * S],
                                            QT[p0:p0 + DM, k, b * S + qt * P:b * S + (qt + 1) * P],
                                            KT[p0:p0 + DM, k, b * S:(b + 1) * S], start=True, stop=True)
                last.then_inc(on["f_scores"], 1)

            def turn_weights(n):
                pe.wait_ge(on["f_exp"], 2 * (n + 1))
                if n >= 2:
                    pe.wait_ge(on["f_pt_copied"], n - 1)
                for k in range(2):
                    for qt in range(2):
                        last = nc.tensor.transpose(psum[:, 2 + n % 2, k * S + qt * P:k * S + (qt + 1) * P],
                                                   PM[n % 2][:, qt, k * P:(k + 1) * P], IDENT)
                last.then_inc(on["f_pt"], 1)

            def weigh_heads(n):
                b, h, _, _ = unit(n)
                o = n // 8
                if n % 8 == 0 and o >= 2:
                    pe.wait_ge(on["f_normed"], 2 * (o - 1))
                pe.wait_ge(on["f_pt_copied"], n + 1)
                for qt in range(2):
                    for k in range(2):
                        last = nc.tensor.matmul(psum[:, 4 + 2 * (o % 2) + qt, (h % 8) * DM:(h % 8 + 1) * DM],
                                                PTM[n % 2][:, k, qt * P:(qt + 1) * P],
                                                VTM[:, 2 * b + k, h * DM:(h + 1) * DM],
                                                start=(k == 0), stop=(k == 1))
                last.then_inc(on["f_pv"], 1)

            head_scores(0)
            for n in range(32):
                if n < 31:
                    head_scores(n + 1)
                turn_weights(n)
                if n:
                    weigh_heads(n - 1)
            weigh_heads(31)
            pe.wait_ge(on["f_normed"], 8)
            for k in range(8):
                for i in range(TT):
                    last = nc.tensor.transpose(psum[:, k, i * P:(i + 1) * P], OTM[:, i, k * P:(k + 1) * P], IDENT)
                last.then_inc(on["f_ot"], 1)
            pe.wait_ge(on["wom_loaded"], 16)
            pe.wait_ge(on["f_ot_copied"], 8)
            for i in range(TT):
                linear_rows(psum[:, i, 0:256], tok(OT, i), WOM, None, "f_out")

            turn(HLE, 4 * TT, h_ready)
            turned()
            pe.wait_ge(on["emb_loaded"], 16)
            pe.wait_ge(on["x_ready"], 5 * TT)
            for i in range(TT):
                for c in range(CT):
                    last = nc.tensor.matmul(psum[:, 0, i * E:(i + 1) * E], HTF[:, c, i * P:(i + 1) * P], EMB[:, c, :],
                                            start=(c == 0), stop=(c == CT - 1))
            last.then_inc(on["g_logits"], 1)
            pe.wait_ge(on["g_chosen"], 1)
            for i in range(TT):
                for j in range(i + 1):
                    last = nc.tensor.matmul(psum[:, 1, i * E:(i + 1) * E], const("upper") if j == i else ONES,
                                            R[4][:, j, :], start=(j == 0), stop=(j == i))
            last.then_inc(on["g_cum"], 1)
            pe.wait_ge(on["g_sel"], TT)
            for c in range(CT):
                for i in range(TT):
                    last = nc.tensor.matmul(psum[:, 2 + c, :], HLE[:, i, c * P:(c + 1) * P],
                                            SEL[:, i].rearrange("p e s -> p (e s)"), start=(i == 0), stop=(i == TT - 1))
                last.then_inc(on["g_xg"], 1)
            pe.wait_ge(on["g_xg_copied"], CT)
            pe.wait_ge(on["w1e_loaded"], 16 * CT)
            for m in range(IT):
                for e in range(E):
                    for c in range(CT):
                        last = nc.tensor.matmul(psum[:, 4 + m, e * CAP:(e + 1) * CAP],
                                                W1E[:, c, e, m * P:(m + 1) * P], XG[:, c, e * CAP:(e + 1) * CAP],
                                                start=(c == 0), stop=(c == CT - 1))
                last.then_inc(on["g_up"], 1)
            pe.wait_ge(on["g_selw"], TT)
            for k in range(4):
                bank = k % 2
                if k >= 2:
                    pe.wait_ge(on["g_selt_copied"], k - 1)
                for i in range(TT):
                    last = nc.tensor.transpose(psum[:, bank, i * P:(i + 1) * P],
                                               SELW[:, i, 2 * k:2 * k + 2, :].rearrange("p e s -> p (e s)"), IDENT)
                last.then_inc(on["g_selt"], 1)
            pe.wait_ge(on["g_up_copied"], IT)
            pe.wait_ge(on["w2e_loaded"], 16 * IT)
            for k in range(4):
                pe.wait_ge(on["g_selt_copied"], 4)
                for m in range(IT):
                    for e in (2 * k, 2 * k + 1):
                        half = e % 2
                        last = nc.tensor.matmul(psum[CAP * half:CAP * (half + 1), k, 0:256],
                                                INTER[:, m, e * CAP:(e + 1) * CAP], W2E[:, m, e, :],
                                                start=(m == 0), stop=(m == IT - 1), skip_group_check=True)
                last.then_inc(on["g_down"], 1)
            pe.wait_ge(on["g_down_copied"], 4)
            for i in range(TT):
                for k in range(4):
                    last = nc.tensor.matmul(psum[:, 4 + i, 0:256], SELT[:, k, i * P:(i + 1) * P], OE[:, k, :],
                                            start=(k == 0), stop=(k == 3))
                last.then_inc(on["g_out"], 1)


def constants():
    n = np.arange(P)
    freq = (1.0 / np.float32(10000.0) ** (np.arange(0, DM, 2, dtype=np.float32) / np.float32(DM))).astype(np.float32)
    angle = np.arange(S, dtype=np.float32)[:, None] * freq[None, :]
    sign = np.concatenate([-np.ones(DM // 2), np.ones(DM // 2)])
    cos = np.cos(np.concatenate([angle, angle], axis=1).astype(np.float64))
    sin = np.sin(np.concatenate([angle, angle], axis=1).astype(np.float64)) * sign
    later = np.arange(S)[None, :] > np.arange(S)[:, None]
    tables = {"upper": n[:, None] <= n[None, :], "slots": np.tile(np.arange(1, CAP + 1), (P, 1)),
              "experts": np.tile(np.arange(E) - E, (P, 1)),
              "cos": cos.reshape(2, P, DM).transpose(1, 0, 2).reshape(P, -1),
              "sin": sin.reshape(2, P, DM).transpose(1, 0, 2).reshape(P, -1),
              "causal": (later * -1e30).reshape(2, P, S).transpose(1, 0, 2).reshape(P, -1)}
    return np.ascontiguousarray(np.concatenate([tables[k].astype(np.float32) for k in CONSTS], axis=1))


def layout(inputs):
    a = {k: np.asarray(v) for k, v in inputs.items()}
    cols = {"bq": a["L0_xattn_bq"], "bk": a["L0_xattn_bk"], "in_b": a["L0_attn_in_b"],
            "dwa_b": a["L0_attn_dwa_b"], "sym_b": a["L0_attn_sym_b"], "pw_b": a["L0_attn_pw_b"],
            "ha_b": a["L0_attn_ha_b"], "hb_b": a["L0_attn_hb_b"], "fuse_b": a["L0_attn_fuse_b"],
            "norm_w": a["L0_attn_norm_w"],
            "dwa_k": a["L0_attn_dwa_k"].reshape(IT, P, TAPS_A).transpose(0, 2, 1),
            "sym_k": a["L0_attn_sym_k"].reshape(IT, P, TAPS_B).transpose(0, 2, 1),
            "bq1": a["L1_xattn_bq"], "bk1": a["L1_xattn_bk"]}
    rows = {"bo": a["L0_xattn_bo"], "out_b": a["L0_attn_out_b"], "g1": a["L0_ffn_ln1_g"],
            "b1": a["L0_ffn_ln1_b"], "w1b": a["L0_ffn_b1"], "g2": a["L0_ffn_ln2_g"], "b2": a["L0_ffn_ln2_b"],
            "w2b": a["L0_ffn_b2"], "bv": a["L0_xattn_bv"], "bv1": a["L1_xattn_bv"]}
    c = np.ascontiguousarray
    return {
        "x": c(a["x"].reshape(T, D)),
        "cols": c(np.concatenate([cols[n].reshape(COLS[n], P).T for n in COLS], axis=1)),
        "rows": c(np.concatenate([rows[n].reshape(1, -1) for n in ROW_NAMES], axis=1)),
        "wqT": c(a["L0_xattn_Wq"].T), "wkT": c(a["L0_xattn_Wk"].T), "wvT": c(a["L0_xattn_Wv"].T),
        "ctxT": c(a["ctx_1024"].transpose(0, 2, 1)),
        "mask": c(a["mask_1x1xSxS2_if1"].reshape(S, S2)),
        "A": c(a["L0_attn_A"]), "Bm": c(a["L0_attn_Bm"]), "woT": c(a["L0_xattn_Wo"].T),
        "winT": c(a["L0_attn_in_w"].T), "wpwT": c(a["L0_attn_pw_w"].T), "whaT": c(a["L0_attn_ha_w"].T),
        "whbT": c(a["L0_attn_hb_w"].T), "wfuT": c(a["L0_attn_fuse_w"].T), "woutT": c(a["L0_attn_out_w"].T),
        "w1T": c(a["L0_ffn_w1"].T), "w2T": c(a["L0_ffn_w2"].T),
        "wq1T": c(a["L1_xattn_Wq"].T), "wk1": c(a["L1_xattn_Wk"]), "wv1T": c(a["L1_xattn_Wv"].T),
        "ctx": c(a["ctx_1024"]), "mask1": c(a["mask_SxS2_ff0"]),
        "wqm": c(a["L1_attn_Wq"]), "wkm": c(a["L1_attn_Wk"]), "wvm": c(a["L1_attn_Wv"]), "wom": c(a["L1_attn_Wo"]),
        "embT": c(a["L1_ffn_expert_embeddings"].T), "w1e": c(a["L1_ffn_first_linear"].transpose(0, 2, 1)),
        "w2e": c(a["L1_ffn_second_linear"].transpose(0, 2, 1)), "consts": constants(),
    }


def kernel(**inputs):
    import concourse.bacc as bacc
    from concourse.bass_utils import run_bass_kernel_spmd

    nc = bacc.Bacc("TRN2", target_bir_lowering=False, num_devices=1)
    arrays = layout(inputs)
    tensors = {name: nc.dram_tensor(name, a.shape, mybir.dt.from_np(a.dtype), kind="ExternalInput").ap()
               for name, a in arrays.items()}
    tensors["out"] = nc.dram_tensor("out", (T, D), F32, kind="ExternalOutput").ap()
    build(nc, tensors)
    got = run_bass_kernel_spmd(nc, [arrays], core_ids=[0])
    return got.results[0]["out"].reshape(B, S, D)
```

```python
from contextlib import ExitStack

import numpy as np

import concourse.bass as bass
from concourse import mybir

F32 = mybir.dt.float32
BF16 = mybir.dt.bfloat16
I32 = mybir.dt.int32
ALU = mybir.AluOpType
ACT = mybir.ActivationFunctionType
AX = mybir.AxisListType

P = 128
B, S, S2, D = 2, 256, 4096, 256
T = B * S
TT = T // P
CT = D // P
H, DH = 16, 16
G = 4
GPB = H // G
NG = B * GPB
KC = S2 // P
CH = 512
NCH = S2 // CH
ROWS = 6 * DH
KROWS = ROWS + 3
VW = DH + 1
MASKED = -(2.0 ** 100)
K_PARTS = (0, 0, 0, 1, 1, 2)
Q_PARTS = (0, 1, 2, 0, 1, 0)

DI = 512
IT = DI // P
DS = 16
TAPS_A, LEFT_A = 4, 1
TAPS_B, LEFT_B = 9, 4
PAD = S + 8
FF = 1024
FT = FF // P
HM, DM = 16, 64
HALF = HM * DM // 2
E, EI, CAP = 8, 512, T // 8
ROUND = 1.5 * 2.0 ** 23

COLS = {"bq": 2, "bk": 2, "in_b": 8, "dwa_b": 4, "sym_b": 4, "pw_b": 4, "ha_b": 2, "hb_b": 2,
        "fuse_b": 4, "norm_w": 2, "dwa_k": 16, "sym_k": 36, "bq1": 2, "bk1": 2}
ROW_NAMES = {"bo": 256, "out_b": 256, "g1": 256, "b1": 256, "w1b": 1024, "g2": 1024, "b2": 1024,
             "w2b": 256, "bv": 256, "bv1": 256}
CONSTS = {"upper": P, "slots": CAP, "experts": E, "cos": 2 * DM, "sin": 2 * DM, "causal": 2 * S}


def offsets(sizes):
    at, out = 0, {}
    for name, n in sizes.items():
        out[name] = at
        at += n
    return out, at


COL_AT, N_COLS = offsets(COLS)
ROW_AT, N_ROWS = offsets(ROW_NAMES)
CONST_AT, N_CONSTS = offsets(CONSTS)
N_FFN_ROWS = ROW_AT["bv"]


def build(nc, t):
    ctx = ExitStack()
    with ctx:
        arena = ctx.enter_context(nc.sbuf_tensor("arena", [P, 53120], F32))
        psum = ctx.enter_context(nc.psum_tensor("psum", [P, 8, 512], F32))

        def sem(name):
            return ctx.enter_context(nc.semaphore(name))

        def f32(at, n):
            return arena[:, at:at + n]

        def b16(at, n):
            return arena[:, at:at + n // 2].bitcast(BF16)

        KST = [b16(8192 * i, 16384).rearrange("p (j n) -> p j n", j=G) for i in range(3)]
        V_AT = 24576
        V = f32(V_AT, KC * H * VW).rearrange("p (k h e) -> p k h e", k=KC, h=H)
        V_flat = f32(V_AT, KC * H * VW + 16)
        MASKB = b16(33296, 8192).rearrange("p (t n) -> p t n", t=2)
        QST = b16(37392, 8192).rearrange("p (h n) -> p h n", h=H)
        PR = [f32(41488 + 1024 * i, 1024) for i in range(2)]
        CTX = [f32(43536 + 1024 * i, 1024).rearrange("p (c n) -> p c n", c=CT) for i in range(2)]
        K32 = [f32(45584 + 512 * i, 512) for i in range(2)]
        KPT = [b16(46608 + 768 * i, 1536).rearrange("p (r n) -> p r n", r=3) for i in range(2)]
        X = f32(48144, 1024).rearrange("p (t c) -> p t c", t=TT)
        PVS = f32(49168, 256)
        CTXN = f32(49424, 1024).rearrange("p (t c) -> p t c", t=TT)
        at = 50448
        IDENT = f32(at, 128); at += 128
        IDENTB = b16(at, 128); at += 64
        COLT = f32(at, N_COLS); at += N_COLS
        BV = f32(at, 256); at += 256
        MX = [f32(at + 64 * i, 64) for i in range(2)]; at += 128
        M8 = f32(at, 8); at += 8
        MR = f32(at, 8); at += 8
        MPART = b16(at, 24).rearrange("p (m r) -> p m r", r=3); at += 12
        RINV = f32(at, 8).rearrange("p (t j) -> p t j", t=2); at += 8
        BN = f32(at, 48); at += 48
        MV = f32(at, 8); at += 8
        SD = f32(at, 8); at += 8
        FLAGF = f32(at, 4); at += 4
        VS = [f32(at + 84 * i, 84) for i in range(4)]; at += 336
        FLAG = arena[0:1, at:at + 1].bitcast(I32); at += 1
        ONES = f32(at, 128); at += 128
        AW = f32(at, IT * DS).rearrange("p (t s) -> p t s", t=IT); at += IT * DS
        assert at <= 52096, at
        MASKI = arena[:, 16384:16384 + 8192].bitcast(I32).rearrange("p (t n) -> p t n", t=2)
        HN = f32(41488, 1024).rearrange("p (t c) -> p t c", t=TT)
        HT = f32(42512, 1024).rearrange("p (c n) -> p c n", c=CT)
        WQ = f32(8192, 512).rearrange("p (c f) -> p c f", c=CT)
        WK = f32(52096, 512).rearrange("p (c f) -> p c f", c=CT)
        WV = f32(52608, 512).rearrange("p (c f) -> p c f", c=CT)

        def col(name, i):
            return COLT[:, COL_AT[name] + i:COL_AT[name] + i + 1]

        def ST(i):
            return psum[:, 2 * i:2 * i + 2, :]

        def SP_(i):
            return psum[:, 4 + i, :]

        PV = psum[:, 6, 0:256]
        PX = psum[:, 7, :]

        ROWS_T = f32(0, N_FFN_ROWS)

        def row(name):
            return ROWS_T[:, ROW_AT[name]:ROW_AT[name] + ROW_NAMES[name]]

        WO = f32(4352, 512).rearrange("p (c f) -> p c f", c=CT)
        WOUT = f32(4864, 1024).rearrange("p (t f) -> p t f", t=IT)
        TW1 = b16(5888, 2048).rearrange("p (c f) -> p c f", c=CT)
        TW2 = b16(6912, 2048).rearrange("p (t f) -> p t f", t=FT)
        WIN = f32(16384, 2048).rearrange("p (c f) -> p c f", c=CT)
        WPW = f32(18432, 2048).rearrange("p (t f) -> p t f", t=IT)
        WHA = f32(20480, 1024).rearrange("p (t f) -> p t f", t=IT)
        WHB = f32(21504, 1024).rearrange("p (t f) -> p t f", t=IT)
        WFU = f32(22528, 2048).rearrange("p (t f) -> p t f", t=IT)
        W1RAW = f32(43536, 2048)
        W2RAW = f32(45584, 2048)
        BM = f32(47632, 512)
        HL = f32(24576, 1024).rearrange("p (t c) -> p t c", t=TT)
        HS = f32(25600, 1024).rearrange("p (t c) -> p t c", t=TT)
        HTC = f32(26624, 1024).rearrange("p (c n) -> p c n", c=CT)
        GATE = f32(27648, 2048).rearrange("p (m n) -> p m n", m=IT)
        VAL = f32(29696, IT * B * PAD).rearrange("p (m b n) -> p m b n", m=IT, b=B)
        AWK = f32(31808, IT * TAPS_A * 32).rearrange("p (m k s) -> p m k s", m=IT, k=TAPS_A)
        CB = f32(33856, 2048).rearrange("p (m n) -> p m n", m=IT)
        SB = f32(35904, 2048).rearrange("p (m n) -> p m n", m=IT)
        PWO = f32(37952, 2048).rearrange("p (m n) -> p m n", m=IT)
        AS = f32(40000, 512)
        AB = f32(40512, 2048).rearrange("p (m n) -> p m n", m=IT)
        YC = f32(31808, 2048).rearrange("p (m n) -> p m n", m=IT)
        YG = CB
        HQ = b16(25600, 1024).rearrange("p (t c) -> p t c", t=TT)
        HQT = b16(26112, 1024).rearrange("p (c n) -> p c n", c=CT)
        UH = f32(26624, 4096).rearrange("p (t f) -> p t f", t=TT)
        QH = b16(30720, 4096).rearrange("p (t f) -> p t f", t=TT)
        QHT = b16(32768, 4096).rearrange("p (k n) -> p k n", k=FT)
        CTXT = [f32(8192, 8192).rearrange("p (c n) -> p c n", c=CT), f32(0, 8192).rearrange("p (c n) -> p c n", c=CT)]
        CTXK = [f32(16384, 8192).rearrange("p (k c) -> p k c", k=KC), f32(8192, 8192).rearrange("p (k c) -> p k c", k=KC)]
        PE1 = [f32(24576 + 4096 * i, 4096) for i in range(2)]
        QE = f32(32768, 1024).rearrange("p (c n) -> p c n", c=CT)
        QC = f32(33792, 1024).rearrange("p (c n) -> p c n", c=CT)
        MRING = [f32(34816 + 2048 * i, 2048) for i in range(2)]
        PT1 = f32(38912, 4096)
        WQ1 = f32(43536, 512).rearrange("p (c f) -> p c f", c=CT)
        WK1 = f32(44048, 512).rearrange("p (c f) -> p c f", c=CT)
        WV1 = f32(44560, 512).rearrange("p (c f) -> p c f", c=CT)
        HTE = f32(45072, 1024).rearrange("p (c n) -> p c n", c=CT)
        AO = f32(46096, 1024).rearrange("p (t c) -> p t c", t=TT)
        HLE = CTXN
        WQKV = [f32(16384 + 2048 * i, 2048).rearrange("p (c f) -> p c f", c=CT) for i in range(3)]
        WOM = f32(22528, 2048).rearrange("p (k f) -> p k f", k=8)
        VTM = f32(24576, 4096).rearrange("p (t f) -> p t f", t=TT)
        QTM = f32(28672, 4096).rearrange("p (t f) -> p t f", t=TT)
        QT = f32(32768, 4096).rearrange("p (k n) -> p k n", k=8)
        OT = QT
        KT = f32(36864, 4096).rearrange("p (k n) -> p k n", k=8)
        PM = [f32(at, 512).rearrange("p (t n) -> p t n", t=2) for at in (40960, 41472, 46096, 46608)]
        PTM = [f32(at, 512).rearrange("p (k n) -> p k n", k=2) for at in (41984, 42496, 45072, 45584)]
        HEAD_SCORES = [psum[:, bank, :] for bank in (0, 1, 6, 7)]
        T2 = [f32(45072 + 512 * i, 512).rearrange("p (h d) -> p h d", h=8) for i in range(2)]
        HTF = f32(43536, 1024).rearrange("p (c n) -> p c n", c=CT)
        CONST = f32(47120, N_CONSTS)

        def const(name):
            return CONST[:, CONST_AT[name]:CONST_AT[name] + CONSTS[name]]

        W1E = f32(0, 8192).rearrange("p (c e i) -> p c e i", c=CT, e=E)
        W2E = f32(8192, 8192).rearrange("p (t e h) -> p t e h", t=IT, e=E)
        EMB = f32(44560, 16).rearrange("p (c e) -> p c e", c=CT)
        SEL = f32(24576, 2048).rearrange("p (t e s) -> p t e s", t=TT, e=E)
        SELW = f32(26624, 2048).rearrange("p (t e s) -> p t e s", t=TT, e=E)
        SELT = f32(28672, 2048).rearrange("p (k n) -> p k n", k=4)
        XG = f32(30720, 1024).rearrange("p (c n) -> p c n", c=CT)
        INTER = f32(31744, 2048).rearrange("p (t n) -> p t n", t=IT)
        OE = f32(33792, 1024).rearrange("p (k c) -> p k c", k=4)
        R = [f32(34816 + 32 * i, 32).rearrange("p (t e) -> p t e", e=E) for i in range(12)]
        R1 = [f32(35200 + 4 * i, 4) for i in range(8)]
        assert 47120 + N_CONSTS <= 48144
        at = 52096
        AMAX = f32(at, 4); at += 4
        QSC = f32(at, 4); at += 4
        OSC = f32(at, 4); at += 4
        MS = f32(at, 4); at += 4
        CQ = f32(at, 4); at += 4
        EMX = f32(at, 32); at += 32
        EM = f32(at, 4); at += 4
        ET = f32(at, 4); at += 4
        ENB = f32(at, 4); at += 4
        ESUM = f32(at, 4); at += 4
        ERI = f32(at, 4); at += 4
        FMX = f32(at, 64); at += 64
        FNB = f32(at, 64); at += 64
        FSUM = f32(at, 64); at += 64
        FRI = f32(at, 64); at += 64
        WSUM = f32(at, 2); at += 2
        WMEAN = f32(at, 2); at += 2
        WSC = f32(at, 2); at += 2
        ABIAS = f32(at, 1); at += 1
        assert at <= 53120

        STACK0 = 96 * NCH // 2
        kparts = nc.dram_tensor("kparts", [B, 3, D, S2], BF16, kind="Internal").ap()
        qparts = nc.dram_tensor("qparts", [3, D, T], BF16, kind="Internal").ap()

        x_loaded = sem("x_loaded")
        cols_loaded = sem("cols_loaded")
        wq_loaded = sem("wq_loaded")
        wkv_loaded = sem("wkv_loaded")
        mask_loaded = sem("mask_loaded")
        ident_built = sem("ident_built")
        ones_built = sem("ones_built")
        kones_built = sem("kones_built")
        mask_counted = sem("mask_counted")
        mask_flagged = sem("mask_flagged")
        mask_step = sem("mask_step")
        ln_step = sem("ln_step")
        ln_var = sem("ln_var")
        ln_sd = sem("ln_sd")
        h_ready = sem("h_ready")
        ht_psum = sem("ht_psum")
        ht_ready = sem("ht_ready")
        q_psum = sem("q_psum")
        q_split = sem("q_split")
        q_ready = sem("q_ready")
        q_stacked = sem("q_stacked")
        ctx_loaded = [sem(f"ctx_loaded{i}") for i in range(2)]
        k_psum = sem("k_psum")
        k_copied = sem("k_copied")
        k_rest = sem("k_rest")
        k_middle = sem("k_middle")
        k_low = sem("k_low")
        k_stored = [sem(f"k_stored{i}") for i in range(2)]
        v_psum = sem("v_psum")
        v_copied = sem("v_copied")
        k_stacked = [sem(f"k_stacked{i}") for i in range(3)]
        s_ready = sem("s_ready")
        s_maxed = sem("s_maxed")
        m_step = sem("m_step")
        m_split = sem("m_split")
        m_turned = sem("m_turned")
        m_stacked = sem("m_stacked")
        st_ready = sem("st_ready")
        exp_ready = sem("exp_ready")
        pv_done = sem("pv_done")
        pv_copied = sem("pv_copied")
        pv_turned = sem("pv_turned")
        norm_step = sem("norm_step")
        v_staged = sem("v_staged")
        out_stored = sem("out_stored")
        SIGNALS = """
            aw_loaded bm_loaded raw_loaded mix_loaded rows_loaded wo_loaded bv1_loaded l1w_loaded
            ctxt_loaded0 ctxt_loaded1 ctxk_loaded0 ctxk_loaded1 mask1_loaded0 mask1_loaded1
            qkv_loaded wom_loaded const_loaded emb_loaded w1e_loaded w2e_loaded
            w_summed w_total w_quantised
            b_out x_ready sq_ready
            c_padded c_in c_in_copied c_a_weights c_conv_b c_sigmoid c_silu c_a c_a_copied c_ab
            c_ab_copied c_ha c_ha_copied c_pw c_pw_copied c_hb c_hb_copied c_fuse c_gated c_out
            d_quant d_turned d_turned_copied d_up d_hidden d_gelu d_quant2 d_turned2
            d_turned2_copied d_down
            e_q e_q_copied e_qc e_qc_copied e_cq e_cq_copied e_scores e_masked e_bias e_exp
            e_turned e_turned_a e_turned_v e_att e_normed e_out
            f_qkv f_roped f_rope_part f_v_copied f_turned f_turned_copied f_scores f_masked f_bias f_exp
            f_scaled f_pt f_pt_copied f_pv f_pv_copied f_out
            g_logits g_chosen g_cum g_sel g_selw g_xg g_xg_copied g_up g_up_copied g_down
            g_down_copied g_selt g_selt_copied g_out step_v
        """.split()
        on = {name: sem(name) for name in SIGNALS}

        def by_part_of(ap):
            return ap.rearrange("(c p) n -> p c n", p=P)

        block = ctx.enter_context(nc.Block())

        @block.sync
        def _(sp):
            sp.dma_start(X, t["x"].rearrange("(t p) c -> p t c", p=P)).then_inc(x_loaded, 16)
            sp.dma_start(COLT, t["cols"]).then_inc(cols_loaded, 16)
            sp.dma_start(AW, t["A"].rearrange("(t p) s -> p t s", p=P)).then_inc(on["aw_loaded"], 16)
            sp.dma_start(BV, t["rows"][:, ROW_AT["bv"]:ROW_AT["bv"] + 256].broadcast_to((P, 256)))\
              .then_inc(cols_loaded, 16)
            sp.dma_start(WQ, t["wqT"].rearrange("(c p) f -> p c f", p=P)).then_inc(wq_loaded, 16)
            sp.dma_start(WK, t["wkT"].rearrange("(c p) f -> p c f", p=P)).then_inc(wkv_loaded, 16)
            sp.dma_start(WV, t["wvT"].rearrange("(c p) f -> p c f", p=P)).then_inc(wkv_loaded, 16)

            def load_ctx(b, ch, slot):
                sp.dma_start(CTX[slot], t["ctxT"][b].rearrange("(c p) n -> p c n", p=P)
                             [:, :, bass.ds(ch * CH, CH)]).then_inc(ctx_loaded[slot], 16)

            def store_k(b, ch, f):
                piece = 16 * b + 2 * ch + f
                sp.wait_ge(k_low, piece + 1)
                sp.dma_start(kparts[b, :, f * P:(f + 1) * P, bass.ds(ch * CH, CH)]
                             .rearrange("r p n -> p r n"), KPT[f]).then_inc(k_stored[f], 16)

            def store_q():
                for f in range(CT):
                    sp.wait_ge(q_ready, f + 1)
                    sp.dma_start(qparts[:, f * P:(f + 1) * P, :].rearrange("r p n -> p r n"), KPT[f])\
                      .then_inc(k_stored[f], 16)
                for f in range(CT):
                    sp.wait_ge(k_stored[f], 16)
                for r in range(6):
                    sp.dma_start(QST[DH * r:DH * (r + 1), :, :],
                                 qparts[Q_PARTS[r]].rearrange("(h d) n -> d h n", d=DH)).then_inc(q_stacked, 16)

            def load_first_stack(i):
                for r in range(6):
                    src = kparts[0, K_PARTS[r], 0:G * DH, bass.ds(i * 2 * CH, 2 * CH)]
                    sp.dma_start(KST[0][DH * r:DH * (r + 1), :, bass.ds(i * 2 * CH, 2 * CH)],
                                 src.rearrange("(j d) n -> d j n", d=DH)).then_inc(k_stacked[0], 16)

            def load_stack(gg):
                b, g, slot = gg // GPB, gg % GPB, gg % 3
                for r in range(6):
                    src = kparts[b, K_PARTS[r], g * G * DH:(g + 1) * G * DH, :]
                    sp.dma_start(KST[slot][DH * r:DH * (r + 1), :, :],
                                 src.rearrange("(j d) n -> d j n", d=DH)).then_inc(k_stacked[slot], 16)

            load_ctx(0, 0, 0)
            load_ctx(0, 1, 1)
            sp.dma_start(MASKI, t["mask"].rearrange("(t p) n -> p t n", p=P)).then_inc(mask_loaded, 16)
            store_q()
            for b in range(B):
                def chunk_pair(i, more, first=False):
                    for u in range(2):
                        if b == 1 and more:
                            sp.wait_ge(k_psum, 4 * i + (2 * u + 18))
                            load_ctx(b, 2 * i + (u + 2), u)
                        for f in range(CT):
                            store_k(b, 2 * i + u, f)
                        if b == 0 and u == 0 and not first:
                            sp.wait_ge(k_stored[0], 32 * i + 16)
                            load_first_stack(i - 1)
                        if b == 0:
                            sp.wait_ge(v_psum, 8 * i + (4 * u + 4))
                            if more:
                                load_ctx(b, 2 * i + (u + 2), u)
                chunk_pair(0, True, True)
                with sp.Fori(1, NCH // 2 - 1) as i:
                    chunk_pair(i, True)
                chunk_pair(NCH // 2 - 1, False)
                if b == 0:
                    load_ctx(1, 0, 0)
                    load_ctx(1, 1, 1)
                for f in range(CT):
                    sp.wait_ge(k_stored[f], 16 + 16 * NCH * (b + 1))
                if b == 0:
                    load_first_stack(NCH // 2 - 1)
                    sp.wait_ge(q_psum, CT)
                    load_stack(1)
            sp.wait_ge(mask_step, 2 * NCH)
            load_stack(2)
            load_ctx(1, 0, 0)
            load_ctx(1, 1, 1)
            sp.wait_ge(st_ready, KC)
            load_stack(3)
            sp.wait_ge(st_ready, 2 * KC)
            load_stack(4)
            sp.wait_ge(st_ready, 3 * KC)
            load_stack(5)
            with sp.Fori(0, NCH // 2 - 1) as i:
                for u in range(2):
                    sp.wait_ge(v_psum, KC + 8 * i + 4 * u + 4)
                    load_ctx(1, 2 * i + u + 2, u)
            sp.wait_ge(st_ready, 4 * KC)
            load_stack(6)
            sp.wait_ge(st_ready, 5 * KC)
            load_stack(7)

            def load(dst, src, name):
                sp.dma_start(dst, src).then_inc(on[name], 16)

            def by_part(name):
                return t[name].rearrange("(c p) f -> p c f", p=P)

            sp.wait_ge(v_psum, 2 * KC)
            load(W1RAW.rearrange("p (c f) -> p c f", c=CT), by_part("w1T"), "raw_loaded")
            load(W2RAW.rearrange("p (c f) -> p c f", c=FT), by_part("w2T"), "raw_loaded")
            for copy in range(P // DS):
                load(BM[copy * DS:(copy + 1) * DS, :], t["Bm"], "bm_loaded")
            sp.wait_ge(st_ready, 6 * KC)
            for dst, name in ((WIN, "winT"), (WPW, "wpwT"), (WHA, "whaT"), (WHB, "whbT"), (WFU, "wfuT")):
                load(dst, by_part(name), "mix_loaded")
            sp.wait_ge(st_ready, 7 * KC)
            load(WO, by_part("woT"), "wo_loaded")
            load(WOUT, by_part("woutT"), "wo_loaded")
            load(ROWS_T, t["rows"][:, 0:N_FFN_ROWS].broadcast_to((P, N_FFN_ROWS)), "rows_loaded")
            sp.wait_ge(st_ready, 8 * KC)
            load(CTXT[0], by_part_of(t["ctxT"][0]), "ctxt_loaded0")
            sp.wait_ge(norm_step, 3 * NG)
            load(BV, t["rows"][:, ROW_AT["bv1"]:ROW_AT["bv1"] + 256].broadcast_to((P, 256)), "bv1_loaded")
            sp.wait_ge(on["w_quantised"], 6)
            load(WQ1, by_part("wq1T"), "l1w_loaded")
            load(WK1, by_part("wk1"), "l1w_loaded")
            load(WV1, by_part("wv1T"), "l1w_loaded")
            sp.wait_ge(on["c_ab"], 4)
            load(CONST, t["consts"], "const_loaded")
            sp.wait_ge(on["c_fuse"], 4)
            load(CTXK[0], t["ctx"][0].rearrange("(k p) c -> p k c", p=P), "ctxk_loaded0")
            sp.wait_ge(on["c_out"], 4)

            def load_mask(n):
                unit, half = n // 2, n % 2
                if n >= 2:
                    sp.wait_ge(on["e_masked"], 4 * (n - 1))
                qt = unit % 2
                load(MRING[half], t["mask1"][qt * P:(qt + 1) * P, half * 2048:(half + 1) * 2048],
                     f"mask1_loaded{half}")

            load_mask(0)
            load_mask(1)
            sp.wait_ge(on["x_ready"], 3 * TT)
            load(CTXT[1], by_part_of(t["ctxT"][1]), "ctxt_loaded1")
            for n in range(2, 4):
                load_mask(n)
            sp.wait_ge(on["e_scores"], 16)
            load(CTXK[1], t["ctx"][1].rearrange("(k p) c -> p k c", p=P), "ctxk_loaded1")
            for n in range(4, 6):
                load_mask(n)
            sp.wait_ge(on["e_att"], 2)
            for dst, name in zip(WQKV, ("wqm", "wkm", "wvm")):
                load(dst, by_part(name), "qkv_loaded")
            load(WOM, by_part("wom"), "wom_loaded")
            for n in range(6, 8):
                load_mask(n)
            sp.wait_ge(on["e_scores"], 32)
            for k in range(CT):
                load(W1E[:, k], t["w1e"][:, k * P:(k + 1) * P, :].rearrange("e p i -> p e i"), "w1e_loaded")
            sp.wait_ge(on["e_att"], 4)
            for k in range(IT):
                load(W2E[:, k], t["w2e"][:, k * P:(k + 1) * P, :].rearrange("e p h -> p e h"), "w2e_loaded")
            sp.wait_ge(on["e_out"], 4)
            load(EMB, by_part("embT"), "emb_loaded")
            sp.wait_ge(on["x_ready"], 6 * TT)
            sp.dma_start(t["out"].rearrange("(t p) c -> p t c", p=P), X).then_inc(out_stored, 16)
            sp.wait_ge(out_stored, 16)

        @block.gpsimd
        def _(pool):
            nc.gpsimd.memset(IDENT, 0.0).then_inc(ident_built, 1)
            nc.gpsimd.memset(IDENTB, 0.0).then_inc(ident_built, 1)
            nc.gpsimd.memset(ONES, 1.0).then_inc(ones_built, 1)
            pool.wait_ge(ident_built, 2)
            for m in (IDENT, IDENTB):
                nc.gpsimd.affine_select(out=m, in_=m, compare_op=ALU.not_equal, fill=1.0, base=0,
                                        pattern=[[-1, P]], channel_multiplier=1).then_inc(ident_built, 1)
            nc.gpsimd.memset(V[:, :, :, DH:VW], 1.0).then_inc(ones_built, 1)
            nc.gpsimd.memset(V_flat[:, KC * H * VW:KC * H * VW + 16], 0.0).then_inc(ones_built, 1)
            two_ones = float(np.array([0x3F803F80], np.uint32).view(np.float32)[0])
            pool.wait_ge(ones_built, 3)
            nc.gpsimd.memset(arena[ROWS:KROWS, 0:8192], two_ones).then_inc(kones_built, 1)
            pool.wait_ge(kones_built, 1)
            nc.gpsimd.memset(arena[ROWS:KROWS, 8192 + 512:16384], two_ones).then_inc(kones_built, 1)
            pool.wait_ge(kones_built, 2)

            def low_part(piece, f):
                pool.wait_ge(k_middle, piece + 1)
                nc.gpsimd.tensor_tensor(KPT[f][:, 2, :], K32[f], KPT[f][:, 1, :], ALU.subtract)\
                  .then_inc(k_low, 1)

            with pool.Fori(0, NCH) as i:
                for f in range(CT):
                    low_part(2 * i + f, f)
            pool.wait_ge(k_low, 2 * NCH)
            pool.wait_ge(q_psum, CT)
            nc.gpsimd.memset(arena[ROWS:KROWS, 8192:8192 + 512], two_ones).then_inc(kones_built, 1)
            pool.wait_ge(kones_built, 3)
            with pool.Fori(0, NCH) as i:
                for f in range(CT):
                    low_part(2 * i + f + 16, f)
            for gg in range(NG):
                g, n0 = gg % GPB, KC * gg
                pool.wait_ge(v_copied, KC * (gg // GPB + 1))

                def stage_values(i, first):
                    for u in range(8):
                        if not first or n0 + u >= 4:
                            pool.wait_ge(pv_done, 8 * i + (n0 + u - 3))
                        nc.gpsimd.tensor_copy(VS[u % 4], V_flat[:, bass.ds(i * (8 * H * VW) + (u * H * VW + g * G * VW), 84)])\
                          .then_inc(v_staged, 1)
                        if first and gg < 2 and u % 2:
                            if gg == 0 and u == 1:
                                pool.wait_ge(mask_step, 2 * NCH)
                            pool.wait_ge(v_staged, n0 + u + 1)
                            piece = 16384 + 1024 * (4 * gg + u // 2)
                            nc.gpsimd.memset(arena[ROWS:KROWS, piece:piece + 1024], two_ones).then_inc(kones_built, 1)
                            pool.wait_ge(kones_built, 4 + 4 * gg + u // 2)
                stage_values(0, True)
                with pool.Fori(1, KC // 8) as i:
                    stage_values(i, False)

            pool.wait_ge(pv_done, NG * KC)
            pool.wait_ge(v_staged, NG * KC)
            nc.gpsimd.memset(VAL[:, :, :, 0:4], 0.0).then_inc(on["c_padded"], 1)
            nc.gpsimd.memset(VAL[:, :, :, S + 4:PAD], 0.0).then_inc(on["c_padded"], 1)
            pool.wait_ge(on["c_padded"], 2)

            nc.gpsimd.memset(AWK, 0.0).then_inc(on["c_a_weights"], 1)
            nc.gpsimd.memset(ABIAS, 0.0).then_inc(on["c_a_weights"], 1)
            pool.wait_ge(on["c_a_weights"], 2)
            pool.wait_ge(on["aw_loaded"], 16)
            for m in range(IT):
                for k in range(TAPS_A):
                    nc.gpsimd.tensor_scalar(AWK[:, m, k, 0:DS], AW[:, m, :], col("dwa_k", TAPS_A * m + k), None,
                                            ALU.mult).then_inc(on["c_a_weights"], 1)

            for piece in range(16):
                pool.wait_ge(on["f_rope_part"], 3 * (piece + 1))
                i, half = piece % 8 // 2, piece % 2
                out = QTM[:, i, half * HALF:(half + 1) * HALF].rearrange("p (h d) -> p h d", h=8)
                nc.gpsimd.tensor_tensor(out, out, T2[piece % 2], ALU.add).then_inc(on["f_roped"], 1)

        @block.scalar
        def _(act):
            act.wait_ge(ln_var, 1)
            nc.scalar.activation(SD[:, 0:4], SD[:, 4:8], ACT.Sqrt).then_inc(ln_sd, 1)
            for c in range(CT):
                act.wait_ge(ht_psum, c + 1)
                nc.scalar.activation(HT[:, c, :], psum[:, 6 + c, :], ACT.Copy).then_inc(ht_ready, 1)

            def copy_k(piece, f, reuse):
                act.wait_ge(k_psum, piece + 1)
                act.wait_ge(k_stored[f], reuse)
                bias = COLT[:, COL_AT["bk"] + f:COL_AT["bk"] + f + 1]
                nc.scalar.activation(K32[f], psum[:, f, :], ACT.Identity, bias=bias).then_inc(k_copied, 1)
                nc.scalar.activation(KPT[f][:, 0, :], psum[:, f, :], ACT.Identity, bias=bias).then_inc(k_copied, 1)

            def middle_part(piece, f):
                act.wait_ge(k_rest, piece + 1)
                nc.scalar.activation(KPT[f][:, 1, :], K32[f], ACT.Copy).then_inc(k_middle, 1)

            def v_tile(done, kc, bank):
                act.wait_ge(v_psum, done + 1)
                nc.scalar.activation(V[:, bass.ds(kc, 1), :, 0:DH],
                                     psum[:, bank, 0:256].rearrange("p (o h d) -> p o h d", o=1, h=H),
                                     ACT.Copy).then_inc(v_copied, 1)

            act.wait_ge(cols_loaded, 32)
            with act.Fori(0, NCH) as i:
                for f in range(CT):
                    copy_k(2 * i + f, f, 16 * i + 16)
                for v in range(4):
                    v_tile(4 * i + v, 4 * i + v, 2 + v % 2)
            with act.Fori(0, NCH) as i:
                for f in range(CT):
                    copy_k(2 * i + f + 16, f, 16 * i + 16 * (NCH + 1))
                    middle_part(2 * i + f + 16, f)

            def stack_max(gg, pair):
                b, j = gg // GPB, G * (gg % GPB) + 2 * pair
                act.wait_ge(m_turned, 2 * gg + pair + 1)
                nc.scalar.activation(QST[ROWS:KROWS, j:j + 2, b * S:(b + 1) * S],
                                     PX[ROWS:KROWS, :].rearrange("p (j n) -> p j n", j=2),
                                     ACT.Copy).then_inc(m_stacked, 1)

            for pair in range(2):
                stack_max(0, pair)

            for gg in range(NG):
                if gg == GPB:
                    act.wait_ge(v_staged, GPB * KC)
                    with act.Fori(0, KC // 4) as i:
                        for v in range(4):
                            v_tile(4 * i + v + KC, 4 * i + v, v)
                n0 = KC * gg

                def exps(i, first, last=False):
                    for u in range(8):
                        act.wait_ge(st_ready, 8 * i + (n0 + u + 1))
                        if not first or n0 + u >= 2:
                            act.wait_ge(pv_done, 8 * i + (n0 + u - 1))
                        nc.scalar.activation(PR[u % 2], ST(u % 2).rearrange("p b n -> p (b n)"), ACT.Exp)\
                          .then_inc(exp_ready, 1)
                        if last and u in (3, 5) and gg + 1 < NG:
                            stack_max(gg + 1, u // 4)
                exps(0, True)
                with act.Fori(1, KC // 8 - 1) as i:
                    exps(i, False)
                exps(KC // 8 - 1, False, True)
                act.wait_ge(pv_done, n0 + KC)
                if gg:
                    act.wait_ge(pv_turned, gg)
                nc.scalar.activation(PVS, PV, ACT.Copy).then_inc(pv_copied, 1)


            sqrts = [1]

            def root():
                sqrts[0] += 1
                act.wait_ge(ln_var, sqrts[0])
                nc.scalar.activation(SD[:, 0:4], SD[:, 4:8], ACT.Sqrt).then_inc(ln_sd, 1)

            turns = [1]

            def copy_turned(dst, scale=None):
                for c in range(CT):
                    act.wait_ge(ht_psum, CT * turns[0] + c + 1)
                    if scale is None:
                        nc.scalar.activation(dst[:, c, :], psum[:, 6 + c, :], ACT.Copy).then_inc(ht_ready, 1)
                    else:
                        nc.scalar.activation(dst[:, c, :], psum[:, 6 + c, :], ACT.Identity,
                                             scale=col(scale, c)).then_inc(ht_ready, 1)
                turns[0] += 1

            def signal(ins, name):
                ins.then_inc(on[name], 1)

            copy_turned(HTC)
            root()
            root()
            copy_turned(HTC, "norm_w")
            act.wait_ge(on["c_padded"], 2)
            for j in range(8):
                act.wait_ge(on["c_in"], j + 1)
                if j < IT:
                    signal(nc.scalar.activation(VAL[:, j, :, 4:S + 4],
                                                psum[:, j, :].rearrange("p (b n) -> p b n", b=B), ACT.Identity,
                                                bias=col("in_b", IT + j)), "c_in_copied")
                else:
                    signal(nc.scalar.activation(GATE[:, j - IT, :], psum[:, j, :], ACT.Sigmoid,
                                                bias=col("in_b", j - IT)), "c_in_copied")
            act.wait_ge(on["c_a"], 1)
            signal(nc.scalar.activation(ABIAS[0:DS, :], psum[0:DS, 1, 0:1], ACT.Copy), "c_a_copied")
            act.wait_ge(on["c_a_copied"], 1)
            act.wait_ge(on["c_a"], 2)
            signal(nc.scalar.activation(AS, psum[:, 0, :], ACT.Identity, bias=ABIAS), "c_a_copied")
            for m in range(IT):
                act.wait_ge(on["c_ab"], m + 1)
                signal(nc.scalar.activation(AB[:, m, :], psum[:, 1 + m, :], ACT.Copy), "c_ab_copied")
            for m in range(IT):
                act.wait_ge(on["c_conv_b"], IT * (TAPS_B - 1) + m + 1)
                signal(nc.scalar.activation(SB[:, m, :], CB[:, m, :], ACT.Sigmoid), "c_sigmoid")
            for m in range(2):
                act.wait_ge(on["c_ha"], m + 1)
                signal(nc.scalar.activation(YC[:, m, :], psum[:, 5 + m, :], ACT.Identity,
                                            bias=col("ha_b", m)), "c_ha_copied")
            for m in range(IT):
                act.wait_ge(on["c_pw"], m + 1)
                signal(nc.scalar.activation(PWO[:, m, :], psum[:, m, :], ACT.Identity,
                                            bias=col("pw_b", m)), "c_pw_copied")
            for m in range(2):
                act.wait_ge(on["c_hb"], m + 1)
                signal(nc.scalar.activation(YC[:, 2 + m, :], psum[:, 4 + m, :], ACT.Identity,
                                            bias=col("hb_b", m)), "c_hb_copied")
            root()
            root()
            for c in range(CT):
                act.wait_ge(on["d_turned"], c + 1)
                signal(nc.scalar.activation(HQT[:, c, :], psum[:, 6 + c, 0:256].bitcast(BF16), ACT.Copy),
                       "d_turned_copied")
            for n in range(8):
                act.wait_ge(on["d_hidden"], n + 1)
                part = UH[:, n // 2, n % 2 * 512:(n % 2 + 1) * 512]
                signal(nc.scalar.activation(part, part, ACT.Gelu), "d_gelu")
            root()
            for k in range(FT):
                act.wait_ge(on["d_turned2"], k + 1)
                signal(nc.scalar.activation(QHT[:, k, :], psum[:, k, 0:256].bitcast(BF16), ACT.Copy),
                       "d_turned2_copied")
            root()
            copy_turned(HTE)
            for f in range(CT):
                act.wait_ge(on["e_q"], f + 1)
                signal(nc.scalar.activation(QE[:, f, :], psum[:, f, :], ACT.Identity, bias=col("bq1", f)),
                       "e_q_copied")
            for c in range(CT):
                act.wait_ge(on["e_qc"], c + 1)
                signal(nc.scalar.activation(QC[:, c, :], psum[:, 2 + c, :], ACT.Copy, scale=D ** -0.5),
                       "e_qc_copied")
            for w in range(4):
                act.wait_ge(on["e_bias"], w + 1)
                signal(nc.scalar.activation(PE1[w % 2], PE1[w % 2], ACT.Exp, bias=ENB[:, w:w + 1],
                                            accum_out=ESUM[:, w:w + 1]), "e_exp")
                for n in range(0, 8, 2):
                    act.wait_ge(on["e_turned"], 8 * w + n + 1)
                    if w:
                        act.wait_ge(on["e_att"], w)
                    signal(nc.scalar.activation(PT1[:, n * 512:(n + 1) * 512], psum[:, 4, :], ACT.Copy),
                           "e_turned_a")
            copy_turned(HTE)
            root()
            copy_turned(HTF)
            for n in range(16):
                act.wait_ge(on["f_turned"], n + 1)
                dst = QT if n < 8 else KT
                signal(nc.scalar.activation(dst[:, n % 8, :], psum[:, n % 8, :], ACT.Copy), "f_turned_copied")
            for n in range(8):
                act.wait_ge(on["f_qkv"], 16 + n + 1)
                signal(nc.scalar.activation(VTM[:, n // 2, n % 2 * HALF:(n % 2 + 1) * HALF], psum[:, n, :],
                                            ACT.Copy), "f_v_copied")
            def head_exps(n):
                act.wait_ge(on["f_bias"], n + 1)
                if n >= 4:
                    act.wait_ge(on["f_pt"], n - 3)
                src = PM[n % 4] if n % HM < 8 else HEAD_SCORES[n % 4].rearrange("p (t n) -> p t n", t=2)
                for qt in range(2):
                    signal(nc.scalar.activation(PM[n % 4][:, qt, :], src[:, qt, :], ACT.Exp, scale=DM ** -0.5,
                                                bias=FNB[:, 2 * n + qt:2 * n + qt + 1],
                                                accum_out=FSUM[:, 2 * n + qt:2 * n + qt + 1]), "f_exp")

            act.wait_ge(on["f_roped"], 16)
            head_exps(0)
            head_exps(1)
            for n in range(32):
                if n + 2 < 32:
                    head_exps(n + 2)
                act.wait_ge(on["f_pt"], n + 1)
                if n >= 4:
                    act.wait_ge(on["f_pv"], (n - 4) // 2 + 1)
                signal(nc.scalar.activation(PTM[n % 4], psum[:, 2 + n % 2, :].rearrange("p (k n) -> p k n", k=2),
                                            ACT.Copy), "f_pt_copied")
            root()
            copy_turned(HTF)
            act.wait_ge(on["g_logits"], 2)
            signal(nc.scalar.activation(R1[3], R1[2], ACT.Exp), "g_logits")
            for c in range(CT):
                act.wait_ge(on["g_xg"], c + 1)
                signal(nc.scalar.activation(XG[:, c, :], psum[:, 2 + c, :], ACT.Copy), "g_xg_copied")
            for m in range(IT):
                act.wait_ge(on["g_up"], m + 1)
                signal(nc.scalar.activation(INTER[:, m, :], psum[:, 4 + m, :], ACT.Relu), "g_up_copied")
            for k in range(4):
                act.wait_ge(on["g_down"], k + 1)
                signal(nc.scalar.activation(OE[:, k, :], psum[:, k, 0:256], ACT.Copy), "g_down_copied")

        @block.vector
        def _(dve):
            dve.wait_ge(x_loaded, 16)
            for i in range(TT):
                nc.vector.bn_stats(BN[:, 6 * i:6 * i + 6], X[:, i, :]).then_inc(ln_step, 1)
            dve.wait_ge(ln_step, TT)
            for i in range(TT):
                nc.vector.bn_aggr(MV[:, 2 * i:2 * i + 2], BN[:, 6 * i:6 * i + 6]).then_inc(ln_step, 1)
            dve.wait_ge(ln_step, 2 * TT)
            mean = MV.rearrange("p (t two) -> p t two", two=2)
            nc.vector.tensor_scalar(SD[:, 4:8], mean[:, :, 1], 1e-5, None, ALU.add).then_inc(ln_var, 1)
            dve.wait_ge(ln_sd, 1)
            nc.vector.reciprocal(SD[:, 4:8], SD[:, 0:4]).then_inc(ln_step, 1)
            dve.wait_ge(ln_step, 2 * TT + 1)
            for i in range(TT):
                nc.vector.tensor_scalar(HN[:, i, :], X[:, i, :], MV[:, 2 * i:2 * i + 1], SD[:, 4 + i:5 + i],
                                        ALU.subtract, ALU.mult).then_inc(h_ready, 1)
            dve.wait_ge(cols_loaded, 32)
            for f in range(CT):
                n = 4 * f
                dve.wait_ge(q_psum, f + 1)
                nc.vector.tensor_scalar(K32[f], psum[:, f, :], COLT[:, COL_AT["bq"] + f:COL_AT["bq"] + f + 1],
                                        DH ** -0.5, ALU.add, ALU.mult).then_inc(q_split, 1)
                dve.wait_ge(q_split, n + 1)
                nc.vector.tensor_copy(KPT[f][:, 0, :], K32[f]).then_inc(q_split, 1)
                dve.wait_ge(q_split, n + 2)
                nc.vector.tensor_tensor(K32[f], K32[f], KPT[f][:, 0, :], ALU.subtract).then_inc(q_split, 1)
                dve.wait_ge(q_split, n + 3)
                nc.vector.tensor_copy(KPT[f][:, 1, :], K32[f]).then_inc(q_split, 1)
                dve.wait_ge(q_split, n + 4)
                nc.vector.tensor_tensor(KPT[f][:, 2, :], K32[f], KPT[f][:, 1, :], ALU.subtract)\
                  .then_inc(q_ready, 1)

            def split_k(piece, f, middle=True):
                dve.wait_ge(k_copied, 2 * piece + 2)
                nc.vector.tensor_tensor(K32[f], K32[f], KPT[f][:, 0, :], ALU.subtract).then_inc(k_rest, 1)
                if middle:
                    dve.wait_ge(k_rest, piece + 1)
                    nc.vector.tensor_copy(KPT[f][:, 1, :], K32[f]).then_inc(k_middle, 1)

            def maxes(n, col, mx, chunks=range(8)):
                for c in chunks:
                    dve.wait_ge(s_ready, n + (c + 1))
                    nc.vector.tensor_reduce(mx[:, bass.ds(col + c, 1)], SP_(c % 2), AX.X, ALU.max)\
                      .then_inc(s_maxed, 1)

            with dve.Fori(0, NCH // 2) as i:
                for f in range(CT):
                    split_k(2 * i + f, f)
            dve.wait_ge(mask_loaded, 16)
            with dve.Fori(0, NCH // 2) as i:
                for f in range(CT):
                    split_k(2 * i + f + NCH, f)
                    part = MASKB[:, f, bass.ds(i * 2 * CH, 2 * CH)]
                    nc.vector.tensor_scalar(part, MASKI[:, f, bass.ds(i * 2 * CH, 2 * CH)], 0.0, MASKED,
                                            ALU.is_equal, ALU.mult).then_inc(mask_step, 1)
                    dve.wait_ge(mask_step, 4 * i + (2 * f + 1))
                    nc.vector.tensor_reduce(MX[1][:, bass.ds(2 * i + f, 1)], part, AX.X, ALU.min).then_inc(mask_step, 1)
            dve.wait_ge(mask_step, 2 * NCH)
            nc.vector.tensor_reduce(FLAGF[:, 0:1], MX[1][:, 0:NCH], AX.X, ALU.min).then_inc(mask_step, 1)
            dve.wait_ge(mask_step, 2 * NCH + 1)
            nc.vector.tensor_scalar(FLAGF[:, 1:2], FLAGF[:, 0:1], 0.0, None, ALU.is_lt).then_inc(mask_step, 1)
            dve.wait_ge(mask_counted, 1)
            nc.vector.tensor_scalar(FLAG, psum[0:1, 5, 0:1], 0.0, None, ALU.is_gt).then_inc(mask_flagged, 1)
            with dve.Fori(0, NCH) as i:
                maxes(8 * i, 8 * i, MX[0], range(6))
                split_k(2 * i + 16, 0, False)
                maxes(8 * i, 8 * i, MX[0], range(6, 8))
                split_k(2 * i + 17, 1, False)

            def split_max(gg):
                n = 4 * gg

                def between(c):
                    if gg + 1 < NG:
                        maxes(64 * (gg + 1), 0, MX[(gg + 1) % 2], (c,))
                dve.wait_ge(s_maxed, 64 * (gg + 1))
                nc.vector.tensor_reduce(M8, MX[gg % 2].rearrange("p (m c) -> p m c", c=8), AX.X, ALU.max)\
                  .then_inc(m_step, 1)
                between(0)
                if gg:
                    dve.wait_ge(m_turned, 2 * gg)
                dve.wait_ge(m_step, n + 1)
                nc.vector.tensor_scalar(MPART[:, :, 0], M8, -1.0, None, ALU.mult).then_inc(m_step, 1)
                between(1)
                dve.wait_ge(m_step, n + 2)
                nc.vector.scalar_tensor_tensor(out=MR, in0=M8, scalar=-1.0, in1=MPART[:, :, 0],
                                               op0=ALU.mult, op1=ALU.subtract).then_inc(m_step, 1)
                between(2)
                dve.wait_ge(m_step, n + 3)
                nc.vector.tensor_copy(MPART[:, :, 1], MR).then_inc(m_step, 1)
                between(3)
                dve.wait_ge(m_step, n + 4)
                nc.vector.tensor_tensor(MPART[:, :, 2], MR, MPART[:, :, 1], ALU.subtract).then_inc(m_split, 1)
                if gg + 1 < NG:
                    maxes(64 * (gg + 1), 0, MX[(gg + 1) % 2], range(4, 8))
                    maxes(64 * (gg + 1) + 8, 8, MX[(gg + 1) % 2])

            def normalise(gg):
                b, g = gg // GPB, gg % GPB
                n = 3 * gg
                dve.wait_ge(pv_turned, gg + 1)
                turned = PX[:, 0:256].rearrange("p (t j e) -> p t j e", t=2, j=G)
                nc.vector.reciprocal(RINV, turned[:, :, :, DH]).then_inc(norm_step, 1)
                dve.wait_ge(norm_step, n + 1)
                out = CTXN[:, 2 * b:2 * b + 2, G * DH * g:G * DH * (g + 1)].rearrange("p t (j d) -> p t j d", j=G)
                nc.vector.tensor_tensor(out, turned[:, :, :, 0:DH],
                                        RINV.unsqueeze(3).broadcast_to((P, 2, G, DH)), ALU.mult)\
                  .then_inc(norm_step, 1)
                dve.wait_ge(norm_step, n + 2)
                flat = CTXN[:, 2 * b:2 * b + 2, G * DH * g:G * DH * (g + 1)]
                bv = BV[:, G * DH * g:G * DH * (g + 1)].unsqueeze(1).broadcast_to((P, 2, G * DH))
                nc.vector.tensor_tensor(flat, flat, bv, ALU.add).then_inc(norm_step, 1)

            split_max(0)
            for gg in range(NG):
                if gg + 1 < NG:
                    mx = MX[(gg + 1) % 2]
                    n = 64 * (gg + 1) + 16
                    maxes(n, 16, mx)
                    if gg:
                        normalise(gg - 1)
                    maxes(n + 8, 24, mx)
                    with dve.Fori(1, KC // 8 - 1) as i:
                        maxes(16 * i + n, 16 * i + 16, mx)
                        maxes(16 * i + (n + 8), 16 * i + 24, mx)
                    split_max(gg + 1)
                else:
                    normalise(gg - 1)
            normalise(NG - 1)


            steps = [0]

            def mark(ins):
                ins.then_inc(on["step_v"], 1)
                steps[0] += 1

            def done():
                dve.wait_ge(on["step_v"], steps[0])

            roots = [1]

            def root():
                roots[0] += 1
                dve.wait_ge(ln_sd, roots[0])
                mark(nc.vector.reciprocal(SD[:, 4:8], SD[:, 0:4]))
                done()

            def statistics(src, n, width):
                for i in range(TT):
                    for j in range(n):
                        mark(nc.vector.bn_stats(BN[:, 6 * (n * i + j):6 * (n * i + j + 1)],
                                                src[:, i, j * width:(j + 1) * width]))
                done()
                for i in range(TT):
                    mark(nc.vector.bn_aggr(MV[:, 2 * i:2 * i + 2], BN[:, 6 * n * i:6 * n * (i + 1)]))
                done()
                nc.vector.tensor_scalar(SD[:, 4:8], mean[:, :, 1], 1e-5, None, ALU.add).then_inc(ln_var, 1)
                root()

            def centred(dst, src, i):
                return nc.vector.tensor_scalar(dst[:, i, :], src[:, i, :], MV[:, 2 * i:2 * i + 1],
                                               SD[:, 4 + i:5 + i], ALU.subtract, ALU.mult)

            def x_ready(ins):
                ins.then_inc(on["x_ready"], 1)

            dve.wait_ge(on["raw_loaded"], 32)
            for n, w in enumerate((W1RAW, W2RAW)):
                nc.vector.tensor_reduce(WSUM[:, n:n + 1], w, AX.X, ALU.add, apply_absolute_value=True)\
                  .then_inc(on["w_summed"], 1)
            dve.wait_ge(on["b_out"], 1)
            for i in range(TT):
                dve.wait_ge(on["b_out"], i + 1)
                x_ready(nc.vector.tensor_tensor(X[:, i, :], X[:, i, :], psum[:, i, 0:256], ALU.add))
            dve.wait_ge(on["x_ready"], TT)
            statistics(X, 1, D)
            for i in range(TT):
                mark(centred(HL, X, i))
            done()
            for i in range(TT):
                mark(nc.vector.tensor_tensor_reduce(HS[:, i, :], HL[:, i, :], HL[:, i, :], 1.0, 0.0,
                                                    ALU.mult, ALU.add, MS[:, i:i + 1]))
            done()
            nc.vector.tensor_scalar(SD[:, 4:8], MS, 1.0 / D, 1e-6, ALU.mult, ALU.add).then_inc(ln_var, 1)
            root()
            for i in range(TT):
                nc.vector.tensor_scalar(HS[:, i, :], HL[:, i, :], SD[:, 4 + i:5 + i], None, ALU.mult)\
                  .then_inc(h_ready, 1)
            for i in range(TT):
                mark(nc.vector.tensor_tensor(X[:, i, :], X[:, i, :], HL[:, i, :], ALU.add))
            dve.wait_ge(on["w_total"], 1)
            mark(nc.vector.tensor_scalar(WMEAN, psum[:, 4, 0:2], 1.0 / (D * FF), 1e-5, ALU.mult, ALU.max))
            done()
            mark(nc.vector.reciprocal(WSC, WMEAN))
            done()
            for n, (w, tw) in enumerate(((W1RAW, TW1), (W2RAW, TW2))):
                flat = tw.rearrange("p a b -> p (a b)")
                signal = on["w_quantised"]
                nc.vector.tensor_scalar(w, w, WSC[:, n:n + 1], ROUND, ALU.mult, ALU.add).then_inc(signal, 1)
                dve.wait_ge(signal, 3 * n + 1)
                nc.vector.tensor_scalar(w, w, ROUND, 1.0, ALU.subtract, ALU.min).then_inc(signal, 1)
                dve.wait_ge(signal, 3 * n + 2)
                nc.vector.tensor_scalar(flat, w, -1.0, None, ALU.max).then_inc(signal, 1)
            for k in range(TAPS_B):
                for m in range(IT):
                    tap = col("sym_k", TAPS_B * m + k)
                    src = VAL[:, m, :, 4 + k - LEFT_B:4 + k - LEFT_B + S]
                    out = CB[:, m, :].rearrange("p (b n) -> p b n", b=B)
                    if k == 0:
                        dve.wait_ge(on["c_in_copied"], m + 1)
                        nc.vector.tensor_scalar(out, src, tap, col("sym_b", m), ALU.mult, ALU.add)\
                          .then_inc(on["c_conv_b"], 1)
                    else:
                        dve.wait_ge(on["c_conv_b"], IT * (k - 1) + m + 1)
                        nc.vector.scalar_tensor_tensor(out=out, in0=src, scalar=tap, in1=out,
                                                       op0=ALU.mult, op1=ALU.add)\
                          .then_inc(on["c_conv_b"], 1)
            for m in range(IT):
                dve.wait_ge(on["c_sigmoid"], m + 1)
                nc.vector.tensor_tensor(SB[:, m, :], SB[:, m, :], CB[:, m, :], ALU.mult).then_inc(on["c_silu"], 1)
            for m in range(IT):
                dve.wait_ge(on["c_fuse"], m + 1)
                nc.vector.scalar_tensor_tensor(out=YG[:, m, :], in0=psum[:, m, :], scalar=col("fuse_b", m),
                                               in1=GATE[:, m, :], op0=ALU.add, op1=ALU.mult)\
                  .then_inc(on["c_gated"], 1)
            for i in range(TT):
                dve.wait_ge(on["c_out"], i + 1)
                x_ready(nc.vector.tensor_tensor(X[:, i, :], X[:, i, :], psum[:, 4 + i, 0:256], ALU.add))
            dve.wait_ge(on["x_ready"], 2 * TT)

            def quantise(src, dst, ready, per_row):
                mark(nc.vector.tensor_reduce(AMAX, src, AX.X, ALU.max, apply_absolute_value=True))
                done()
                mark(nc.vector.tensor_scalar(AMAX, AMAX, 1e-5, None, ALU.max))
                done()
                mark(nc.vector.reciprocal(QSC, AMAX))
                done()
                mark(nc.vector.tensor_scalar(QSC, QSC, 127.0, None, ALU.mult))
                mark(nc.vector.tensor_scalar(OSC, AMAX, per_row, 1.0 / 127.0, ALU.mult, ALU.mult))
                done()
                for i in range(TT):
                    mark(nc.vector.tensor_scalar(src[:, i, :], src[:, i, :], QSC[:, i:i + 1], ROUND,
                                                 ALU.mult, ALU.add))
                    done()
                    mark(nc.vector.tensor_scalar(dst[:, i, :], src[:, i, :], ROUND, 127.0, ALU.subtract, ALU.min))
                    done()
                    nc.vector.tensor_scalar(dst[:, i, :], dst[:, i, :], -128.0, None, ALU.max)\
                      .then_inc(on[ready], 1)

            def scaled(src, i, g, b):
                mark(nc.vector.tensor_tensor(src[:, i, :], src[:, i, :], row(g), ALU.mult))
                done()
                mark(nc.vector.tensor_tensor(src[:, i, :], src[:, i, :], row(b), ALU.add))

            statistics(X, 1, D)
            for i in range(TT):
                mark(centred(HL, X, i))
            done()
            statistics(HL, 1, D)
            dve.wait_ge(on["rows_loaded"], 16)
            for i in range(TT):
                mark(centred(HL, HL, i))
                done()
                scaled(HL, i, "g1", "b1")
            done()
            quantise(HL, HQ, "d_quant", WMEAN[:, 0:1])
            for n in range(8):
                i, half = n // 2, n % 2
                dve.wait_ge(on["d_up"], n + 1)
                nc.vector.scalar_tensor_tensor(out=UH[:, i, half * 512:(half + 1) * 512], in0=psum[:, n, :],
                                               scalar=OSC[:, i:i + 1], in1=row("w1b")[:, half * 512:(half + 1) * 512],
                                               op0=ALU.mult, op1=ALU.add).then_inc(on["d_hidden"], 1)
            dve.wait_ge(on["d_gelu"], 8)
            statistics(UH, 2, 512)
            for i in range(TT):
                mark(centred(UH, UH, i))
                done()
                scaled(UH, i, "g2", "b2")
            done()
            quantise(UH, QH, "d_quant2", WMEAN[:, 1:2])
            for i in range(TT):
                mark(nc.vector.tensor_tensor(X[:, i, :], X[:, i, :], row("w2b"), ALU.add))
            done()
            for i in range(TT):
                dve.wait_ge(on["d_down"], i + 1)
                x_ready(nc.vector.scalar_tensor_tensor(out=X[:, i, :], in0=psum[:, i, 0:256], scalar=OSC[:, i:i + 1],
                                                       in1=X[:, i, :], op0=ALU.mult, op1=ALU.add))
            dve.wait_ge(on["x_ready"], 3 * TT)

            statistics(X, 1, D)
            for i in range(TT):
                centred(HLE, X, i).then_inc(h_ready, 1)
            dve.wait_ge(on["e_cq"], 1)
            nc.vector.tensor_scalar(CQ, psum[:, 4, 0:4], D ** -0.5, None, ALU.mult).then_inc(on["e_cq_copied"], 1)
            dve.wait_ge(on["e_cq_copied"], 1)

            def mask_scores(w):
                for n in range(8):
                    half = n // 4
                    if n % 4 == 0:
                        dve.wait_ge(on[f"mask1_loaded{half}"], 16 * (w + 1))
                    dve.wait_ge(on["e_scores"], 8 * w + n + 1)
                    if w >= 2:
                        dve.wait_ge(on["e_turned"], 8 * (w - 1))
                    nc.vector.tensor_tensor_reduce(PE1[w % 2][:, n * 512:(n + 1) * 512], psum[:, n % 4, :],
                                                   MRING[half][:, n % 4 * 512:(n % 4 + 1) * 512], 1.0, -3.0e38,
                                                   ALU.add, ALU.max, EMX[:, 8 * w + n:8 * w + n + 1])\
                      .then_inc(on["e_masked"], 1)
                dve.wait_ge(on["e_masked"], 8 * (w + 1))
                one = slice(w, w + 1)
                mark(nc.vector.tensor_reduce(EM[:, one], EMX[:, 8 * w:8 * w + 8], AX.X, ALU.max))
                done()
                mark(nc.vector.tensor_tensor(ET[:, one], EM[:, one], CQ[:, one], ALU.add))
                done()
                nc.vector.tensor_tensor(ENB[:, one], CQ[:, one], ET[:, one], ALU.subtract).then_inc(on["e_bias"], 1)

            def copy_exps(w):
                for n in range(1, 8, 2):
                    dve.wait_ge(on["e_turned"], 8 * w + n + 1)
                    if w:
                        dve.wait_ge(on["e_att"], w)
                    nc.vector.tensor_copy(PT1[:, n * 512:(n + 1) * 512], psum[:, 5, :]).then_inc(on["e_turned_v"], 1)

            def norm_att(w):
                dve.wait_ge(on["e_exp"], w + 1)
                mark(nc.vector.reciprocal(ERI[:, w:w + 1], ESUM[:, w:w + 1]))
                done()
                dve.wait_ge(on["e_att"], w + 1)
                nc.vector.tensor_scalar(AO[:, w, :], psum[:, 6, 0:256], ERI[:, w:w + 1], None, ALU.mult)\
                  .then_inc(on["e_normed"], 1)

            mask_scores(0)
            for w in range(4):
                if w < 3:
                    mask_scores(w + 1)
                copy_exps(w)
                norm_att(w)
            for i in range(TT):
                dve.wait_ge(on["e_out"], i + 1)
                x_ready(nc.vector.tensor_tensor(X[:, i, :], X[:, i, :], psum[:, i, 0:256], ALU.add))
            dve.wait_ge(on["x_ready"], 4 * TT)

            statistics(X, 1, D)
            for i in range(TT):
                centred(HLE, X, i).then_inc(h_ready, 1)
            dve.wait_ge(on["const_loaded"], 16)
            cos = const("cos").rearrange("p (t d) -> p t d", t=2)
            sin = const("sin").rearrange("p (t d) -> p t d", t=2)
            for piece in range(16):
                which, i, half = piece // 8, piece % 8 // 2, piece % 2
                dve.wait_ge(on["f_qkv"], piece + 1)
                if which:
                    dve.wait_ge(on["f_turned"], 8)
                if piece >= 2:
                    dve.wait_ge(on["f_roped"], piece - 1)
                src = psum[:, piece % 8, :].rearrange("p (h d) -> p h d", h=8)
                out = QTM[:, i, half * HALF:(half + 1) * HALF].rearrange("p (h d) -> p h d", h=8)
                c = cos[:, i % 2, :].unsqueeze(1).broadcast_to((P, 8, DM))
                lo = sin[:, i % 2, 0:DM // 2].unsqueeze(1).broadcast_to((P, 8, DM // 2))
                hi = sin[:, i % 2, DM // 2:DM].unsqueeze(1).broadcast_to((P, 8, DM // 2))
                part = on["f_rope_part"]
                nc.vector.tensor_tensor(T2[piece % 2][:, :, 0:DM // 2], src[:, :, DM // 2:DM], lo, ALU.mult)\
                  .then_inc(part, 1)
                nc.vector.tensor_tensor(T2[piece % 2][:, :, DM // 2:DM], src[:, :, 0:DM // 2], hi, ALU.mult)\
                  .then_inc(part, 1)
                nc.vector.tensor_tensor(out, src, c, ALU.mult).then_inc(part, 1)
            causal = const("causal").rearrange("p (t n) -> p t n", t=2)

            def row_maxima(n):
                dve.wait_ge(on["f_scores"], n + 1)
                src = HEAD_SCORES[n % 4].rearrange("p (t n) -> p t n", t=2)
                if n % HM < 8:
                    if n >= 4:
                        dve.wait_ge(on["f_pt"], n - 3)
                    for qt in range(2):
                        mark(nc.vector.tensor_tensor_reduce(PM[n % 4][:, qt, :], src[:, qt, :], causal[:, qt, :],
                                                            1.0, -3.0e38, ALU.add, ALU.max,
                                                            FMX[:, 2 * n + qt:2 * n + qt + 1]))
                else:
                    mark(nc.vector.tensor_reduce(FMX[:, 2 * n:2 * n + 2], src, AX.X, ALU.max))
                done()
                nc.vector.tensor_scalar(FNB[:, 2 * n:2 * n + 2], FMX[:, 2 * n:2 * n + 2], -(DM ** -0.5), None,
                                        ALU.mult).then_inc(on["f_bias"], 1)

            def scale_exps(n):
                dve.wait_ge(on["f_exp"], 2 * (n + 1))
                mark(nc.vector.reciprocal(FRI[:, 2 * n:2 * n + 2], FSUM[:, 2 * n:2 * n + 2]))
                done()
                for qt in range(2):
                    nc.vector.tensor_scalar(PM[n % 4][:, qt, :], PM[n % 4][:, qt, :],
                                            FRI[:, 2 * n + qt:2 * n + qt + 1], None, ALU.mult)\
                      .then_inc(on["f_scaled"], 1)

            def copy_contexts(pair):
                b, k = pair // 8, pair % 8
                dve.wait_ge(on["f_pv"], pair + 1)
                nc.vector.tensor_copy(OT[:, k, b * S:(b + 1) * S], psum[:, 4 + pair % 2, 0:S])\
                  .then_inc(on["f_pv_copied"], 1)

            for n in range(3):
                row_maxima(n)
            for n in range(32):
                scale_exps(n)
                if n + 3 < 32:
                    row_maxima(n + 3)
                if n % 2 and n > 2:
                    copy_contexts((n - 3) // 2)
            copy_contexts(15)
            for i in range(TT):
                dve.wait_ge(on["f_out"], i + 1)
                x_ready(nc.vector.tensor_tensor(X[:, i, :], X[:, i, :], psum[:, i, 0:256], ALU.add))
            dve.wait_ge(on["x_ready"], 5 * TT)

            statistics(X, 1, D)
            for i in range(TT):
                centred(HLE, X, i).then_inc(h_ready, 1)
            dve.wait_ge(on["g_logits"], 1)
            logits, hot1, hot2, weights, chosen, slot, pick = R[0], R[1], R[2], R[3], R[4], R[5], R[6]
            best1, best2, gap, egap, den, share1, share2 = R1[0], R1[1], R1[2], R1[3], R1[4], R1[5], R1[6]
            less8 = const("experts").unsqueeze(1).broadcast_to((P, TT, E))

            def over_e(ap):
                return ap.unsqueeze(2).broadcast_to((P, TT, E))

            mark(nc.vector.tensor_copy(logits, psum[:, 0, 0:TT * E].rearrange("p (t e) -> p t e", t=TT)))
            done()
            for best, hot in ((best1, hot1), (best2, hot2)):
                mark(nc.vector.tensor_reduce(best, logits, AX.X, ALU.max))
                done()
                mark(nc.vector.tensor_tensor(pick, logits, over_e(best), ALU.is_equal))
                done()
                mark(nc.vector.tensor_tensor(pick, pick, less8, ALU.mult))
                done()
                mark(nc.vector.tensor_reduce(R1[7], pick, AX.X, ALU.min))
                done()
                mark(nc.vector.tensor_tensor(hot, less8, over_e(R1[7]), ALU.is_equal))
                done()
                if best is best1:
                    mark(nc.vector.scalar_tensor_tensor(out=logits, in0=hot, scalar=-3.0e38, in1=logits,
                                                        op0=ALU.mult, op1=ALU.add))
                    done()
            nc.vector.tensor_tensor(gap, best2, best1, ALU.subtract).then_inc(on["g_logits"], 1)
            dve.wait_ge(on["g_logits"], 3)
            mark(nc.vector.tensor_scalar(den, egap, 1.0, None, ALU.add))
            done()
            mark(nc.vector.reciprocal(share1, den))
            done()
            mark(nc.vector.tensor_tensor(share2, egap, share1, ALU.mult))
            done()
            mark(nc.vector.tensor_tensor(hot1, hot1, over_e(share1), ALU.mult))
            mark(nc.vector.tensor_tensor(hot2, hot2, over_e(share2), ALU.mult))
            done()
            mark(nc.vector.tensor_tensor(weights, hot1, hot2, ALU.add))
            done()
            nc.vector.tensor_scalar(chosen, weights, 0.0, None, ALU.is_gt).then_inc(on["g_chosen"], 1)
            dve.wait_ge(on["g_cum"], 1)
            cum = psum[:, 1, 0:TT * E].rearrange("p (t e) -> p t e", t=TT)
            mark(nc.vector.scalar_tensor_tensor(out=slot, in0=cum, scalar=float(CAP), in1=chosen,
                                                op0=ALU.is_le, op1=ALU.mult))
            done()
            mark(nc.vector.tensor_tensor(slot, slot, cum, ALU.mult))
            done()
            for i in range(TT):
                nc.vector.tensor_tensor(SEL[:, i], slot[:, i, :].unsqueeze(2).broadcast_to((P, E, CAP)),
                                        const("slots").unsqueeze(1).broadcast_to((P, E, CAP)), ALU.is_equal)\
                  .then_inc(on["g_sel"], 1)
            for i in range(TT):
                dve.wait_ge(on["g_sel"], i + 1)
                nc.vector.tensor_tensor(SELW[:, i], SEL[:, i],
                                        weights[:, i, :].unsqueeze(2).broadcast_to((P, E, CAP)), ALU.mult)\
                  .then_inc(on["g_selw"], 1)
            for k in range(4):
                dve.wait_ge(on["g_selt"], k + 1)
                nc.vector.tensor_copy(SELT[:, k, :], psum[:, [0, 1, 0, 1][k], :]).then_inc(on["g_selt_copied"], 1)
            for i in range(TT):
                dve.wait_ge(on["g_out"], i + 1)
                x_ready(nc.vector.tensor_tensor(X[:, i, :], X[:, i, :], psum[:, 4 + i, 0:256], ALU.add))

        @block.tensor
        def _(pe):
            pe.wait_ge(ident_built, 4)
            for c in range(CT):
                for i in range(TT):
                    pe.wait_ge(h_ready, i + 1)
                    last = nc.tensor.transpose(psum[:, 6 + c, i * P:(i + 1) * P], HN[:, i, c * P:(c + 1) * P],
                                               IDENT)
                last.then_inc(ht_psum, 1)
            pe.wait_ge(wq_loaded, 16)
            pe.wait_ge(ht_ready, CT)
            for f in range(CT):
                for c in range(CT):
                    last = nc.tensor.matmul(psum[:, f, :], WQ[:, c, f * P:(f + 1) * P], HT[:, c, :],
                                            start=(c == 0), stop=(c == CT - 1))
                last.then_inc(q_psum, 1)
            pe.wait_ge(wkv_loaded, 32)
            pe.wait_ge(q_ready, CT)

            def project_k(piece, f, slot, first=False, cs=range(CT)):
                if not first and 0 in cs:
                    pe.wait_ge(k_copied, 2 * piece - 2)
                for c in cs:
                    last = nc.tensor.matmul(psum[:, f, :], WK[:, c, f * P:(f + 1) * P], CTX[slot][:, c, :],
                                            start=(c == 0), stop=(c == CT - 1), skip_group_check=True)
                if CT - 1 in cs:
                    last.then_inc(k_psum, 1)

            def project_v(tile, v, bank, slot, banks, first=False):
                if not first:
                    pe.wait_ge(v_copied, tile + (1 - banks))
                for c in range(CT):
                    last = nc.tensor.matmul(psum[:, bank, 0:256], CTX[slot][:, c, v * P:(v + 1) * P],
                                            WV[:, c, :], start=(c == 0), stop=(c == CT - 1))
                last.then_inc(v_psum, 1)

            def scores(n, masked, slot, qh, jh, qt, c, b, first=False):
                if not first:
                    pe.wait_ge(s_maxed, n - 1)
                q = QST[0:ROWS, bass.ds(qh, 1), b * S + qt * P:b * S + (qt + 1) * P]
                k = KST[slot][0:ROWS, bass.ds(jh, 1), c * CH:(c + 1) * CH]
                last = nc.tensor.matmul(SP_(c % 2), q, k, start=True, stop=not masked, skip_group_check=True)
                if masked:
                    last = nc.tensor.matmul(SP_(c % 2), IDENTB, MASKB[:, qt, c * CH:(c + 1) * CH],
                                            start=False, stop=True, skip_group_check=True)
                last.then_inc(s_ready, 1)

            def turn_max(gg, pair):
                if pair == 0:
                    pe.wait_ge(m_split, gg + 1)
                    if gg > 1:
                        pe.wait_ge(norm_step, 3 * (gg - 1))
                else:
                    pe.wait_ge(m_stacked, 2 * gg + 1)
                for m in range(4):
                    last = nc.tensor.matmul(PX[ROWS:KROWS, m * P:(m + 1) * P], MPART[:, 4 * pair + m, :], IDENTB,
                                            start=True, stop=True)
                last.then_inc(m_turned, 1)

            def turned_scores(masked, slot, g, b, kc, u):
                for j in range(G):
                    last = nc.tensor.matmul(ST(u % 2)[:, j // 2, (j % 2) * S:(j % 2 + 1) * S],
                                            KST[slot][0:KROWS, j, bass.ds(kc * P, P)],
                                            QST[0:KROWS, G * g + j, b * S:(b + 1) * S],
                                            start=(j % 2 == 0), stop=not masked and j % 2 == 1,
                                            skip_group_check=True)
                if masked:
                    for bank in range(2):
                        for qt in range(2):
                            out = ST(u % 2)[:, bank, :].rearrange("p (j n) -> p j n", j=2)
                            last = nc.tensor.matmul(out[:, :, qt * P:(qt + 1) * P],
                                                    MASKB[:, qt, bass.ds(kc * P, P)],
                                                    IDENTB.unsqueeze(1).broadcast_to((P, 2, P)),
                                                    start=False, stop=qt == 1, skip_group_check=True)
                last.then_inc(st_ready, 1)

            def weigh_values(n, u, start, stop):
                pe.wait_ge(v_staged, n + 1)
                for j in range(G):
                    last = nc.tensor.matmul(PV[32 * j:32 * (j + 1), :],
                                            VS[u % 4][:, j * VW:j * VW + 32],
                                            PR[u % 2][:, j * S:(j + 1) * S], start=start, stop=stop,
                                            skip_group_check=True)
                last.then_inc(pv_done, 1)

            def first_batch():
                def chunk(i, u, first):
                    pe.wait_ge(ctx_loaded[u], 16 * i + 16)
                    for f in range(CT):
                        project_k(4 * i + (2 * u + f), f, u, first and u == 0)
                    for v in range(4):
                        project_v(8 * i + (4 * u + v), v, 2 + v % 2, u, 2, first and 4 * u + v < 2)
                for u in range(2):
                    chunk(0, u, True)
                with pe.Fori(1, NCH // 2) as i:
                    for u in range(2):
                        chunk(i, u, False)

            def second_batch(masked):
                pe.wait_ge(q_stacked, 96)
                def chunk(i, u, first):
                    pe.wait_ge(ctx_loaded[u], 16 * i + 16 * (NCH // 2 + 1))
                    for f in range(CT):
                        for c in range(CT):
                            project_k(4 * i + (2 * u + f + 16), f, u, cs=(c,))
                            if first and u == 0 and f == 0 and c == 0:
                                pe.wait_ge(k_stacked[0], STACK0)
                            for s in (4 * f + 2 * c, 4 * f + 2 * c + 1):
                                scores(16 * i + (8 * u + s), masked, 0, i, i, u, s, 0, first and u == 0 and s < 2)
                for u in range(2):
                    chunk(0, u, True)
                with pe.Fori(1, NCH // 2) as i:
                    for u in range(2):
                        chunk(i, u, False)

            def attend(masked):
                second_batch(masked)
                pe.wait_ge(k_stacked[1], 96)
                for c in range(16):
                    scores(64 + c, masked, 1, G, 0, c // 8, c % 8, 0)
                    if c in (5, 9):
                        turn_max(0, c // 9)
                pe.wait_ge(m_stacked, 2)
                pe.wait_ge(kones_built, 3)
                for gg in range(NG):
                    b, g, slot = gg // GPB, gg % GPB, gg % 3
                    n0 = KC * gg
                    if gg == GPB:
                        def chunk(i, u):
                            pe.wait_ge(ctx_loaded[u], 16 * i + 16 * (NCH + 1))
                            for v in range(4):
                                project_v(8 * i + (4 * u + v + KC), v, v, u, 4)
                        pe.wait_ge(exp_ready, KC * gg)
                        pe.wait_ge(v_copied, KC)
                        with pe.Fori(0, NCH // 2) as i:
                            for u in range(2):
                                chunk(i, u)
                        pe.wait_ge(v_copied, 2 * KC)
                    pe.wait_ge(m_stacked, 2 * gg + 2)
                    if gg == 2:
                        pe.wait_ge(kones_built, 11)

                    def ahead(i, last, s):
                        ng, j = (gg + 2, 0) if last else (gg + 1, i + 1)
                        if ng < NG:
                            scores(16 * i + (64 * (gg + 1) + 16 + s), masked, ng % 3, j + G * (ng % GPB), j,
                                   s // 8, s % 8, ng // GPB)

                    def steps(i, first, last=False):
                        if last and gg + 2 < NG:
                            times = 96 * ((gg + 2) // 3 + 1)
                            pe.wait_ge(k_stacked[(gg + 2) % 3], times if (gg + 2) % 3 else times - 96 + STACK0)
                        for u in range(8):
                            if n0 + u >= 2 or not first:
                                pe.wait_ge(exp_ready, 8 * i + (n0 + u - 1))
                            turned_scores(masked, slot, g, b, 8 * i + u, u)
                            ahead(i, last, 2 * u)
                            if first and u == 2 and gg:
                                pe.wait_ge(pv_copied, gg)
                                pe.wait_ge(m_stacked, 2 * gg + 2)
                                turn_context(gg - 1)
                            if last and u in (2, 5) and gg + 1 < NG:
                                turn_max(gg + 1, u // 4)
                            if u == 0 and first:
                                ahead(i, last, 2 * u + 1)
                                continue
                            if u == 1 and first and gg:
                                pe.wait_ge(pv_copied, gg)
                            pe.wait_ge(exp_ready, 8 * i + (n0 + u))
                            weigh_values(8 * i + (n0 + u - 1), (u - 1) % 8, first and u == 1, False)
                            ahead(i, last, 2 * u + 1)

                    steps(0, True)
                    with pe.Fori(1, KC // 8 - 1) as i:
                        steps(i, False)
                    steps(KC // 8 - 1, False, True)
                    pe.wait_ge(exp_ready, n0 + KC)
                    weigh_values(n0 + KC - 1, KC - 1, False, True)

            def turn_context(gg):
                for qt in range(2):
                    last = nc.tensor.transpose(PX[:, qt * P:(qt + 1) * P], PVS[:, qt * P:(qt + 1) * P], IDENT)
                last.then_inc(pv_turned, 1)

            first_batch()
            pe.wait_ge(mask_step, 2 * NCH + 2)
            pe.wait_ge(ones_built, 3)
            nc.tensor.matmul(psum[0:1, 5, 0:1], FLAGF[:, 1:2], ONES[:, 0:1], start=True, stop=True)\
              .then_inc(mask_counted, 1)
            pe.wait_ge(mask_flagged, 1)
            any_masked = pe.value_load(FLAG, min_val=0, max_val=1)
            with pe.If(any_masked == 1):
                attend(True)
            with pe.Else():
                attend(False)
            pe.wait_ge(pv_copied, NG)
            pe.wait_ge(norm_step, 3 * (NG - 1))
            turn_context(NG - 1)

            turns = [1]

            def turn(src, need, sem_=None):
                pe.wait_ge(ht_ready, CT * turns[0])
                for c in range(CT):
                    for i in range(TT):
                        if c == 0 and sem_ is not None:
                            pe.wait_ge(sem_, need + i + 1)
                        last = nc.tensor.transpose(psum[:, 6 + c, i * P:(i + 1) * P],
                                                   src[:, i, c * P:(c + 1) * P], IDENT)
                    last.then_inc(ht_psum, 1)
                turns[0] += 1

            def turned():
                pe.wait_ge(ht_ready, CT * turns[0])

            def linear(out, weights, xs, m, name, width=P):
                n = len(xs)
                for k in range(n):
                    last = nc.tensor.matmul(out, weights[:, k, m * P:m * P + width], xs[k],
                                            start=(k == 0), stop=(k == n - 1))
                last.then_inc(on[name], 1)

            def linear_rows(out, lhs, weights, bias, name):
                n = len(lhs)
                if bias is not None:
                    nc.tensor.matmul(out, ONES[0:1, :], bias, start=True, stop=False)
                for k in range(n):
                    last = nc.tensor.matmul(out, lhs[k], weights[:, k, :], start=(k == 0 and bias is None),
                                            stop=(k == n - 1))
                last.then_inc(on[name], 1)

            def tok(ap, i):
                return [ap[:, k, i * P:(i + 1) * P] for k in range(ap.shape[1])]

            pe.wait_ge(norm_step, 3 * NG)
            turn(CTXN, 0)
            turned()
            pe.wait_ge(on["wo_loaded"], 32)
            pe.wait_ge(on["rows_loaded"], 16)
            pe.wait_ge(exp_ready, NG * KC)
            for i in range(TT):
                linear_rows(psum[:, i, 0:256], tok(HTC, i), WO, row("bo")[0:1, :], "b_out")
            pe.wait_ge(on["w_summed"], 2)
            nc.tensor.matmul(psum[:, 4, 0:2], ONES, WSUM, start=True, stop=True).then_inc(on["w_total"], 1)
            turn(HS, TT, h_ready)
            turned()
            pe.wait_ge(on["mix_loaded"], 80)
            pe.wait_ge(on["x_ready"], TT)
            for j in range(8):
                if j == 4:
                    pe.wait_ge(on["w_quantised"], 1)
                linear(psum[:, j, :], WIN, [HTC[:, c, :] for c in range(CT)], (j + IT) % 8, "c_in")
            pe.wait_ge(on["c_a_weights"], 2 + IT * TAPS_A)
            pe.wait_ge(on["c_in_copied"], IT)
            for m in range(IT):
                last = nc.tensor.matmul(psum[0:DS, 1, 0:1], AW[:, m, :], col("dwa_b", m), start=(m == 0),
                                        stop=(m == IT - 1))
            last.then_inc(on["c_a"], 1)
            for m in range(IT):
                for k in range(TAPS_A):
                    src = VAL[:, m, :, 4 + k - LEFT_A:4 + k - LEFT_A + S]
                    last = nc.tensor.matmul(psum[32 * k:32 * k + 32, 0, :].rearrange("p (b n) -> p b n", b=B),
                                            AWK[:, m, k, :], src, start=(m == 0), stop=(m == IT - 1),
                                            tile_position=(0, 32 * k))
            last.then_inc(on["c_a"], 1)
            pe.wait_ge(on["c_a_copied"], 2)
            pe.wait_ge(on["bm_loaded"], 16 * P // DS)
            for m in range(IT):
                pe.wait_ge(on["c_in_copied"], m + 2)
                nc.tensor.matmul(psum[:, 1 + m, :], BM[:, m * P:(m + 1) * P], AS, start=True, stop=True)\
                  .then_inc(on["c_ab"], 1)
            pe.wait_ge(on["c_ab_copied"], IT)
            for m in range(2):
                pe.wait_ge(on["c_in_copied"], 6 + m)
                linear(psum[:, 5 + m, :], WHA, [AB[:, k, :] for k in range(IT)], m, "c_ha")
            pe.wait_ge(on["c_silu"], IT)
            for m in range(IT):
                linear(psum[:, m, :], WPW, [SB[:, k, :] for k in range(IT)], m, "c_pw")
            pe.wait_ge(on["c_pw_copied"], IT)
            pe.wait_ge(on["c_ha_copied"], 1)
            for m in range(2):
                linear(psum[:, 4 + m, :], WHB, [PWO[:, k, :] for k in range(IT)], m, "c_hb")
            pe.wait_ge(on["c_ha_copied"], 2)
            pe.wait_ge(on["c_hb_copied"], 2)
            for m in range(IT):
                linear(psum[:, m, :], WFU, [YC[:, k, :] for k in range(IT)], m, "c_fuse")
            pe.wait_ge(on["c_in_copied"], 8)
            pe.wait_ge(on["c_gated"], IT)
            for i in range(TT):
                linear_rows(psum[:, 4 + i, 0:256], tok(YG, i), WOUT, row("out_b")[0:1, :], "c_out")

            pe.wait_ge(on["x_ready"], 2 * TT)
            for c in range(CT):
                for i in range(TT):
                    if c == 0:
                        pe.wait_ge(on["d_quant"], i + 1)
                    last = nc.tensor.transpose(psum[:, 6 + c, i * 64:(i + 1) * 64].bitcast(BF16),
                                               HQ[:, i, c * P:(c + 1) * P], IDENTB)
                last.then_inc(on["d_turned"], 1)
            pe.wait_ge(on["d_turned_copied"], CT)
            pe.wait_ge(on["w_quantised"], 6)
            for n in range(8):
                i, half = n // 2, n % 2
                for c in range(CT):
                    last = nc.tensor.matmul(psum[:, n, :], HQT[:, c, i * P:(i + 1) * P],
                                            TW1[:, c, half * 512:(half + 1) * 512], start=(c == 0), stop=(c == 1))
                last.then_inc(on["d_up"], 1)
            pe.wait_ge(on["d_hidden"], 8)
            pe.wait_ge(on["d_quant2"], TT)
            for k in range(FT):
                for i in range(TT):
                    last = nc.tensor.transpose(psum[:, k, i * 64:(i + 1) * 64].bitcast(BF16),
                                               QH[:, i, k * P:(k + 1) * P], IDENTB)
                last.then_inc(on["d_turned2"], 1)
            pe.wait_ge(on["d_turned2_copied"], FT)
            for i in range(TT):
                linear_rows(psum[:, i, 0:256], tok(QHT, i), TW2, None, "d_down")

            turn(HLE, 2 * TT, h_ready)
            turned()
            pe.wait_ge(on["l1w_loaded"], 48)
            pe.wait_ge(on["x_ready"], 3 * TT)
            hs = [HTE[:, c, :] for c in range(CT)]
            for f in range(CT):
                linear(psum[:, f, :], WQ1, hs, f, "e_q")
            pe.wait_ge(on["e_q_copied"], CT)
            for c in range(CT):
                linear(psum[:, 2 + c, :], WK1, [QE[:, k, :] for k in range(CT)], c, "e_qc")
            for i in range(TT):
                for k in range(CT):
                    last = nc.tensor.matmul(psum[:, 4, i:i + 1], QE[:, k, i * P:(i + 1) * P], col("bk1", k),
                                            start=(k == 0), stop=(k == CT - 1))
            last.then_inc(on["e_cq"], 1)
            pe.wait_ge(on["e_qc_copied"], CT)

            def key_scores(w):
                pe.wait_ge(on[f"ctxt_loaded{w // 2}"], 16)
                for n in range(8):
                    if 8 * w + n >= 4:
                        pe.wait_ge(on["e_masked"], 8 * w + n - 3)
                    for c in range(CT):
                        last = nc.tensor.matmul(psum[:, n % 4, :], QC[:, c, w * P:(w + 1) * P],
                                                CTXT[w // 2][:, c, n * 512:(n + 1) * 512],
                                                start=(c == 0), stop=(c == CT - 1))
                    last.then_inc(on["e_scores"], 1)

            def turn_exps(w):
                pe.wait_ge(on["e_exp"], w + 1)
                if w == 0:
                    pe.wait_ge(on["e_cq_copied"], 1)
                for n in range(8):
                    m = 4 * w + n // 2
                    if m:
                        pe.wait_ge(on["e_turned_a" if n % 2 == 0 else "e_turned_v"], m)
                    for j in range(4):
                        k = 4 * n + j
                        last = nc.tensor.transpose(psum[:, 4 + n % 2, j * P:(j + 1) * P],
                                                   PE1[w % 2][:, k * P:(k + 1) * P], IDENT)
                    last.then_inc(on["e_turned"], 1)

            def weigh_context(w):
                pe.wait_ge(on[f"ctxk_loaded{w // 2}"], 16)
                if w:
                    pe.wait_ge(on["e_normed"], w)
                for k in range(KC):
                    if k % 8 == 0:
                        pe.wait_ge(on["e_turned_a"], 4 * w + k // 8 + 1)
                        pe.wait_ge(on["e_turned_v"], 4 * w + k // 8 + 1)
                    last = nc.tensor.matmul(psum[:, 6, 0:256], PT1[:, k * P:(k + 1) * P], CTXK[w // 2][:, k, :],
                                            start=(k == 0), stop=(k == KC - 1))
                last.then_inc(on["e_att"], 1)

            key_scores(0)
            for w in range(4):
                if w < 3:
                    key_scores(w + 1)
                turn_exps(w)
                weigh_context(w)
            pe.wait_ge(on["e_normed"], 4)
            turn(AO, 0)
            turned()
            pe.wait_ge(on["bv1_loaded"], 16)
            pe.wait_ge(on["e_masked"], 32)
            for i in range(TT):
                linear_rows(psum[:, i, 0:256], tok(HTE, i), WV1, BV[0:1, :], "e_out")

            turn(HLE, 3 * TT, h_ready)
            turned()
            pe.wait_ge(on["qkv_loaded"], 48)

            def project(which, first_wait):
                for n in range(8):
                    i, half = n // 2, n % 2
                    first_wait(n)
                    for c in range(CT):
                        last = nc.tensor.matmul(psum[:, n, :], HTF[:, c, i * P:(i + 1) * P],
                                                WQKV[which][:, c, half * HALF:(half + 1) * HALF],
                                                start=(c == 0), stop=(c == CT - 1))
                    last.then_inc(on["f_qkv"], 1)

            def turn_heads(base, roped):
                pe.wait_ge(on["f_roped"], roped)
                for k in range(8):
                    for i in range(TT):
                        last = nc.tensor.transpose(psum[:, k, i * P:(i + 1) * P], QTM[:, i, k * P:(k + 1) * P],
                                                   IDENT)
                    last.then_inc(on["f_turned"], 1)

            pe.wait_ge(on["x_ready"], 4 * TT)
            project(0, lambda n: None)
            turn_heads(0, 8)
            project(1, lambda n: pe.wait_ge(on["f_turned_copied"], n + 1))
            turn_heads(8, 16)
            project(2, lambda n: pe.wait_ge(on["f_turned_copied"], 8 + n + 1))
            pe.wait_ge(on["f_v_copied"], 8)

            def unit(n):
                b, h = n // HM, n % HM
                return b, h, 64 * (h % 2), h // 2

            def head_scores(n):
                b, h, p0, k = unit(n)
                if n >= 4:
                    pe.wait_ge(on["f_exp"], 2 * (n - 3))
                for qt in range(2):
                    last = nc.tensor.matmul(HEAD_SCORES[n % 4][:, qt * S:(qt + 1) * S],
                                            QT[p0:p0 + DM, k, b * S + qt * P:b * S + (qt + 1) * P],
                                            KT[p0:p0 + DM, k, b * S:(b + 1) * S], start=True, stop=True)
                last.then_inc(on["f_scores"], 1)

            def turn_weights(n):
                pe.wait_ge(on["f_scaled"], 2 * (n + 1))
                if n >= 2:
                    pe.wait_ge(on["f_pt_copied"], n - 1)
                for k in range(2):
                    for qt in range(2):
                        last = nc.tensor.transpose(psum[:, 2 + n % 2, k * S + qt * P:k * S + (qt + 1) * P],
                                                   PM[n % 4][:, qt, k * P:(k + 1) * P], IDENT)
                last.then_inc(on["f_pt"], 1)

            def weigh_heads(pair):
                if pair >= 2:
                    pe.wait_ge(on["f_pv_copied"], pair - 1)
                pe.wait_ge(on["f_pt_copied"], 2 * pair + 2)
                for k in range(2):
                    for j in range(2):
                        b, h, p0, _ = unit(2 * pair + j)
                        last = nc.tensor.matmul(psum[p0:p0 + DM, 4 + pair % 2, 0:S],
                                                VTM[:, 2 * b + k, h * DM:(h + 1) * DM],
                                                PTM[(2 * pair + j) % 4][:, k, :], start=(k == 0), stop=(k == 1),
                                                skip_group_check=True)
                last.then_inc(on["f_pv"], 1)

            for n in range(3):
                head_scores(n)
            for n in range(32):
                if n + 3 < 32:
                    head_scores(n + 3)
                turn_weights(n)
                if n % 2 and n > 2:
                    weigh_heads((n - 3) // 2)
            weigh_heads(15)
            pe.wait_ge(on["wom_loaded"], 16)
            pe.wait_ge(on["f_pv_copied"], 16)
            for i in range(TT):
                linear_rows(psum[:, i, 0:256], tok(OT, i), WOM, None, "f_out")

            turn(HLE, 4 * TT, h_ready)
            turned()
            pe.wait_ge(on["emb_loaded"], 16)
            pe.wait_ge(on["x_ready"], 5 * TT)
            for i in range(TT):
                for c in range(CT):
                    last = nc.tensor.matmul(psum[:, 0, i * E:(i + 1) * E], HTF[:, c, i * P:(i + 1) * P], EMB[:, c, :],
                                            start=(c == 0), stop=(c == CT - 1))
            last.then_inc(on["g_logits"], 1)
            pe.wait_ge(on["g_chosen"], 1)
            for i in range(TT):
                for j in range(i + 1):
                    last = nc.tensor.matmul(psum[:, 1, i * E:(i + 1) * E], const("upper") if j == i else ONES,
                                            R[4][:, j, :], start=(j == 0), stop=(j == i))
            last.then_inc(on["g_cum"], 1)
            pe.wait_ge(on["g_sel"], TT)
            for c in range(CT):
                for i in range(TT):
                    last = nc.tensor.matmul(psum[:, 2 + c, :], HLE[:, i, c * P:(c + 1) * P],
                                            SEL[:, i].rearrange("p e s -> p (e s)"), start=(i == 0), stop=(i == TT - 1))
                last.then_inc(on["g_xg"], 1)
            pe.wait_ge(on["g_xg_copied"], CT)
            pe.wait_ge(on["w1e_loaded"], 16 * CT)
            for m in range(IT):
                for e in range(E):
                    for c in range(CT):
                        last = nc.tensor.matmul(psum[:, 4 + m, e * CAP:(e + 1) * CAP],
                                                W1E[:, c, e, m * P:(m + 1) * P], XG[:, c, e * CAP:(e + 1) * CAP],
                                                start=(c == 0), stop=(c == CT - 1))
                last.then_inc(on["g_up"], 1)
            pe.wait_ge(on["g_selw"], TT)
            for k in range(4):
                bank = k % 2
                if k >= 2:
                    pe.wait_ge(on["g_selt_copied"], k - 1)
                for i in range(TT):
                    last = nc.tensor.transpose(psum[:, bank, i * P:(i + 1) * P],
                                               SELW[:, i, 2 * k:2 * k + 2, :].rearrange("p e s -> p (e s)"), IDENT)
                last.then_inc(on["g_selt"], 1)
            pe.wait_ge(on["g_up_copied"], IT)
            pe.wait_ge(on["w2e_loaded"], 16 * IT)
            for k in range(4):
                pe.wait_ge(on["g_selt_copied"], 4)
                for m in range(IT):
                    for e in (2 * k, 2 * k + 1):
                        half = e % 2
                        last = nc.tensor.matmul(psum[CAP * half:CAP * (half + 1), k, 0:256],
                                                INTER[:, m, e * CAP:(e + 1) * CAP], W2E[:, m, e, :],
                                                start=(m == 0), stop=(m == IT - 1), skip_group_check=True)
                last.then_inc(on["g_down"], 1)
            pe.wait_ge(on["g_down_copied"], 4)
            for i in range(TT):
                for k in range(4):
                    last = nc.tensor.matmul(psum[:, 4 + i, 0:256], SELT[:, k, i * P:(i + 1) * P], OE[:, k, :],
                                            start=(k == 0), stop=(k == 3))
                last.then_inc(on["g_out"], 1)


def constants():
    n = np.arange(P)
    freq = (1.0 / np.float32(10000.0) ** (np.arange(0, DM, 2, dtype=np.float32) / np.float32(DM))).astype(np.float32)
    angle = np.arange(S, dtype=np.float32)[:, None] * freq[None, :]
    sign = np.concatenate([-np.ones(DM // 2), np.ones(DM // 2)])
    cos = np.cos(np.concatenate([angle, angle], axis=1).astype(np.float64))
    sin = np.sin(np.concatenate([angle, angle], axis=1).astype(np.float64)) * sign
    later = np.arange(S)[None, :] > np.arange(S)[:, None]
    tables = {"upper": n[:, None] <= n[None, :], "slots": np.tile(np.arange(1, CAP + 1), (P, 1)),
              "experts": np.tile(np.arange(E) - E, (P, 1)),
              "cos": cos.reshape(2, P, DM).transpose(1, 0, 2).reshape(P, -1),
              "sin": sin.reshape(2, P, DM).transpose(1, 0, 2).reshape(P, -1),
              "causal": (later * -1e30).reshape(2, P, S).transpose(1, 0, 2).reshape(P, -1)}
    return np.ascontiguousarray(np.concatenate([tables[k].astype(np.float32) for k in CONSTS], axis=1))


def layout(inputs):
    a = {k: np.asarray(v) for k, v in inputs.items()}
    cols = {"bq": a["L0_xattn_bq"], "bk": a["L0_xattn_bk"], "in_b": a["L0_attn_in_b"],
            "dwa_b": a["L0_attn_dwa_b"], "sym_b": a["L0_attn_sym_b"], "pw_b": a["L0_attn_pw_b"],
            "ha_b": a["L0_attn_ha_b"], "hb_b": a["L0_attn_hb_b"], "fuse_b": a["L0_attn_fuse_b"],
            "norm_w": a["L0_attn_norm_w"],
            "dwa_k": a["L0_attn_dwa_k"].reshape(IT, P, TAPS_A).transpose(0, 2, 1),
            "sym_k": a["L0_attn_sym_k"].reshape(IT, P, TAPS_B).transpose(0, 2, 1),
            "bq1": a["L1_xattn_bq"], "bk1": a["L1_xattn_bk"]}
    rows = {"bo": a["L0_xattn_bo"], "out_b": a["L0_attn_out_b"], "g1": a["L0_ffn_ln1_g"],
            "b1": a["L0_ffn_ln1_b"], "w1b": a["L0_ffn_b1"], "g2": a["L0_ffn_ln2_g"], "b2": a["L0_ffn_ln2_b"],
            "w2b": a["L0_ffn_b2"], "bv": a["L0_xattn_bv"], "bv1": a["L1_xattn_bv"]}
    c = np.ascontiguousarray
    return {
        "x": c(a["x"].reshape(T, D)),
        "cols": c(np.concatenate([cols[n].reshape(COLS[n], P).T for n in COLS], axis=1)),
        "rows": c(np.concatenate([rows[n].reshape(1, -1) for n in ROW_NAMES], axis=1)),
        "wqT": c(a["L0_xattn_Wq"].T), "wkT": c(a["L0_xattn_Wk"].T), "wvT": c(a["L0_xattn_Wv"].T),
        "ctxT": c(a["ctx_1024"].transpose(0, 2, 1)),
        "mask": c(a["mask_1x1xSxS2_if1"].reshape(S, S2)),
        "A": c(a["L0_attn_A"]), "Bm": c(a["L0_attn_Bm"]), "woT": c(a["L0_xattn_Wo"].T),
        "winT": c(a["L0_attn_in_w"].T), "wpwT": c(a["L0_attn_pw_w"].T), "whaT": c(a["L0_attn_ha_w"].T),
        "whbT": c(a["L0_attn_hb_w"].T), "wfuT": c(a["L0_attn_fuse_w"].T), "woutT": c(a["L0_attn_out_w"].T),
        "w1T": c(a["L0_ffn_w1"].T), "w2T": c(a["L0_ffn_w2"].T),
        "wq1T": c(a["L1_xattn_Wq"].T), "wk1": c(a["L1_xattn_Wk"]), "wv1T": c(a["L1_xattn_Wv"].T),
        "ctx": c(a["ctx_1024"]), "mask1": c(a["mask_SxS2_ff0"]),
        "wqm": c(a["L1_attn_Wq"]), "wkm": c(a["L1_attn_Wk"]), "wvm": c(a["L1_attn_Wv"]), "wom": c(a["L1_attn_Wo"]),
        "embT": c(a["L1_ffn_expert_embeddings"].T), "w1e": c(a["L1_ffn_first_linear"].transpose(0, 2, 1)),
        "w2e": c(a["L1_ffn_second_linear"].transpose(0, 2, 1)), "consts": constants(),
    }


def kernel(**inputs):
    import concourse.bacc as bacc
    from concourse.bass_utils import run_bass_kernel_spmd

    nc = bacc.Bacc("TRN2", target_bir_lowering=False, num_devices=1)
    arrays = layout(inputs)
    tensors = {name: nc.dram_tensor(name, a.shape, mybir.dt.from_np(a.dtype), kind="ExternalInput").ap()
               for name, a in arrays.items()}
    tensors["out"] = nc.dram_tensor("out", (T, D), F32, kind="ExternalOutput").ap()
    build(nc, tensors)
    got = run_bass_kernel_spmd(nc, [arrays], core_ids=[0])
    return got.results[0]["out"].reshape(B, S, D)
```

```python
from contextlib import ExitStack

import numpy as np

import concourse.bass as bass
from concourse import mybir

F32 = mybir.dt.float32
BF16 = mybir.dt.bfloat16
I32 = mybir.dt.int32
ALU = mybir.AluOpType
ACT = mybir.ActivationFunctionType
AX = mybir.AxisListType

P = 128
B, S, S2, D = 2, 256, 4096, 256
T = B * S
TT = T // P
CT = D // P
H, DH = 16, 16
G = 4
GPB = H // G
NG = B * GPB
KC = S2 // P
CH = 512
NCH = S2 // CH
ROWS = 6 * DH
KROWS = ROWS + 3
VW = DH + 1
MASKED = -(2.0 ** 100)
K_PARTS = (0, 0, 0, 1, 1, 2)
Q_PARTS = (0, 1, 2, 0, 1, 0)

DI = 512
IT = DI // P
DS = 16
TAPS_A, LEFT_A = 4, 1
TAPS_B, LEFT_B = 9, 4
PAD = S + 8
FF = 1024
FT = FF // P
HM, DM = 16, 64
HALF = HM * DM // 2
E, EI, CAP = 8, 512, T // 8
ROUND = 1.5 * 2.0 ** 23

COLS = {"bq": 2, "bk": 2, "in_b": 8, "dwa_b": 4, "sym_b": 4, "pw_b": 4, "ha_b": 2, "hb_b": 2,
        "fuse_b": 4, "norm_w": 2, "dwa_k": 16, "sym_k": 36, "bq1": 2, "bk1": 2}
ROW_NAMES = {"bo": 256, "out_b": 256, "g1": 256, "b1": 256, "w1b": 1024, "g2": 1024, "b2": 1024,
             "w2b": 256, "bv": 256, "bv1": 256}
CONSTS = {"upper": P, "slots": CAP, "experts": E, "cos": 2 * DM, "sin": 2 * DM, "causal": 2 * S}


def offsets(sizes):
    at, out = 0, {}
    for name, n in sizes.items():
        out[name] = at
        at += n
    return out, at


COL_AT, N_COLS = offsets(COLS)
ROW_AT, N_ROWS = offsets(ROW_NAMES)
CONST_AT, N_CONSTS = offsets(CONSTS)
N_FFN_ROWS = ROW_AT["bv"]


def build(nc, t):
    ctx = ExitStack()
    with ctx:
        arena = ctx.enter_context(nc.sbuf_tensor("arena", [P, 53120], F32))
        psum = ctx.enter_context(nc.psum_tensor("psum", [P, 8, 512], F32))

        def sem(name):
            return ctx.enter_context(nc.semaphore(name))

        def f32(at, n):
            return arena[:, at:at + n]

        def b16(at, n):
            return arena[:, at:at + n // 2].bitcast(BF16)

        KST = [b16(8192 * i, 16384).rearrange("p (j n) -> p j n", j=G) for i in range(3)]
        V_AT = 24576
        V = f32(V_AT, KC * H * VW).rearrange("p (k h e) -> p k h e", k=KC, h=H)
        V_flat = f32(V_AT, KC * H * VW + 16)
        MASKB = b16(33296, 8192).rearrange("p (t n) -> p t n", t=2)
        QST = b16(37392, 8192).rearrange("p (h n) -> p h n", h=H)
        PR = [f32(41488 + 1024 * i, 1024) for i in range(2)]
        CTX = [f32(43536 + 1024 * i, 1024).rearrange("p (c n) -> p c n", c=CT) for i in range(2)]
        K32 = [f32(45584 + 512 * i, 512) for i in range(2)]
        KPT = [b16(46608 + 768 * i, 1536).rearrange("p (r n) -> p r n", r=3) for i in range(2)]
        X = f32(48144, 1024).rearrange("p (t c) -> p t c", t=TT)
        PVS = f32(49168, 256)
        CTXN = f32(49424, 1024).rearrange("p (t c) -> p t c", t=TT)
        at = 50448
        IDENT = f32(at, 128); at += 128
        IDENTB = b16(at, 128); at += 64
        COLT = f32(at, N_COLS); at += N_COLS
        BV = f32(at, 256); at += 256
        MX = [f32(at + 64 * i, 64) for i in range(2)]; at += 128
        M8 = f32(at, 8); at += 8
        MR = f32(at, 8); at += 8
        MPART = b16(at, 24).rearrange("p (m r) -> p m r", r=3); at += 12
        RINV = f32(at, 8).rearrange("p (t j) -> p t j", t=2); at += 8
        BN = f32(at, 48); at += 48
        MV = f32(at, 8); at += 8
        SD = f32(at, 8); at += 8
        FLAGF = f32(at, 4); at += 4
        VS = [f32(at + 84 * i, 84) for i in range(4)]; at += 336
        FLAG = arena[0:1, at:at + 1].bitcast(I32); at += 1
        ONES = f32(at, 128); at += 128
        AW = f32(at, IT * DS).rearrange("p (t s) -> p t s", t=IT); at += IT * DS
        assert at <= 52096, at
        MASKI = arena[:, 16384:16384 + 8192].bitcast(I32).rearrange("p (t n) -> p t n", t=2)
        HN = f32(41488, 1024).rearrange("p (t c) -> p t c", t=TT)
        HT = f32(42512, 1024).rearrange("p (c n) -> p c n", c=CT)
        WQ = f32(8192, 512).rearrange("p (c f) -> p c f", c=CT)
        WK = f32(52096, 512).rearrange("p (c f) -> p c f", c=CT)
        WV = f32(52608, 512).rearrange("p (c f) -> p c f", c=CT)

        def col(name, i):
            return COLT[:, COL_AT[name] + i:COL_AT[name] + i + 1]

        def ST(i):
            return psum[:, 2 * i:2 * i + 2, :]

        def SP_(i):
            return psum[:, 4 + i, :]

        PV = psum[:, 6, 0:256]
        PX = psum[:, 7, :]

        ROWS_T = f32(0, N_FFN_ROWS)

        def row(name):
            return ROWS_T[:, ROW_AT[name]:ROW_AT[name] + ROW_NAMES[name]]

        WO = f32(4352, 512).rearrange("p (c f) -> p c f", c=CT)
        WOUT = f32(4864, 1024).rearrange("p (t f) -> p t f", t=IT)
        TW1 = b16(5888, 2048).rearrange("p (c f) -> p c f", c=CT)
        TW2 = b16(6912, 2048).rearrange("p (t f) -> p t f", t=FT)
        WIN = f32(16384, 2048).rearrange("p (c f) -> p c f", c=CT)
        WPW = f32(18432, 2048).rearrange("p (t f) -> p t f", t=IT)
        WHA = f32(20480, 1024).rearrange("p (t f) -> p t f", t=IT)
        WHB = f32(21504, 1024).rearrange("p (t f) -> p t f", t=IT)
        WFU = f32(22528, 2048).rearrange("p (t f) -> p t f", t=IT)
        W1RAW = f32(43536, 2048)
        W2RAW = f32(45584, 2048)
        BMT = f32(47632, IT * 32).rearrange("p (t s) -> p t s", t=IT)
        HL = f32(24576, 1024).rearrange("p (t c) -> p t c", t=TT)
        HS = f32(25600, 1024).rearrange("p (t c) -> p t c", t=TT)
        HTC = f32(26624, 1024).rearrange("p (c n) -> p c n", c=CT)
        GATE = f32(27648, 2048).rearrange("p (m n) -> p m n", m=IT)
        VAL = f32(29696, IT * B * PAD).rearrange("p (m b n) -> p m b n", m=IT, b=B)
        AWK = f32(31808, IT * TAPS_A * 32).rearrange("p (m k s) -> p m k s", m=IT, k=TAPS_A)
        CB = f32(33856, 2048).rearrange("p (m n) -> p m n", m=IT)
        SB = f32(35904, 2048).rearrange("p (m n) -> p m n", m=IT)
        WHABM = f32(40512, 256)
        WHBPW = f32(37952, 1024).rearrange("p (m f) -> p m f", m=IT)
        HBBIAS = f32(40768, 2)
        AS = f32(40000, 512)
        YC = f32(31808, 2048).rearrange("p (m n) -> p m n", m=IT)
        YG = CB
        HQ = b16(25600, 1024).rearrange("p (t c) -> p t c", t=TT)
        HQT = b16(26112, 1024).rearrange("p (c n) -> p c n", c=CT)
        UH = f32(26624, 4096).rearrange("p (t f) -> p t f", t=TT)
        QH = b16(30720, 4096).rearrange("p (t f) -> p t f", t=TT)
        QHT = b16(32768, 4096).rearrange("p (k n) -> p k n", k=FT)
        CTXT = [f32(8192, 8192).rearrange("p (c n) -> p c n", c=CT), f32(0, 8192).rearrange("p (c n) -> p c n", c=CT)]
        CTXK = [f32(16384, 8192).rearrange("p (k c) -> p k c", k=KC), f32(8192, 8192).rearrange("p (k c) -> p k c", k=KC)]
        PE1 = [f32(24576 + 4096 * i, 4096) for i in range(2)]
        QE = f32(32768, 1024).rearrange("p (c n) -> p c n", c=CT)
        QC = f32(33792, 1024).rearrange("p (c n) -> p c n", c=CT)
        MRING = [f32(34816 + 2048 * i, 2048) for i in range(2)]
        PT1 = f32(38912, 4096)
        WQ1 = f32(43536, 512).rearrange("p (c f) -> p c f", c=CT)
        WK1 = f32(44048, 512).rearrange("p (c f) -> p c f", c=CT)
        WV1 = f32(44560, 512).rearrange("p (c f) -> p c f", c=CT)
        HTE = f32(45072, 1024).rearrange("p (c n) -> p c n", c=CT)
        AO = f32(46096, 1024).rearrange("p (t c) -> p t c", t=TT)
        HLE = CTXN
        WQKV = [f32(16384 + 2048 * i, 2048).rearrange("p (c f) -> p c f", c=CT) for i in range(3)]
        WOM = f32(22528, 2048).rearrange("p (k f) -> p k f", k=8)
        KTM = f32(24576, 4096).rearrange("p (t f) -> p t f", t=TT)
        QTM = f32(28672, 4096).rearrange("p (t f) -> p t f", t=TT)
        VTM = QTM
        QT = f32(32768, 4096).rearrange("p (k n) -> p k n", k=8)
        OT = QT
        KT = f32(36864, 4096).rearrange("p (k n) -> p k n", k=8)
        PM = [f32(at, 512).rearrange("p (t n) -> p t n", t=2) for at in (40960, 41472, 46096, 46608)]
        PTM = [f32(at, 512) for at in (41984, 42496, 45072, 45584)]
        HEAD_SCORES = [psum[:, bank, :] for bank in (0, 1, 6, 7)]
        VALUE_BANKS = (2, 3, 4, 5, 7)
        T2 = [f32(45072 + 512 * i, 512).rearrange("p (h d) -> p h d", h=8) for i in range(2)]
        HTF = f32(43536, 1024).rearrange("p (c n) -> p c n", c=CT)

        def causal_head(n):
            return n % HM < 8

        def keys(n, qt):
            return P if causal_head(n) and qt == 0 else S

        CONST = f32(47120, N_CONSTS)

        def const(name):
            return CONST[:, CONST_AT[name]:CONST_AT[name] + CONSTS[name]]

        W1E = f32(0, 8192).rearrange("p (c e i) -> p c e i", c=CT, e=E)
        W2E = f32(8192, 8192).rearrange("p (t e h) -> p t e h", t=IT, e=E)
        EMB = f32(44560, 16).rearrange("p (c e) -> p c e", c=CT)
        SEL = f32(24576, 2048).rearrange("p (t e s) -> p t e s", t=TT, e=E)
        SELW = f32(26624, 2048).rearrange("p (t e s) -> p t e s", t=TT, e=E)
        SELT = f32(28672, 2048).rearrange("p (k n) -> p k n", k=4)
        XG = f32(30720, 1024).rearrange("p (c n) -> p c n", c=CT)
        INTER = f32(31744, 2048).rearrange("p (t n) -> p t n", t=IT)
        OE = f32(33792, 1024).rearrange("p (k c) -> p k c", k=4)
        R = [f32(34816 + 32 * i, 32).rearrange("p (t e) -> p t e", e=E) for i in range(12)]
        UPPER = b16(44576, P)
        ONESB = b16(44576 + P // 2, P)
        CHOSENB = b16(44576 + P, TT * E).rearrange("p (t e) -> p t e", e=E)
        R1 = [f32(35200 + 4 * i, 4) for i in range(8)]
        assert 47120 + N_CONSTS <= 48144
        at = 52096
        AMAX = f32(at, 4); at += 4
        QSC = f32(at, 4); at += 4
        OSC = f32(at, 4); at += 4
        CQ = f32(at, 4); at += 4
        EMX = f32(at, 32); at += 32
        EM = f32(at, 4); at += 4
        ET = f32(at, 4); at += 4
        ENB = f32(at, 4); at += 4
        ESUM = f32(at, 4); at += 4
        ERI = f32(at, 4); at += 4
        FMX = f32(at, 64); at += 64
        FNB = f32(at, 64); at += 64
        FSUM = f32(at, 64); at += 64
        FRI = f32(at, 64); at += 64
        WSUM = f32(at, 2); at += 2
        WMEAN = f32(at, 2); at += 2
        WSC = f32(at, 2); at += 2
        ABIAS = f32(at, 1); at += 1
        NEGM = f32(at, 4); at += 4
        assert at <= 53120

        STACK0 = 96 * NCH // 2
        kparts = nc.dram_tensor("kparts", [B, 3, D, S2], BF16, kind="Internal").ap()
        qparts = nc.dram_tensor("qparts", [3, D, T], BF16, kind="Internal").ap()

        x_loaded = sem("x_loaded")
        cols_loaded = sem("cols_loaded")
        wq_loaded = sem("wq_loaded")
        wkv_loaded = sem("wkv_loaded")
        mask_loaded = sem("mask_loaded")
        ident_built = sem("ident_built")
        ones_built = sem("ones_built")
        kones_built = sem("kones_built")
        mask_counted = sem("mask_counted")
        mask_flagged = sem("mask_flagged")
        mask_step = sem("mask_step")
        ln_step = sem("ln_step")
        ln_var = sem("ln_var")
        ln_sd = sem("ln_sd")
        h_ready = sem("h_ready")
        ht_psum = sem("ht_psum")
        ht_ready = sem("ht_ready")
        q_psum = sem("q_psum")
        q_split = sem("q_split")
        q_ready = sem("q_ready")
        q_stacked = sem("q_stacked")
        ctx_loaded = [sem(f"ctx_loaded{i}") for i in range(2)]
        k_psum = sem("k_psum")
        k_copied = sem("k_copied")
        k_rest = sem("k_rest")
        k_middle = sem("k_middle")
        k_low = sem("k_low")
        k_stored = [sem(f"k_stored{i}") for i in range(2)]
        v_psum = sem("v_psum")
        v_copied = sem("v_copied")
        k_stacked = [sem(f"k_stacked{i}") for i in range(3)]
        s_ready = sem("s_ready")
        s_maxed = sem("s_maxed")
        m_step = sem("m_step")
        m_split = sem("m_split")
        m_turned = sem("m_turned")
        m_stacked = sem("m_stacked")
        st_ready = sem("st_ready")
        exp_ready = sem("exp_ready")
        pv_done = sem("pv_done")
        pv_copied = sem("pv_copied")
        pv_turned = sem("pv_turned")
        norm_step = sem("norm_step")
        v_staged = sem("v_staged")
        out_stored = sem("out_stored")
        SIGNALS = """
            aw_loaded bm_loaded raw_loaded mix_loaded rows_loaded wo_loaded bv1_loaded l1w_loaded
            ctxt_loaded0 ctxt_loaded1 ctxk_loaded0 ctxk_loaded1 mask1_loaded0 mask1_loaded1
            qkv_loaded wom_loaded const_loaded emb_loaded w1e_loaded w2e_loaded
            w_summed w_total w_quantised
            b_out x_ready
            c_padded c_in c_in_copied c_a_weights c_conv_b c_sigmoid c_silu c_a c_a_copied
            c_habm c_habm_copied c_ha c_ha_copied c_hbpw c_hbpw_copied c_hb c_hb_copied c_fuse c_gated c_out
            d_quant d_turned d_turned_copied d_up d_hidden d_gelu d_means d_centred d_gained d_quant2 d_turned2
            d_turned2_copied d_down
            e_q e_q_copied e_qc e_qc_copied e_cq e_cq_copied e_scores e_masked e_bias e_exp
            e_turned e_turned_a e_turned_v e_att e_normed e_out
            f_qkv f_roped f_rope_part f_v_copied f_turned f_turned_copied f_scores f_bias f_exp
            f_scaled f_pt f_pt_copied f_pv f_pv_copied f_out
            g_counters g_logits g_chosen g_cum g_sel g_selw g_xg g_xg_copied g_up g_up_copied g_down
            g_down_copied g_selt g_selt_copied g_out step_v
        """.split()
        on = {name: sem(name) for name in SIGNALS}

        def by_part_of(ap):
            return ap.rearrange("(c p) n -> p c n", p=P)

        block = ctx.enter_context(nc.Block())

        @block.sync
        def _(sp):
            sp.dma_start(X, t["x"].rearrange("(t p) c -> p t c", p=P)).then_inc(x_loaded, 16)
            sp.dma_start(COLT, t["cols"]).then_inc(cols_loaded, 16)
            sp.dma_start(AW, t["A"].rearrange("(t p) s -> p t s", p=P)).then_inc(on["aw_loaded"], 16)
            sp.dma_start(BV, t["rows"][:, ROW_AT["bv"]:ROW_AT["bv"] + 256].broadcast_to((P, 256)))\
              .then_inc(cols_loaded, 16)
            sp.dma_start(WQ, t["wqT"].rearrange("(c p) f -> p c f", p=P)).then_inc(wq_loaded, 16)
            sp.dma_start(WK, t["wkT"].rearrange("(c p) f -> p c f", p=P)).then_inc(wkv_loaded, 16)
            sp.dma_start(WV, t["wvT"].rearrange("(c p) f -> p c f", p=P)).then_inc(wkv_loaded, 16)

            def load_ctx(b, ch, slot):
                sp.dma_start(CTX[slot], t["ctxT"][b].rearrange("(c p) n -> p c n", p=P)
                             [:, :, bass.ds(ch * CH, CH)]).then_inc(ctx_loaded[slot], 16)

            def store_k(b, ch, f):
                piece = 16 * b + 2 * ch + f
                sp.wait_ge(k_low, piece + 1)
                sp.dma_start(kparts[b, :, f * P:(f + 1) * P, bass.ds(ch * CH, CH)]
                             .rearrange("r p n -> p r n"), KPT[f]).then_inc(k_stored[f], 16)

            def store_q():
                for f in range(CT):
                    sp.wait_ge(q_ready, f + 1)
                    sp.dma_start(qparts[:, f * P:(f + 1) * P, :].rearrange("r p n -> p r n"), KPT[f])\
                      .then_inc(k_stored[f], 16)
                for f in range(CT):
                    sp.wait_ge(k_stored[f], 16)
                for r in range(6):
                    sp.dma_start(QST[DH * r:DH * (r + 1), :, :],
                                 qparts[Q_PARTS[r]].rearrange("(h d) n -> d h n", d=DH)).then_inc(q_stacked, 16)

            def load_first_stack(i):
                for r in range(6):
                    src = kparts[0, K_PARTS[r], 0:G * DH, bass.ds(i * 2 * CH, 2 * CH)]
                    sp.dma_start(KST[0][DH * r:DH * (r + 1), :, bass.ds(i * 2 * CH, 2 * CH)],
                                 src.rearrange("(j d) n -> d j n", d=DH)).then_inc(k_stacked[0], 16)

            def load_stack(gg):
                b, g, slot = gg // GPB, gg % GPB, gg % 3
                for r in range(6):
                    src = kparts[b, K_PARTS[r], g * G * DH:(g + 1) * G * DH, :]
                    sp.dma_start(KST[slot][DH * r:DH * (r + 1), :, :],
                                 src.rearrange("(j d) n -> d j n", d=DH)).then_inc(k_stacked[slot], 16)

            load_ctx(0, 0, 0)
            load_ctx(0, 1, 1)
            sp.dma_start(MASKI, t["mask"].rearrange("(t p) n -> p t n", p=P)).then_inc(mask_loaded, 16)
            store_q()
            for b in range(B):
                def chunk_pair(i, more, first=False):
                    for u in range(2):
                        if b == 1 and more:
                            sp.wait_ge(k_psum, 4 * i + (2 * u + 18))
                            load_ctx(b, 2 * i + (u + 2), u)
                        for f in range(CT):
                            store_k(b, 2 * i + u, f)
                        if b == 0 and u == 0 and not first:
                            sp.wait_ge(k_stored[0], 32 * i + 16)
                            load_first_stack(i - 1)
                        if b == 0:
                            sp.wait_ge(v_psum, 8 * i + (4 * u + 4))
                            if more:
                                load_ctx(b, 2 * i + (u + 2), u)
                chunk_pair(0, True, True)
                with sp.Fori(1, NCH // 2 - 1) as i:
                    chunk_pair(i, True)
                chunk_pair(NCH // 2 - 1, False)
                if b == 0:
                    load_ctx(1, 0, 0)
                    load_ctx(1, 1, 1)
                for f in range(CT):
                    sp.wait_ge(k_stored[f], 16 + 16 * NCH * (b + 1))
                if b == 0:
                    load_first_stack(NCH // 2 - 1)
                    sp.wait_ge(q_psum, CT)
                    load_stack(1)
            sp.wait_ge(mask_step, 2 * NCH)
            load_stack(2)
            load_ctx(1, 0, 0)
            load_ctx(1, 1, 1)
            sp.wait_ge(st_ready, KC)
            load_stack(3)
            sp.wait_ge(st_ready, 2 * KC)
            load_stack(4)
            sp.wait_ge(st_ready, 3 * KC)
            load_stack(5)
            with sp.Fori(0, NCH // 2 - 1) as i:
                for u in range(2):
                    sp.wait_ge(v_psum, KC + 8 * i + 4 * u + 4)
                    load_ctx(1, 2 * i + u + 2, u)
            sp.wait_ge(st_ready, 4 * KC)
            load_stack(6)
            sp.wait_ge(st_ready, 5 * KC)
            load_stack(7)

            def load(dst, src, name):
                sp.dma_start(dst, src).then_inc(on[name], 16)

            def by_part(name):
                return t[name].rearrange("(c p) f -> p c f", p=P)

            sp.wait_ge(v_psum, 2 * KC)
            load(W1RAW.rearrange("p (c f) -> p c f", c=CT), by_part("w1T"), "raw_loaded")
            load(W2RAW.rearrange("p (c f) -> p c f", c=FT), by_part("w2T"), "raw_loaded")
            for copy in range(2):
                load(BMT[:, :, copy * DS:(copy + 1) * DS], by_part("BmT"), "bm_loaded")
            sp.wait_ge(st_ready, 6 * KC)
            for dst, name in ((WIN, "winT"), (WPW, "wpw"), (WHA, "whaT"), (WHB, "whbT"), (WFU, "wfuT")):
                load(dst, by_part(name), "mix_loaded")
            sp.wait_ge(st_ready, 7 * KC)
            load(WO, by_part("woT"), "wo_loaded")
            load(WOUT, by_part("woutT"), "wo_loaded")
            load(ROWS_T, t["rows"][:, 0:N_FFN_ROWS].broadcast_to((P, N_FFN_ROWS)), "rows_loaded")
            sp.wait_ge(st_ready, 8 * KC)
            load(CTXT[0], by_part_of(t["ctxT"][0]), "ctxt_loaded0")
            sp.wait_ge(norm_step, 3 * NG)
            load(BV, t["rows"][:, ROW_AT["bv1"]:ROW_AT["bv1"] + 256].broadcast_to((P, 256)), "bv1_loaded")
            sp.wait_ge(on["w_quantised"], 6)
            load(WQ1, by_part("wq1T"), "l1w_loaded")
            load(WK1, by_part("wk1"), "l1w_loaded")
            load(WV1, by_part("wv1T"), "l1w_loaded")
            sp.wait_ge(on["c_habm"], 1)
            load(CONST, t["consts"], "const_loaded")
            sp.wait_ge(on["c_fuse"], 4)
            load(CTXK[0], t["ctx"][0].rearrange("(k p) c -> p k c", p=P), "ctxk_loaded0")
            sp.wait_ge(on["c_out"], 4)

            def load_mask(n):
                unit, half = n // 2, n % 2
                if n >= 2:
                    sp.wait_ge(on["e_masked"], 4 * (n - 1))
                qt = unit % 2
                load(MRING[half], t["mask1"][qt * P:(qt + 1) * P, half * 2048:(half + 1) * 2048],
                     f"mask1_loaded{half}")

            load_mask(0)
            load_mask(1)
            sp.wait_ge(on["x_ready"], 3 * TT)
            load(CTXT[1], by_part_of(t["ctxT"][1]), "ctxt_loaded1")
            for n in range(2, 4):
                load_mask(n)
            sp.wait_ge(on["e_scores"], 16)
            load(CTXK[1], t["ctx"][1].rearrange("(k p) c -> p k c", p=P), "ctxk_loaded1")
            for n in range(4, 8):
                load_mask(n)
            sp.wait_ge(on["e_att"], 2)
            for dst, name in zip(WQKV, ("wqm", "wkm", "wvm")):
                load(dst, by_part(name), "qkv_loaded")
            load(WOM, by_part("wom"), "wom_loaded")
            sp.wait_ge(on["e_scores"], 32)
            for k in range(CT):
                load(W1E[:, k], t["w1e"][:, k * P:(k + 1) * P, :].rearrange("e p i -> p e i"), "w1e_loaded")
            sp.wait_ge(on["e_att"], 4)
            for k in range(IT):
                load(W2E[:, k], t["w2e"][:, k * P:(k + 1) * P, :].rearrange("e p h -> p e h"), "w2e_loaded")
            sp.wait_ge(on["e_out"], 4)
            load(EMB, by_part("embT"), "emb_loaded")
            sp.wait_ge(on["x_ready"], 6 * TT)
            sp.dma_start(t["out"].rearrange("(t p) c -> p t c", p=P), X).then_inc(out_stored, 16)
            sp.wait_ge(out_stored, 16)

        @block.gpsimd
        def _(pool):
            nc.gpsimd.memset(IDENT, 0.0).then_inc(ident_built, 1)
            nc.gpsimd.memset(IDENTB, 0.0).then_inc(ident_built, 1)
            nc.gpsimd.memset(ONES, 1.0).then_inc(ones_built, 1)
            pool.wait_ge(ident_built, 2)
            for m in (IDENT, IDENTB):
                nc.gpsimd.affine_select(out=m, in_=m, compare_op=ALU.not_equal, fill=1.0, base=0,
                                        pattern=[[-1, P]], channel_multiplier=1).then_inc(ident_built, 1)
            nc.gpsimd.memset(V[:, :, :, DH:VW], 1.0).then_inc(ones_built, 1)
            nc.gpsimd.memset(V_flat[:, KC * H * VW:KC * H * VW + 16], 0.0).then_inc(ones_built, 1)
            two_ones = float(np.array([0x3F803F80], np.uint32).view(np.float32)[0])
            pool.wait_ge(ones_built, 3)
            nc.gpsimd.memset(arena[ROWS:KROWS, 0:8192], two_ones).then_inc(kones_built, 1)
            pool.wait_ge(kones_built, 1)
            nc.gpsimd.memset(arena[ROWS:KROWS, 8192 + 512:16384], two_ones).then_inc(kones_built, 1)
            pool.wait_ge(kones_built, 2)

            def low_part(piece, f):
                pool.wait_ge(k_middle, piece + 1)
                nc.gpsimd.tensor_tensor(KPT[f][:, 2, :], K32[f], KPT[f][:, 1, :], ALU.subtract)\
                  .then_inc(k_low, 1)

            with pool.Fori(0, NCH) as i:
                for f in range(CT):
                    low_part(2 * i + f, f)
            pool.wait_ge(k_low, 2 * NCH)
            pool.wait_ge(q_psum, CT)
            nc.gpsimd.memset(arena[ROWS:KROWS, 8192:8192 + 512], two_ones).then_inc(kones_built, 1)
            pool.wait_ge(kones_built, 3)
            with pool.Fori(0, NCH) as i:
                for f in range(CT):
                    low_part(2 * i + f + 16, f)
            for gg in range(NG):
                g, n0 = gg % GPB, KC * gg
                pool.wait_ge(v_copied, KC * (gg // GPB + 1))

                def stage_values(i, first):
                    for u in range(8):
                        if not first or n0 + u >= 4:
                            pool.wait_ge(pv_done, 8 * i + (n0 + u - 3))
                        nc.gpsimd.tensor_copy(VS[u % 4], V_flat[:, bass.ds(i * (8 * H * VW) + (u * H * VW + g * G * VW), 84)])\
                          .then_inc(v_staged, 1)
                        if first and gg < 2 and u % 2:
                            if gg == 0 and u == 1:
                                pool.wait_ge(mask_step, 2 * NCH)
                            pool.wait_ge(v_staged, n0 + u + 1)
                            piece = 16384 + 1024 * (4 * gg + u // 2)
                            nc.gpsimd.memset(arena[ROWS:KROWS, piece:piece + 1024], two_ones).then_inc(kones_built, 1)
                            pool.wait_ge(kones_built, 4 + 4 * gg + u // 2)
                stage_values(0, True)
                with pool.Fori(1, KC // 8) as i:
                    stage_values(i, False)

            pool.wait_ge(pv_done, NG * KC)
            pool.wait_ge(v_staged, NG * KC)
            nc.gpsimd.memset(VAL[:, :, :, 0:4], 0.0).then_inc(on["c_padded"], 1)
            nc.gpsimd.memset(VAL[:, :, :, S + 4:PAD], 0.0).then_inc(on["c_padded"], 1)
            pool.wait_ge(on["c_padded"], 2)

            nc.gpsimd.memset(AWK, 0.0).then_inc(on["c_a_weights"], 1)
            nc.gpsimd.memset(ABIAS, 0.0).then_inc(on["c_a_weights"], 1)
            pool.wait_ge(on["c_a_weights"], 2)
            pool.wait_ge(on["aw_loaded"], 16)
            for m in range(IT):
                for k in range(TAPS_A):
                    nc.gpsimd.tensor_scalar(AWK[:, m, k, 0:DS], AW[:, m, :], col("dwa_k", TAPS_A * m + k), None,
                                            ALU.mult).then_inc(on["c_a_weights"], 1)

            for i in range(1, TT):
                pool.wait_ge(on["d_centred"], i)
                nc.gpsimd.tensor_tensor(UH[:, i, :], UH[:, i, :], row("g2"), ALU.mult).then_inc(on["d_gained"], 1)

            for piece in range(16):
                pool.wait_ge(on["f_rope_part"], 3 * (piece + 1))
                i, half = piece % 8 // 2, piece % 2
                out = (KTM if piece >= 8 else QTM)[:, i, half * HALF:(half + 1) * HALF]\
                    .rearrange("p (h d) -> p h d", h=8)
                nc.gpsimd.tensor_tensor(out, out, T2[piece % 2], ALU.add).then_inc(on["f_roped"], 1)
            pool.wait_ge(on["f_roped"], 16)
            nc.gpsimd.memset(ONESB, 1.0).then_inc(on["g_counters"], 1)
            pool.wait_ge(on["const_loaded"], 16)
            nc.gpsimd.tensor_copy(UPPER, const("upper")).then_inc(on["g_counters"], 1)

        @block.scalar
        def _(act):
            act.wait_ge(ln_var, 1)
            nc.scalar.activation(SD[:, 0:4], SD[:, 4:8], ACT.Sqrt).then_inc(ln_sd, 1)
            for c in range(CT):
                act.wait_ge(ht_psum, c + 1)
                nc.scalar.activation(HT[:, c, :], psum[:, 6 + c, :], ACT.Copy).then_inc(ht_ready, 1)

            def copy_k(piece, f, reuse):
                act.wait_ge(k_psum, piece + 1)
                act.wait_ge(k_stored[f], reuse)
                bias = COLT[:, COL_AT["bk"] + f:COL_AT["bk"] + f + 1]
                nc.scalar.activation(K32[f], psum[:, f, :], ACT.Identity, bias=bias).then_inc(k_copied, 1)
                nc.scalar.activation(KPT[f][:, 0, :], psum[:, f, :], ACT.Identity, bias=bias).then_inc(k_copied, 1)

            def middle_part(piece, f):
                act.wait_ge(k_rest, piece + 1)
                nc.scalar.activation(KPT[f][:, 1, :], K32[f], ACT.Copy).then_inc(k_middle, 1)

            def v_tile(done, kc, bank):
                act.wait_ge(v_psum, done + 1)
                nc.scalar.activation(V[:, bass.ds(kc, 1), :, 0:DH],
                                     psum[:, bank, 0:256].rearrange("p (o h d) -> p o h d", o=1, h=H),
                                     ACT.Copy).then_inc(v_copied, 1)

            act.wait_ge(cols_loaded, 32)
            with act.Fori(0, NCH) as i:
                for f in range(CT):
                    copy_k(2 * i + f, f, 16 * i + 16)
                for v in range(4):
                    v_tile(4 * i + v, 4 * i + v, 2 + v % 2)
            def second_batch(i, first):
                if not first:
                    middle_part(2 * i + 15, 1)
                copy_k(2 * i + 16, 0, 16 * i + 16 * (NCH + 1))
                middle_part(2 * i + 16, 0)
                copy_k(2 * i + 17, 1, 16 * i + 16 * (NCH + 1))

            second_batch(0, True)
            with act.Fori(1, NCH) as i:
                second_batch(i, False)
            middle_part(4 * NCH - 1, 1)

            def stack_max(gg, pair):
                b, j = gg // GPB, G * (gg % GPB) + 2 * pair
                act.wait_ge(m_turned, 2 * gg + pair + 1)
                nc.scalar.activation(QST[ROWS:KROWS, j:j + 2, b * S:(b + 1) * S],
                                     PX[ROWS:KROWS, :].rearrange("p (j n) -> p j n", j=2),
                                     ACT.Copy).then_inc(m_stacked, 1)

            for pair in range(2):
                stack_max(0, pair)

            for gg in range(NG):
                if gg == GPB:
                    act.wait_ge(v_staged, GPB * KC)
                    with act.Fori(0, KC // 4) as i:
                        for v in range(4):
                            v_tile(4 * i + v + KC, 4 * i + v, v)
                n0 = KC * gg

                def exps(i, first, last=False):
                    for u in range(8):
                        act.wait_ge(st_ready, 8 * i + (n0 + u + 1))
                        if not first or n0 + u >= 2:
                            act.wait_ge(pv_done, 8 * i + (n0 + u - 1))
                        nc.scalar.activation(PR[u % 2], ST(u % 2).rearrange("p b n -> p (b n)"), ACT.Exp)\
                          .then_inc(exp_ready, 1)
                        if last and u in (3, 5) and gg + 1 < NG:
                            stack_max(gg + 1, u // 4)
                exps(0, True)
                with act.Fori(1, KC // 8 - 1) as i:
                    exps(i, False)
                exps(KC // 8 - 1, False, True)
                act.wait_ge(pv_done, n0 + KC)
                if gg:
                    act.wait_ge(pv_turned, gg)
                nc.scalar.activation(PVS, PV, ACT.Copy).then_inc(pv_copied, 1)


            sqrts = [1]

            def root():
                sqrts[0] += 1
                act.wait_ge(ln_var, sqrts[0])
                nc.scalar.activation(SD[:, 0:4], SD[:, 4:8], ACT.Sqrt).then_inc(ln_sd, 1)

            turns = [1]

            def copy_turned(dst, scale=None):
                for c in range(CT):
                    act.wait_ge(ht_psum, CT * turns[0] + c + 1)
                    if scale is None:
                        nc.scalar.activation(dst[:, c, :], psum[:, 6 + c, :], ACT.Copy).then_inc(ht_ready, 1)
                    else:
                        nc.scalar.activation(dst[:, c, :], psum[:, 6 + c, :], ACT.Identity,
                                             scale=col(scale, c)).then_inc(ht_ready, 1)
                turns[0] += 1

            def signal(ins, name):
                ins.then_inc(on[name], 1)

            copy_turned(HTC)
            root()
            root()
            copy_turned(HTC, "norm_w")
            act.wait_ge(on["c_habm"], 1)
            signal(nc.scalar.activation(WHABM, psum[:, 4, 0:256], ACT.Copy), "c_habm_copied")
            act.wait_ge(on["c_padded"], 2)
            for j in range(8):
                act.wait_ge(on["c_in"], j + 1)
                if j < IT:
                    signal(nc.scalar.activation(VAL[:, j, :, 4:S + 4],
                                                psum[:, j, :].rearrange("p (b n) -> p b n", b=B), ACT.Identity,
                                                bias=col("in_b", IT + j)), "c_in_copied")
                else:
                    signal(nc.scalar.activation(GATE[:, j - IT, :], psum[:, j, :], ACT.Sigmoid,
                                                bias=col("in_b", j - IT)), "c_in_copied")
            act.wait_ge(on["c_a"], 1)
            signal(nc.scalar.activation(ABIAS[0:DS, :], psum[0:DS, 1, 0:1], ACT.Copy), "c_a_copied")
            act.wait_ge(on["c_a_copied"], 1)
            act.wait_ge(on["c_a"], 2)
            signal(nc.scalar.activation(AS, psum[:, 0, :], ACT.Identity, bias=ABIAS), "c_a_copied")
            for m in range(2):
                act.wait_ge(on["c_ha"], m + 1)
                signal(nc.scalar.activation(YC[:, m, :], psum[:, 5 + m, :], ACT.Identity,
                                            bias=col("ha_b", m)), "c_ha_copied")

            def sigmoids(pair):
                for m in (2 * pair, 2 * pair + 1):
                    act.wait_ge(on["c_conv_b"], 2 * TAPS_B * pair + 2 * (TAPS_B - 1) + m % 2 + 1)
                    signal(nc.scalar.activation(SB[:, m, :], CB[:, m, :], ACT.Sigmoid), "c_sigmoid")

            sigmoids(0)
            for m in range(IT):
                act.wait_ge(on["c_hbpw"], 2 * (m // 2) + 2)
                signal(nc.scalar.activation(WHBPW[:, m, :], psum[:, 2 + m // 2, m % 2 * 256:(m % 2 + 1) * 256],
                                            ACT.Copy), "c_hbpw_copied")
            act.wait_ge(on["c_hbpw"], IT + 1)
            for m in range(2):
                signal(nc.scalar.activation(HBBIAS[:, m:m + 1], psum[:, 1, 2 + m:3 + m], ACT.Identity,
                                            bias=col("hb_b", m)), "c_hbpw_copied")
            sigmoids(1)
            act.wait_ge(on["c_hbpw_copied"], IT + 2)
            for m in range(2):
                act.wait_ge(on["c_hb"], m + 1)
                signal(nc.scalar.activation(YC[:, 2 + m, :], psum[:, m, :], ACT.Identity,
                                            bias=HBBIAS[:, m:m + 1]), "c_hb_copied")
            root()
            for c in range(CT):
                act.wait_ge(on["d_turned"], c + 1)
                signal(nc.scalar.activation(HQT[:, c, :], psum[:, 6 + c, 0:256].bitcast(BF16), ACT.Copy),
                       "d_turned_copied")
            for n in range(8):
                act.wait_ge(on["d_hidden"], n + 1)
                part = UH[:, n // 2, n % 2 * 512:(n % 2 + 1) * 512]
                signal(nc.scalar.activation(part, part, ACT.Gelu), "d_gelu")
            root()
            act.wait_ge(on["d_means"], 1)
            for i in range(1, TT):
                signal(nc.scalar.activation(UH[:, i, :], UH[:, i, :], ACT.Identity, scale=SD[:, 4 + i:5 + i],
                                            bias=NEGM[:, i:i + 1]), "d_centred")
            for i in range(TT):
                act.wait_ge(on["d_turned2"], i + 1)
                signal(nc.scalar.activation(QHT[:, :, i * P:(i + 1) * P],
                                            psum[:, 4 + i, :].bitcast(BF16).rearrange("p (k n) -> p k n", k=FT),
                                            ACT.Copy), "d_turned2_copied")
            root()
            copy_turned(HTE)
            for f in range(CT):
                act.wait_ge(on["e_q"], f + 1)
                signal(nc.scalar.activation(QE[:, f, :], psum[:, f, :], ACT.Identity, bias=col("bq1", f)),
                       "e_q_copied")
            for c in range(CT):
                act.wait_ge(on["e_qc"], c + 1)
                signal(nc.scalar.activation(QC[:, c, :], psum[:, 2 + c, :], ACT.Copy, scale=D ** -0.5),
                       "e_qc_copied")
            for w in range(4):
                act.wait_ge(on["e_bias"], w + 1)
                signal(nc.scalar.activation(PE1[w % 2], PE1[w % 2], ACT.Exp, bias=ENB[:, w:w + 1],
                                            accum_out=ESUM[:, w:w + 1]), "e_exp")
                for n in range(0, 8, 2):
                    act.wait_ge(on["e_turned"], 8 * w + n + 1)
                    if w:
                        act.wait_ge(on["e_att"], w)
                    signal(nc.scalar.activation(PT1[:, n * 512:(n + 1) * 512], psum[:, 4, :], ACT.Copy),
                           "e_turned_a")
            copy_turned(HTE)
            root()
            copy_turned(HTF)
            for n in range(16):
                act.wait_ge(on["f_turned"], n + 1)
                dst = QT if n < 8 else KT
                signal(nc.scalar.activation(dst[:, n % 8, :], psum[:, n % 8, :], ACT.Copy), "f_turned_copied")
            def head_exps(n):
                act.wait_ge(on["f_bias"], n + 1)
                if n >= 4:
                    act.wait_ge(on["f_pt"], n - 3)
                src = PM[n % 4] if causal_head(n) else HEAD_SCORES[n % 4].rearrange("p (t n) -> p t n", t=2)
                for qt in range(2):
                    seen = keys(n, qt)
                    signal(nc.scalar.activation(PM[n % 4][:, qt, 0:seen], src[:, qt, 0:seen], ACT.Exp, scale=DM ** -0.5,
                                                bias=FNB[:, 2 * n + qt:2 * n + qt + 1],
                                                accum_out=FSUM[:, 2 * n + qt:2 * n + qt + 1]), "f_exp")

            act.wait_ge(on["f_roped"], 16)
            head_exps(0)
            head_exps(1)
            for n in range(8):
                act.wait_ge(on["f_qkv"], 16 + n + 1)
                signal(nc.scalar.activation(VTM[:, n // 2, n % 2 * HALF:(n % 2 + 1) * HALF], psum[:, VALUE_BANKS[n % 5], :],
                                            ACT.Copy), "f_v_copied")
            for n in range(32):
                if n + 2 < 32:
                    head_exps(n + 2)
                act.wait_ge(on["f_pt"], n + 1)
                if n >= 4:
                    act.wait_ge(on["f_pv"], (n - 4) // 2 + 1)
                width = keys(n, 0) + keys(n, 1)
                signal(nc.scalar.activation(PTM[n % 4][:, 0:width], psum[:, 2 + n % 2, 0:width], ACT.Copy),
                       "f_pt_copied")
            root()
            copy_turned(HTF)
            act.wait_ge(on["g_logits"], 2)
            signal(nc.scalar.activation(R1[3], R1[2], ACT.Exp), "g_logits")
            for c in range(CT):
                act.wait_ge(on["g_xg"], c + 1)
                signal(nc.scalar.activation(XG[:, c, :], psum[:, 2 + c, :], ACT.Copy), "g_xg_copied")
            for m in range(IT):
                act.wait_ge(on["g_up"], m + 1)
                signal(nc.scalar.activation(INTER[:, m, :], psum[:, 4 + m, :], ACT.Relu), "g_up_copied")
            for k in range(4):
                act.wait_ge(on["g_down"], k + 1)
                signal(nc.scalar.activation(OE[:, k, :], psum[:, k, 0:256], ACT.Copy), "g_down_copied")

        @block.vector
        def _(dve):
            dve.wait_ge(x_loaded, 16)
            for i in range(TT):
                nc.vector.bn_stats(BN[:, 6 * i:6 * i + 6], X[:, i, :]).then_inc(ln_step, 1)
            dve.wait_ge(ln_step, TT)
            for i in range(TT):
                nc.vector.bn_aggr(MV[:, 2 * i:2 * i + 2], BN[:, 6 * i:6 * i + 6]).then_inc(ln_step, 1)
            dve.wait_ge(ln_step, 2 * TT)
            mean = MV.rearrange("p (t two) -> p t two", two=2)
            nc.vector.tensor_scalar(SD[:, 4:8], mean[:, :, 1], 1e-5, None, ALU.add).then_inc(ln_var, 1)
            dve.wait_ge(ln_sd, 1)
            nc.vector.reciprocal(SD[:, 4:8], SD[:, 0:4]).then_inc(ln_step, 1)
            dve.wait_ge(ln_step, 2 * TT + 1)
            for i in range(TT):
                nc.vector.tensor_scalar(HN[:, i, :], X[:, i, :], MV[:, 2 * i:2 * i + 1], SD[:, 4 + i:5 + i],
                                        ALU.subtract, ALU.mult).then_inc(h_ready, 1)
            dve.wait_ge(cols_loaded, 32)
            for f in range(CT):
                n = 4 * f
                dve.wait_ge(q_psum, f + 1)
                nc.vector.tensor_scalar(K32[f], psum[:, f, :], COLT[:, COL_AT["bq"] + f:COL_AT["bq"] + f + 1],
                                        DH ** -0.5, ALU.add, ALU.mult).then_inc(q_split, 1)
                dve.wait_ge(q_split, n + 1)
                nc.vector.tensor_copy(KPT[f][:, 0, :], K32[f]).then_inc(q_split, 1)
                dve.wait_ge(q_split, n + 2)
                nc.vector.tensor_tensor(K32[f], K32[f], KPT[f][:, 0, :], ALU.subtract).then_inc(q_split, 1)
                dve.wait_ge(q_split, n + 3)
                nc.vector.tensor_copy(KPT[f][:, 1, :], K32[f]).then_inc(q_split, 1)
                dve.wait_ge(q_split, n + 4)
                nc.vector.tensor_tensor(KPT[f][:, 2, :], K32[f], KPT[f][:, 1, :], ALU.subtract)\
                  .then_inc(q_ready, 1)

            def split_k(piece, f, middle=True):
                dve.wait_ge(k_copied, 2 * piece + 2)
                nc.vector.tensor_tensor(K32[f], K32[f], KPT[f][:, 0, :], ALU.subtract).then_inc(k_rest, 1)
                if middle:
                    dve.wait_ge(k_rest, piece + 1)
                    nc.vector.tensor_copy(KPT[f][:, 1, :], K32[f]).then_inc(k_middle, 1)

            def maxes(n, col, mx, chunks=range(8)):
                for c in chunks:
                    dve.wait_ge(s_ready, n + (c + 1))
                    nc.vector.tensor_reduce(mx[:, bass.ds(col + c, 1)], SP_(c % 2), AX.X, ALU.max)\
                      .then_inc(s_maxed, 1)

            with dve.Fori(0, NCH // 2) as i:
                for f in range(CT):
                    split_k(2 * i + f, f)
            dve.wait_ge(mask_loaded, 16)
            with dve.Fori(0, NCH // 2) as i:
                for f in range(CT):
                    split_k(2 * i + f + NCH, f)
                    part = MASKB[:, f, bass.ds(i * 2 * CH, 2 * CH)]
                    nc.vector.tensor_scalar(part, MASKI[:, f, bass.ds(i * 2 * CH, 2 * CH)], 0.0, MASKED,
                                            ALU.is_equal, ALU.mult).then_inc(mask_step, 1)
                    dve.wait_ge(mask_step, 4 * i + (2 * f + 1))
                    nc.vector.tensor_reduce(MX[1][:, bass.ds(2 * i + f, 1)], part, AX.X, ALU.min).then_inc(mask_step, 1)
            dve.wait_ge(mask_step, 2 * NCH)
            nc.vector.tensor_reduce(FLAGF[:, 0:1], MX[1][:, 0:NCH], AX.X, ALU.min).then_inc(mask_step, 1)
            dve.wait_ge(mask_step, 2 * NCH + 1)
            nc.vector.tensor_scalar(FLAGF[:, 1:2], FLAGF[:, 0:1], 0.0, None, ALU.is_lt).then_inc(mask_step, 1)
            dve.wait_ge(mask_counted, 1)
            nc.vector.tensor_scalar(FLAG, psum[0:1, 5, 0:1], 0.0, None, ALU.is_gt).then_inc(mask_flagged, 1)
            def second_batch(i, first):
                maxes(8 * i, 8 * i, MX[0], range(2))
                if not first:
                    split_k(2 * i + 15, 1, False)
                maxes(8 * i, 8 * i, MX[0], range(2, 6))
                split_k(2 * i + 16, 0, False)
                maxes(8 * i, 8 * i, MX[0], range(6, 8))

            second_batch(0, True)
            with dve.Fori(1, NCH) as i:
                second_batch(i, False)
            split_k(4 * NCH - 1, 1, False)

            def split_max(gg):
                n = 4 * gg

                def between(c):
                    if gg + 1 < NG:
                        maxes(64 * (gg + 1), 0, MX[(gg + 1) % 2], (c,))
                dve.wait_ge(s_maxed, 64 * (gg + 1))
                nc.vector.tensor_reduce(M8, MX[gg % 2].rearrange("p (m c) -> p m c", c=8), AX.X, ALU.max)\
                  .then_inc(m_step, 1)
                between(0)
                if gg:
                    dve.wait_ge(m_turned, 2 * gg)
                dve.wait_ge(m_step, n + 1)
                nc.vector.tensor_scalar(MPART[:, :, 0], M8, -1.0, None, ALU.mult).then_inc(m_step, 1)
                between(1)
                dve.wait_ge(m_step, n + 2)
                nc.vector.scalar_tensor_tensor(out=MR, in0=M8, scalar=-1.0, in1=MPART[:, :, 0],
                                               op0=ALU.mult, op1=ALU.subtract).then_inc(m_step, 1)
                between(2)
                dve.wait_ge(m_step, n + 3)
                nc.vector.tensor_copy(MPART[:, :, 1], MR).then_inc(m_step, 1)
                between(3)
                dve.wait_ge(m_step, n + 4)
                nc.vector.tensor_tensor(MPART[:, :, 2], MR, MPART[:, :, 1], ALU.subtract).then_inc(m_split, 1)
                if gg + 1 < NG:
                    maxes(64 * (gg + 1), 0, MX[(gg + 1) % 2], range(4, 8))
                    maxes(64 * (gg + 1) + 8, 8, MX[(gg + 1) % 2])

            def normalise(gg):
                b, g = gg // GPB, gg % GPB
                n = 3 * gg
                dve.wait_ge(pv_turned, gg + 1)
                turned = PX[:, 0:256].rearrange("p (t j e) -> p t j e", t=2, j=G)
                nc.vector.reciprocal(RINV, turned[:, :, :, DH]).then_inc(norm_step, 1)
                dve.wait_ge(norm_step, n + 1)
                out = CTXN[:, 2 * b:2 * b + 2, G * DH * g:G * DH * (g + 1)].rearrange("p t (j d) -> p t j d", j=G)
                nc.vector.tensor_tensor(out, turned[:, :, :, 0:DH],
                                        RINV.unsqueeze(3).broadcast_to((P, 2, G, DH)), ALU.mult)\
                  .then_inc(norm_step, 1)
                dve.wait_ge(norm_step, n + 2)
                flat = CTXN[:, 2 * b:2 * b + 2, G * DH * g:G * DH * (g + 1)]
                bv = BV[:, G * DH * g:G * DH * (g + 1)].unsqueeze(1).broadcast_to((P, 2, G * DH))
                nc.vector.tensor_tensor(flat, flat, bv, ALU.add).then_inc(norm_step, 1)

            steps = [0]

            def mark(ins):
                ins.then_inc(on["step_v"], 1)
                steps[0] += 1

            def done():
                dve.wait_ge(on["step_v"], steps[0])

            def quantise_weights():
                dve.wait_ge(on["raw_loaded"], 32)
                for n, w in enumerate((W1RAW, W2RAW)):
                    nc.vector.tensor_reduce(WSUM[:, n:n + 1], w, AX.X, ALU.add, apply_absolute_value=True)\
                      .then_inc(on["w_summed"], 1)
                dve.wait_ge(st_ready, (NG - 1) * KC)
                dve.wait_ge(on["w_total"], 1)
                mark(nc.vector.tensor_scalar(WMEAN, psum[:, 4, 0:2], 1.0 / (D * FF), 1e-5, ALU.mult, ALU.max))
                done()
                mark(nc.vector.reciprocal(WSC, WMEAN))
                done()
                for n, (w, tw) in enumerate(((W1RAW, TW1), (W2RAW, TW2))):
                    flat = tw.rearrange("p a b -> p (a b)")
                    signal = on["w_quantised"]
                    nc.vector.tensor_scalar(w, w, WSC[:, n:n + 1], ROUND, ALU.mult, ALU.add).then_inc(signal, 1)
                    dve.wait_ge(signal, 3 * n + 1)
                    nc.vector.tensor_scalar(w, w, ROUND, 1.0, ALU.subtract, ALU.min).then_inc(signal, 1)
                    dve.wait_ge(signal, 3 * n + 2)
                    nc.vector.tensor_scalar(flat, w, -1.0, None, ALU.max).then_inc(signal, 1)

            split_max(0)
            for gg in range(NG):
                if gg + 1 < NG:
                    mx = MX[(gg + 1) % 2]
                    n = 64 * (gg + 1) + 16
                    maxes(n, 16, mx)
                    if gg:
                        normalise(gg - 1)
                    maxes(n + 8, 24, mx)
                    with dve.Fori(1, KC // 8 - 1) as i:
                        maxes(16 * i + n, 16 * i + 16, mx)
                        maxes(16 * i + (n + 8), 16 * i + 24, mx)
                    split_max(gg + 1)
                else:
                    normalise(gg - 1)
                    quantise_weights()
            normalise(NG - 1)


            roots = [1]

            def root():
                roots[0] += 1
                dve.wait_ge(ln_sd, roots[0])
                mark(nc.vector.reciprocal(SD[:, 4:8], SD[:, 0:4]))
                done()

            def deviation(factor=1.0, eps=1e-5):
                if factor == 1.0:
                    ins = nc.vector.tensor_scalar(SD[:, 4:8], mean[:, :, 1], eps, None, ALU.add)
                else:
                    ins = nc.vector.tensor_scalar(SD[:, 4:8], mean[:, :, 1], factor, eps, ALU.mult, ALU.add)
                ins.then_inc(ln_var, 1)
                root()

            def aggregate(n):
                done()
                for i in range(TT):
                    mark(nc.vector.bn_aggr(MV[:, 2 * i:2 * i + 2], BN[:, 6 * n * i:6 * n * (i + 1)]))
                done()

            def add_to_x(name, n, add):
                for i in range(TT + 1):
                    if i < TT:
                        dve.wait_ge(on[name], i + 1)
                        x_ready(add(i))
                    if i:
                        dve.wait_ge(on["x_ready"], TT * n + i)
                        mark(nc.vector.bn_stats(BN[:, 6 * (i - 1):6 * i], X[:, i - 1, :]))
                aggregate(1)

            def centred(dst, src, i):
                return nc.vector.tensor_scalar(dst[:, i, :], src[:, i, :], MV[:, 2 * i:2 * i + 1],
                                               SD[:, 4 + i:5 + i], ALU.subtract, ALU.mult)

            def x_ready(ins):
                ins.then_inc(on["x_ready"], 1)

            add_to_x("b_out", 0, lambda i: nc.vector.tensor_tensor(X[:, i, :], X[:, i, :], psum[:, i, 0:256], ALU.add))
            deviation(1.0 + 1e-6, 1e-6 * 1e-5)
            for i in range(TT):
                centred(HS, X, i).then_inc(h_ready, 1)
            dve.wait_ge(h_ready, 2 * TT)
            deviation()
            for i in range(TT):
                mark(centred(HL, X, i))
            done()
            for i in range(TT):
                mark(nc.vector.tensor_tensor(X[:, i, :], X[:, i, :], HL[:, i, :], ALU.add))
            def silu(pair):
                for m in (2 * pair, 2 * pair + 1):
                    dve.wait_ge(on["c_sigmoid"], m + 1)
                    nc.vector.tensor_tensor(SB[:, m, :], SB[:, m, :], CB[:, m, :], ALU.mult).then_inc(on["c_silu"], 1)

            for pair in range(2):
                for k in range(TAPS_B):
                    for m in (2 * pair, 2 * pair + 1):
                        tap = col("sym_k", TAPS_B * m + k)
                        src = VAL[:, m, :, 4 + k - LEFT_B:4 + k - LEFT_B + S]
                        out = CB[:, m, :].rearrange("p (b n) -> p b n", b=B)
                        if k == 0:
                            dve.wait_ge(on["c_in_copied"], m + 1)
                            nc.vector.tensor_scalar(out, src, tap, col("sym_b", m), ALU.mult, ALU.add)\
                              .then_inc(on["c_conv_b"], 1)
                        else:
                            dve.wait_ge(on["c_conv_b"], 2 * TAPS_B * pair + 2 * (k - 1) + m % 2 + 1)
                            nc.vector.scalar_tensor_tensor(out=out, in0=src, scalar=tap, in1=out,
                                                           op0=ALU.mult, op1=ALU.add)\
                              .then_inc(on["c_conv_b"], 1)
                    if pair == 1 and k == 2:
                        silu(0)
            silu(1)
            for m in range(IT):
                dve.wait_ge(on["c_fuse"], m + 1)
                nc.vector.scalar_tensor_tensor(out=YG[:, m, :], in0=psum[:, m, :], scalar=col("fuse_b", m),
                                               in1=GATE[:, m, :], op0=ALU.add, op1=ALU.mult)\
                  .then_inc(on["c_gated"], 1)
            add_to_x("c_out", 1, lambda i: nc.vector.tensor_tensor(X[:, i, :], X[:, i, :], psum[:, 4 + i, 0:256],
                                                                   ALU.add))

            def quantise_scale(src, tiles, per_row):
                mark(nc.vector.tensor_reduce(AMAX[:, tiles], src[:, tiles, :], AX.X, ALU.max,
                                             apply_absolute_value=True))
                done()
                mark(nc.vector.tensor_scalar(AMAX[:, tiles], AMAX[:, tiles], 1e-5, 1.0 / 127.0, ALU.max, ALU.mult))
                done()
                mark(nc.vector.reciprocal(QSC[:, tiles], AMAX[:, tiles]))
                mark(nc.vector.tensor_scalar(OSC[:, tiles], AMAX[:, tiles], per_row, None, ALU.mult))
                done()

            def rounded(src, i):
                return nc.vector.tensor_scalar(src[:, i, :], src[:, i, :], QSC[:, i:i + 1], ROUND, ALU.mult, ALU.add)

            def clipped(dst, src, i):
                return nc.vector.tensor_scalar(dst[:, i, :], src[:, i, :], ROUND, 127.0, ALU.subtract, ALU.min)

            def gained(dst, src, i, g):
                return nc.vector.scalar_tensor_tensor(out=dst[:, i, :], in0=src[:, i, :],
                                                      scalar=MV[:, 2 * i:2 * i + 1], in1=row(g),
                                                      op0=ALU.subtract, op1=ALU.mult)

            def shifted(src, i, b):
                return nc.vector.scalar_tensor_tensor(out=src[:, i, :], in0=src[:, i, :],
                                                      scalar=SD[:, 4 + i:5 + i], in1=row(b),
                                                      op0=ALU.mult, op1=ALU.add)

            deviation(1.0 + 1e-5, 1e-5 * 1e-5)
            dve.wait_ge(on["rows_loaded"], 16)
            for i in range(TT):
                mark(gained(HL, X, i, "g1"))
            done()
            for i in range(TT):
                mark(shifted(HL, i, "b1"))
            done()
            quantise_scale(HL, slice(0, TT), WMEAN[:, 0:1])
            for i in range(TT):
                mark(rounded(HL, i))
            done()
            for i in range(TT):
                mark(clipped(HQ, HL, i))
            done()
            for i in range(TT):
                nc.vector.tensor_scalar(HQ[:, i, :], HQ[:, i, :], -128.0, None, ALU.max).then_inc(on["d_quant"], 1)
            for n in range(8):
                i, half = n // 2, n % 2
                dve.wait_ge(on["d_up"], n + 1)
                nc.vector.scalar_tensor_tensor(out=UH[:, i, half * 512:(half + 1) * 512], in0=psum[:, n, :],
                                               scalar=OSC[:, i:i + 1], in1=row("w1b")[:, half * 512:(half + 1) * 512],
                                               op0=ALU.mult, op1=ALU.add).then_inc(on["d_hidden"], 1)
            for i in range(TT):
                mark(nc.vector.tensor_tensor(X[:, i, :], X[:, i, :], row("w2b"), ALU.add))
            for n in range(8):
                dve.wait_ge(on["d_gelu"], n + 1)
                mark(nc.vector.bn_stats(BN[:, 6 * n:6 * (n + 1)], UH[:, n // 2, n % 2 * 512:(n % 2 + 1) * 512]))
            aggregate(2)
            deviation()
            nc.vector.scalar_tensor_tensor(out=NEGM, in0=mean[:, :, 0], scalar=-1.0, in1=SD[:, 4:8],
                                           op0=ALU.mult, op1=ALU.mult).then_inc(on["d_means"], 1)

            for i in range(TT):
                if i == 0:
                    mark(gained(UH, UH, i, "g2"))
                    done()
                    mark(shifted(UH, i, "b2"))
                else:
                    dve.wait_ge(on["d_gained"], i)
                    mark(nc.vector.tensor_tensor(UH[:, i, :], UH[:, i, :], row("b2"), ALU.add))
                done()
                quantise_scale(UH, slice(i, i + 1), WMEAN[:, 1:2])
                mark(rounded(UH, i))
                done()
                mark(clipped(QH, UH, i))
                done()
                nc.vector.tensor_scalar(QH[:, i, :], QH[:, i, :], -128.0, None, ALU.max).then_inc(on["d_quant2"], 1)
            add_to_x("d_down", 2, lambda i: nc.vector.scalar_tensor_tensor(
                out=X[:, i, :], in0=psum[:, i, 0:256], scalar=OSC[:, i:i + 1], in1=X[:, i, :],
                op0=ALU.mult, op1=ALU.add))

            deviation()
            for i in range(TT):
                centred(HLE, X, i).then_inc(h_ready, 1)
            dve.wait_ge(on["e_cq"], 1)
            nc.vector.tensor_scalar(CQ, psum[:, 4, 0:4], D ** -0.5, None, ALU.mult).then_inc(on["e_cq_copied"], 1)
            dve.wait_ge(on["e_cq_copied"], 1)

            def mask_scores(w):
                for n in range(8):
                    half = n // 4
                    if n % 4 == 0:
                        dve.wait_ge(on[f"mask1_loaded{half}"], 16 * (w + 1))
                    dve.wait_ge(on["e_scores"], 8 * w + n + 1)
                    if w >= 2:
                        dve.wait_ge(on["e_turned"], 8 * (w - 1))
                    nc.vector.tensor_tensor_reduce(PE1[w % 2][:, n * 512:(n + 1) * 512], psum[:, n % 4, :],
                                                   MRING[half][:, n % 4 * 512:(n % 4 + 1) * 512], 1.0, -3.0e38,
                                                   ALU.add, ALU.max, EMX[:, 8 * w + n:8 * w + n + 1])\
                      .then_inc(on["e_masked"], 1)
                dve.wait_ge(on["e_masked"], 8 * (w + 1))
                one = slice(w, w + 1)
                mark(nc.vector.tensor_reduce(EM[:, one], EMX[:, 8 * w:8 * w + 8], AX.X, ALU.max))
                done()
                mark(nc.vector.tensor_tensor(ET[:, one], EM[:, one], CQ[:, one], ALU.add))
                done()
                nc.vector.tensor_tensor(ENB[:, one], CQ[:, one], ET[:, one], ALU.subtract).then_inc(on["e_bias"], 1)

            def copy_exps(w):
                for n in range(1, 8, 2):
                    dve.wait_ge(on["e_turned"], 8 * w + n + 1)
                    if w:
                        dve.wait_ge(on["e_att"], w)
                    nc.vector.tensor_copy(PT1[:, n * 512:(n + 1) * 512], psum[:, 5, :]).then_inc(on["e_turned_v"], 1)

            def norm_att(w):
                dve.wait_ge(on["e_exp"], w + 1)
                mark(nc.vector.reciprocal(ERI[:, w:w + 1], ESUM[:, w:w + 1]))
                done()
                dve.wait_ge(on["e_att"], w + 1)
                nc.vector.tensor_scalar(AO[:, w, :], psum[:, 6, 0:256], ERI[:, w:w + 1], None, ALU.mult)\
                  .then_inc(on["e_normed"], 1)

            mask_scores(0)
            for w in range(4):
                if w < 3:
                    mask_scores(w + 1)
                copy_exps(w)
                norm_att(w)
            add_to_x("e_out", 3, lambda i: nc.vector.tensor_tensor(X[:, i, :], X[:, i, :], psum[:, i, 0:256], ALU.add))

            deviation()
            for i in range(TT):
                centred(HLE, X, i).then_inc(h_ready, 1)
            dve.wait_ge(on["const_loaded"], 16)
            cos = const("cos").rearrange("p (t d) -> p t d", t=2)
            sin = const("sin").rearrange("p (t d) -> p t d", t=2)
            for piece in range(16):
                which, i, half = piece // 8, piece % 8 // 2, piece % 2
                dve.wait_ge(on["f_qkv"], piece + 1)
                if piece >= 2:
                    dve.wait_ge(on["f_roped"], piece - 1)
                src = psum[:, piece % 8, :].rearrange("p (h d) -> p h d", h=8)
                out = (KTM if which else QTM)[:, i, half * HALF:(half + 1) * HALF]\
                    .rearrange("p (h d) -> p h d", h=8)
                c = cos[:, i % 2, :].unsqueeze(1).broadcast_to((P, 8, DM))
                lo = sin[:, i % 2, 0:DM // 2].unsqueeze(1).broadcast_to((P, 8, DM // 2))
                hi = sin[:, i % 2, DM // 2:DM].unsqueeze(1).broadcast_to((P, 8, DM // 2))
                part = on["f_rope_part"]
                nc.vector.tensor_tensor(T2[piece % 2][:, :, 0:DM // 2], src[:, :, DM // 2:DM], lo, ALU.mult)\
                  .then_inc(part, 1)
                nc.vector.tensor_tensor(T2[piece % 2][:, :, DM // 2:DM], src[:, :, 0:DM // 2], hi, ALU.mult)\
                  .then_inc(part, 1)
                nc.vector.tensor_tensor(out, src, c, ALU.mult).then_inc(part, 1)
            causal = const("causal").rearrange("p (t n) -> p t n", t=2)

            def row_maxima(n):
                dve.wait_ge(on["f_scores"], n + 1)
                src = HEAD_SCORES[n % 4].rearrange("p (t n) -> p t n", t=2)
                if causal_head(n):
                    if n >= 4:
                        dve.wait_ge(on["f_pt"], n - 3)
                    for qt in range(2):
                        seen = keys(n, qt)
                        mark(nc.vector.tensor_tensor_reduce(PM[n % 4][:, qt, 0:seen], src[:, qt, 0:seen],
                                                            causal[:, qt, 0:seen],
                                                            1.0, -3.0e38, ALU.add, ALU.max,
                                                            FMX[:, 2 * n + qt:2 * n + qt + 1]))
                else:
                    mark(nc.vector.tensor_reduce(FMX[:, 2 * n:2 * n + 2], src, AX.X, ALU.max))
                done()
                nc.vector.tensor_scalar(FNB[:, 2 * n:2 * n + 2], FMX[:, 2 * n:2 * n + 2], -(DM ** -0.5), None,
                                        ALU.mult).then_inc(on["f_bias"], 1)

            def scale_exps(n):
                dve.wait_ge(on["f_exp"], 2 * (n + 1))
                mark(nc.vector.reciprocal(FRI[:, 2 * n:2 * n + 2], FSUM[:, 2 * n:2 * n + 2]))
                done()
                for qt in range(2):
                    part = PM[n % 4][:, qt, 0:keys(n, qt)]
                    nc.vector.tensor_scalar(part, part,
                                            FRI[:, 2 * n + qt:2 * n + qt + 1], None, ALU.mult)\
                      .then_inc(on["f_scaled"], 1)

            def copy_contexts(pair):
                b, k = pair // 8, pair % 8
                dve.wait_ge(on["f_pv"], pair + 1)
                nc.vector.tensor_copy(OT[:, k, b * S:(b + 1) * S], psum[:, 4 + pair % 2, 0:S])\
                  .then_inc(on["f_pv_copied"], 1)

            for n in range(3):
                row_maxima(n)
            scale_exps(0)
            for n in range(32):
                if n + 1 < 32:
                    scale_exps(n + 1)
                if n + 3 < 32:
                    row_maxima(n + 3)
                if n % 2 == 0 and n > 2:
                    copy_contexts((n - 4) // 2)
            copy_contexts(14)
            copy_contexts(15)
            add_to_x("f_out", 4, lambda i: nc.vector.tensor_tensor(X[:, i, :], X[:, i, :], psum[:, i, 0:256], ALU.add))

            deviation()
            for i in range(TT):
                centred(HLE, X, i).then_inc(h_ready, 1)
            dve.wait_ge(on["g_logits"], 1)
            logits, hot1, hot2, weights, chosen, slot, pick = R[0], R[1], R[2], R[3], R[4], R[5], R[6]
            best1, best2, gap, egap, den, share1, share2 = R1[0], R1[1], R1[2], R1[3], R1[4], R1[5], R1[6]
            less8 = const("experts").unsqueeze(1).broadcast_to((P, TT, E))

            def over_e(ap):
                return ap.unsqueeze(2).broadcast_to((P, TT, E))

            mark(nc.vector.tensor_copy(logits, psum[:, 0, 0:TT * E].rearrange("p (t e) -> p t e", t=TT)))
            done()
            for best, hot in ((best1, hot1), (best2, hot2)):
                mark(nc.vector.tensor_reduce(best, logits, AX.X, ALU.max))
                done()
                mark(nc.vector.tensor_tensor(pick, logits, over_e(best), ALU.is_equal))
                done()
                mark(nc.vector.tensor_tensor(pick, pick, less8, ALU.mult))
                done()
                mark(nc.vector.tensor_reduce(R1[7], pick, AX.X, ALU.min))
                done()
                mark(nc.vector.tensor_tensor(hot, less8, over_e(R1[7]), ALU.is_equal))
                done()
                if best is best1:
                    mark(nc.vector.scalar_tensor_tensor(out=logits, in0=hot, scalar=-3.0e38, in1=logits,
                                                        op0=ALU.mult, op1=ALU.add))
                    done()
            nc.vector.tensor_tensor(gap, best2, best1, ALU.subtract).then_inc(on["g_logits"], 1)
            dve.wait_ge(on["g_logits"], 3)
            mark(nc.vector.tensor_scalar(den, egap, 1.0, None, ALU.add))
            done()
            mark(nc.vector.reciprocal(share1, den))
            done()
            mark(nc.vector.tensor_tensor(share2, egap, share1, ALU.mult))
            done()
            mark(nc.vector.tensor_tensor(hot1, hot1, over_e(share1), ALU.mult))
            mark(nc.vector.tensor_tensor(hot2, hot2, over_e(share2), ALU.mult))
            done()
            mark(nc.vector.tensor_tensor(weights, hot1, hot2, ALU.add))
            done()
            nc.vector.tensor_scalar(CHOSENB, weights, 0.0, None, ALU.is_gt).then_inc(on["g_chosen"], 1)
            mark(nc.vector.tensor_scalar(chosen, weights, 0.0, None, ALU.is_gt))
            done()
            dve.wait_ge(on["g_cum"], 1)
            cum = psum[:, 1, 0:TT * E].rearrange("p (t e) -> p t e", t=TT)
            mark(nc.vector.scalar_tensor_tensor(out=slot, in0=cum, scalar=float(CAP), in1=chosen,
                                                op0=ALU.is_le, op1=ALU.mult))
            done()
            mark(nc.vector.tensor_tensor(slot, slot, cum, ALU.mult))
            done()
            for i in range(TT):
                nc.vector.tensor_tensor(SEL[:, i], slot[:, i, :].unsqueeze(2).broadcast_to((P, E, CAP)),
                                        const("slots").unsqueeze(1).broadcast_to((P, E, CAP)), ALU.is_equal)\
                  .then_inc(on["g_sel"], 1)
            for i in range(TT):
                dve.wait_ge(on["g_sel"], i + 1)
                nc.vector.tensor_tensor(SELW[:, i], SEL[:, i],
                                        weights[:, i, :].unsqueeze(2).broadcast_to((P, E, CAP)), ALU.mult)\
                  .then_inc(on["g_selw"], 1)
            for k in range(4):
                dve.wait_ge(on["g_selt"], k + 1)
                nc.vector.tensor_copy(SELT[:, k, :], psum[:, [0, 1, 0, 1][k], :]).then_inc(on["g_selt_copied"], 1)
            for i in range(TT):
                dve.wait_ge(on["g_out"], i + 1)
                x_ready(nc.vector.tensor_tensor(X[:, i, :], X[:, i, :], psum[:, 4 + i, 0:256], ALU.add))

        @block.tensor
        def _(pe):
            pe.wait_ge(ident_built, 4)
            for c in range(CT):
                for i in range(TT):
                    pe.wait_ge(h_ready, i + 1)
                    last = nc.tensor.transpose(psum[:, 6 + c, i * P:(i + 1) * P], HN[:, i, c * P:(c + 1) * P],
                                               IDENT)
                last.then_inc(ht_psum, 1)
            pe.wait_ge(wq_loaded, 16)
            pe.wait_ge(ht_ready, CT)
            for f in range(CT):
                for c in range(CT):
                    last = nc.tensor.matmul(psum[:, f, :], WQ[:, c, f * P:(f + 1) * P], HT[:, c, :],
                                            start=(c == 0), stop=(c == CT - 1))
                last.then_inc(q_psum, 1)
            pe.wait_ge(wkv_loaded, 32)
            pe.wait_ge(q_ready, CT)

            def project_k(piece, f, slot, first=False, cs=range(CT)):
                if not first and 0 in cs:
                    pe.wait_ge(k_copied, 2 * piece - 2)
                for c in cs:
                    last = nc.tensor.matmul(psum[:, f, :], WK[:, c, f * P:(f + 1) * P], CTX[slot][:, c, :],
                                            start=(c == 0), stop=(c == CT - 1), skip_group_check=True)
                if CT - 1 in cs:
                    last.then_inc(k_psum, 1)

            def project_v(tile, v, bank, slot, banks, first=False):
                if not first:
                    pe.wait_ge(v_copied, tile + (1 - banks))
                for c in range(CT):
                    last = nc.tensor.matmul(psum[:, bank, 0:256], CTX[slot][:, c, v * P:(v + 1) * P],
                                            WV[:, c, :], start=(c == 0), stop=(c == CT - 1))
                last.then_inc(v_psum, 1)

            def scores(n, masked, slot, qh, jh, qt, c, b, first=False):
                if not first:
                    pe.wait_ge(s_maxed, n - 1)
                q = QST[0:ROWS, bass.ds(qh, 1), b * S + qt * P:b * S + (qt + 1) * P]
                k = KST[slot][0:ROWS, bass.ds(jh, 1), c * CH:(c + 1) * CH]
                last = nc.tensor.matmul(SP_(c % 2), q, k, start=True, stop=not masked, skip_group_check=True)
                if masked:
                    last = nc.tensor.matmul(SP_(c % 2), IDENTB, MASKB[:, qt, c * CH:(c + 1) * CH],
                                            start=False, stop=True, skip_group_check=True)
                last.then_inc(s_ready, 1)

            def turn_max(gg, pair):
                if pair == 0:
                    pe.wait_ge(m_split, gg + 1)
                    if gg > 1:
                        pe.wait_ge(norm_step, 3 * (gg - 1))
                else:
                    pe.wait_ge(m_stacked, 2 * gg + 1)
                for m in range(4):
                    last = nc.tensor.matmul(PX[ROWS:KROWS, m * P:(m + 1) * P], MPART[:, 4 * pair + m, :], IDENTB,
                                            start=True, stop=True)
                last.then_inc(m_turned, 1)

            def turned_scores(masked, slot, g, b, kc, u):
                for j in range(G):
                    last = nc.tensor.matmul(ST(u % 2)[:, j // 2, (j % 2) * S:(j % 2 + 1) * S],
                                            KST[slot][0:KROWS, j, bass.ds(kc * P, P)],
                                            QST[0:KROWS, G * g + j, b * S:(b + 1) * S],
                                            start=(j % 2 == 0), stop=not masked and j % 2 == 1,
                                            skip_group_check=True)
                if masked:
                    for bank in range(2):
                        for qt in range(2):
                            out = ST(u % 2)[:, bank, :].rearrange("p (j n) -> p j n", j=2)
                            last = nc.tensor.matmul(out[:, :, qt * P:(qt + 1) * P],
                                                    MASKB[:, qt, bass.ds(kc * P, P)],
                                                    IDENTB.unsqueeze(1).broadcast_to((P, 2, P)),
                                                    start=False, stop=qt == 1, skip_group_check=True)
                last.then_inc(st_ready, 1)

            def weigh_values(n, u, start, stop):
                pe.wait_ge(v_staged, n + 1)
                for j in range(G):
                    last = nc.tensor.matmul(PV[32 * j:32 * (j + 1), :],
                                            VS[u % 4][:, j * VW:j * VW + 32],
                                            PR[u % 2][:, j * S:(j + 1) * S], start=start, stop=stop,
                                            skip_group_check=True)
                last.then_inc(pv_done, 1)

            def first_batch():
                def chunk(i, u, first):
                    pe.wait_ge(ctx_loaded[u], 16 * i + 16)
                    for f in range(CT):
                        project_k(4 * i + (2 * u + f), f, u, first and u == 0)
                    for v in range(4):
                        project_v(8 * i + (4 * u + v), v, 2 + v % 2, u, 2, first and 4 * u + v < 2)
                for u in range(2):
                    chunk(0, u, True)
                with pe.Fori(1, NCH // 2) as i:
                    for u in range(2):
                        chunk(i, u, False)

            def second_batch(masked):
                pe.wait_ge(q_stacked, 96)
                def chunk(i, u, first):
                    pe.wait_ge(ctx_loaded[u], 16 * i + 16 * (NCH // 2 + 1))
                    for f in range(CT):
                        for c in range(CT):
                            project_k(4 * i + (2 * u + f + 16), f, u, cs=(c,))
                            if first and u == 0 and f == 0 and c == 0:
                                pe.wait_ge(k_stacked[0], STACK0)
                            for s in (4 * f + 2 * c, 4 * f + 2 * c + 1):
                                scores(16 * i + (8 * u + s), masked, 0, i, i, u, s, 0, first and u == 0 and s < 2)
                for u in range(2):
                    chunk(0, u, True)
                with pe.Fori(1, NCH // 2) as i:
                    for u in range(2):
                        chunk(i, u, False)

            def attend(masked):
                second_batch(masked)
                pe.wait_ge(k_stacked[1], 96)
                for c in range(16):
                    scores(64 + c, masked, 1, G, 0, c // 8, c % 8, 0)
                    if c in (5, 9):
                        turn_max(0, c // 9)
                pe.wait_ge(m_stacked, 2)
                pe.wait_ge(kones_built, 3)
                for gg in range(NG):
                    b, g, slot = gg // GPB, gg % GPB, gg % 3
                    n0 = KC * gg
                    if gg == GPB:
                        def chunk(i, u):
                            pe.wait_ge(ctx_loaded[u], 16 * i + 16 * (NCH + 1))
                            for v in range(4):
                                project_v(8 * i + (4 * u + v + KC), v, v, u, 4)
                        pe.wait_ge(exp_ready, KC * gg)
                        pe.wait_ge(v_copied, KC)
                        with pe.Fori(0, NCH // 2) as i:
                            for u in range(2):
                                chunk(i, u)
                        pe.wait_ge(v_copied, 2 * KC)
                    pe.wait_ge(m_stacked, 2 * gg + 2)
                    if gg == 2:
                        pe.wait_ge(kones_built, 11)

                    def ahead(i, last, s):
                        ng, j = (gg + 2, 0) if last else (gg + 1, i + 1)
                        if ng < NG:
                            scores(16 * i + (64 * (gg + 1) + 16 + s), masked, ng % 3, j + G * (ng % GPB), j,
                                   s // 8, s % 8, ng // GPB)

                    def steps(i, first, last=False):
                        if last and gg + 2 < NG:
                            times = 96 * ((gg + 2) // 3 + 1)
                            pe.wait_ge(k_stacked[(gg + 2) % 3], times if (gg + 2) % 3 else times - 96 + STACK0)
                        for u in range(8):
                            if n0 + u >= 2 or not first:
                                pe.wait_ge(exp_ready, 8 * i + (n0 + u - 1))
                            turned_scores(masked, slot, g, b, 8 * i + u, u)
                            ahead(i, last, 2 * u)
                            if first and u == 2 and gg:
                                pe.wait_ge(pv_copied, gg)
                                pe.wait_ge(m_stacked, 2 * gg + 2)
                                turn_context(gg - 1)
                            if last and u in (2, 5) and gg + 1 < NG:
                                turn_max(gg + 1, u // 4)
                            if u == 0 and first:
                                ahead(i, last, 2 * u + 1)
                                continue
                            if u == 1 and first and gg:
                                pe.wait_ge(pv_copied, gg)
                            pe.wait_ge(exp_ready, 8 * i + (n0 + u))
                            weigh_values(8 * i + (n0 + u - 1), (u - 1) % 8, first and u == 1, False)
                            ahead(i, last, 2 * u + 1)

                    steps(0, True)
                    with pe.Fori(1, KC // 8 - 1) as i:
                        steps(i, False)
                    if gg + 1 == NG:
                        pe.wait_ge(on["w_summed"], 2)
                        nc.tensor.matmul(psum[:, 4, 0:2], ONES, WSUM, start=True, stop=True)\
                          .then_inc(on["w_total"], 1)
                    steps(KC // 8 - 1, False, True)
                    pe.wait_ge(exp_ready, n0 + KC)
                    weigh_values(n0 + KC - 1, KC - 1, False, True)

            def turn_context(gg):
                for qt in range(2):
                    last = nc.tensor.transpose(PX[:, qt * P:(qt + 1) * P], PVS[:, qt * P:(qt + 1) * P], IDENT)
                last.then_inc(pv_turned, 1)

            first_batch()
            pe.wait_ge(mask_step, 2 * NCH + 2)
            pe.wait_ge(ones_built, 3)
            nc.tensor.matmul(psum[0:1, 5, 0:1], FLAGF[:, 1:2], ONES[:, 0:1], start=True, stop=True)\
              .then_inc(mask_counted, 1)
            pe.wait_ge(mask_flagged, 1)
            any_masked = pe.value_load(FLAG, min_val=0, max_val=1)
            with pe.If(any_masked == 1):
                attend(True)
            with pe.Else():
                attend(False)
            pe.wait_ge(pv_copied, NG)
            pe.wait_ge(norm_step, 3 * (NG - 1))
            turn_context(NG - 1)

            turns = [1]

            def turn(src, need, sem_=None):
                pe.wait_ge(ht_ready, CT * turns[0])
                for c in range(CT):
                    for i in range(TT):
                        if c == 0 and sem_ is not None:
                            pe.wait_ge(sem_, need + i + 1)
                        last = nc.tensor.transpose(psum[:, 6 + c, i * P:(i + 1) * P],
                                                   src[:, i, c * P:(c + 1) * P], IDENT)
                    last.then_inc(ht_psum, 1)
                turns[0] += 1

            def turned():
                pe.wait_ge(ht_ready, CT * turns[0])

            def linear(out, weights, xs, m, name, width=P):
                n = len(xs)
                for k in range(n):
                    last = nc.tensor.matmul(out, weights[:, k, m * P:m * P + width], xs[k],
                                            start=(k == 0), stop=(k == n - 1))
                last.then_inc(on[name], 1)

            def bias_rows(outs, bias):
                for out in outs:
                    nc.tensor.matmul(out, ONES[0:1, :], bias, start=True, stop=False, skip_group_check=True)

            def linear_rows(out, lhs, weights, biased, name):
                n = len(lhs)
                for k in range(n):
                    last = nc.tensor.matmul(out, lhs[k], weights[:, k, :], start=(k == 0 and not biased),
                                            stop=(k == n - 1), skip_group_check=biased)
                last.then_inc(on[name], 1)

            def tok(ap, i):
                return [ap[:, k, i * P:(i + 1) * P] for k in range(ap.shape[1])]

            pe.wait_ge(on["rows_loaded"], 16)
            pe.wait_ge(exp_ready, NG * KC)
            bias_rows([psum[:, i, 0:256] for i in range(TT)], row("bo")[0:1, :])
            pe.wait_ge(norm_step, 3 * NG)
            turn(CTXN, 0)
            turned()
            pe.wait_ge(on["wo_loaded"], 32)
            for i in range(TT):
                linear_rows(psum[:, i, 0:256], tok(HTC, i), WO, True, "b_out")
            pe.wait_ge(on["mix_loaded"], 80)
            pe.wait_ge(on["bm_loaded"], 32)
            pe.wait_ge(on["w_quantised"], 1)
            for k in range(IT):
                for g in range(4):
                    last = nc.tensor.matmul(psum[32 * g:32 * g + 32, 4, 0:256], BMT[:, k, :], WHA[:, k, :],
                                            start=(k == 0), stop=(k == IT - 1), tile_position=(0, 32 * g),
                                            skip_group_check=True)
            last.then_inc(on["c_habm"], 1)
            turn(HS, TT, h_ready)
            turned()
            pe.wait_ge(on["x_ready"], TT)
            for j in range(8):
                if j == 4:
                    pe.wait_ge(on["c_habm_copied"], 1)
                linear(psum[:, j, :], WIN, [HTC[:, c, :] for c in range(CT)], (j + IT) % 8, "c_in")
            pe.wait_ge(on["c_a_weights"], 2 + IT * TAPS_A)
            pe.wait_ge(on["c_in_copied"], IT)
            for m in range(IT):
                last = nc.tensor.matmul(psum[0:DS, 1, 0:1], AW[:, m, :], col("dwa_b", m), start=(m == 0),
                                        stop=(m == IT - 1))
            last.then_inc(on["c_a"], 1)
            for m in range(IT):
                for k in range(TAPS_A):
                    src = VAL[:, m, :, 4 + k - LEFT_A:4 + k - LEFT_A + S]
                    last = nc.tensor.matmul(psum[32 * k:32 * k + 32, 0, :].rearrange("p (b n) -> p b n", b=B),
                                            AWK[:, m, k, :], src, start=(m == 0), stop=(m == IT - 1),
                                            tile_position=(0, 32 * k))
            last.then_inc(on["c_a"], 1)
            pe.wait_ge(on["c_a_copied"], 2)
            for m in range(2):
                pe.wait_ge(on["c_in_copied"], 6 + m)
                nc.tensor.matmul(psum[:, 5 + m, :], WHABM[:, m * P:(m + 1) * P], AS, start=True, stop=True)\
                  .then_inc(on["c_ha"], 1)
            for m in range(IT):
                linear(psum[:, 2 + m // 2, m % 2 * 256:(m % 2 + 1) * 256], WPW, [WHB[:, k, :] for k in range(IT)],
                       m, "c_hbpw")
            for m in range(2):
                for k in range(IT):
                    last = nc.tensor.matmul(psum[:, 1, 2 + m:3 + m], WHB[:, k, m * P:(m + 1) * P], col("pw_b", k),
                                            start=(k == 0), stop=(k == IT - 1))
            last.then_inc(on["c_hbpw"], 1)
            pe.wait_ge(on["c_hbpw_copied"], IT + 2)
            for k in range(IT):
                pe.wait_ge(on["c_silu"], k + 1)
                for m in range(2):
                    last = nc.tensor.matmul(psum[:, m, :], WHBPW[:, k, m * P:(m + 1) * P], SB[:, k, :],
                                            start=(k == 0), stop=(k == IT - 1), skip_group_check=True)
                    if k == IT - 1:
                        last.then_inc(on["c_hb"], 1)
            pe.wait_ge(on["c_ha_copied"], 2)
            pe.wait_ge(on["c_hb_copied"], 2)
            for m in range(IT):
                linear(psum[:, m, :], WFU, [YC[:, k, :] for k in range(IT)], m, "c_fuse")
            pe.wait_ge(on["c_in_copied"], 8)
            bias_rows([psum[:, 4 + i, 0:256] for i in range(TT)], row("out_b")[0:1, :])
            pe.wait_ge(on["c_gated"], IT)
            for i in range(TT):
                linear_rows(psum[:, 4 + i, 0:256], tok(YG, i), WOUT, True, "c_out")

            pe.wait_ge(on["x_ready"], 2 * TT)
            for c in range(CT):
                for i in range(TT):
                    if c == 0:
                        pe.wait_ge(on["d_quant"], i + 1)
                    last = nc.tensor.transpose(psum[:, 6 + c, i * 64:(i + 1) * 64].bitcast(BF16),
                                               HQ[:, i, c * P:(c + 1) * P], IDENTB)
                last.then_inc(on["d_turned"], 1)
            pe.wait_ge(on["d_turned_copied"], CT)
            pe.wait_ge(on["w_quantised"], 6)
            for n in range(8):
                i, half = n // 2, n % 2
                for c in range(CT):
                    last = nc.tensor.matmul(psum[:, n, :], HQT[:, c, i * P:(i + 1) * P],
                                            TW1[:, c, half * 512:(half + 1) * 512], start=(c == 0), stop=(c == 1))
                last.then_inc(on["d_up"], 1)
            pe.wait_ge(on["d_hidden"], 8)
            for i in range(TT):
                pe.wait_ge(on["d_quant2"], i + 1)
                for k in range(FT):
                    last = nc.tensor.transpose(psum[:, 4 + i, k * 64:(k + 1) * 64].bitcast(BF16),
                                               QH[:, i, k * P:(k + 1) * P], IDENTB)
                last.then_inc(on["d_turned2"], 1)
            for i in range(TT):
                pe.wait_ge(on["d_turned2_copied"], i + 1)
                linear_rows(psum[:, i, 0:256], tok(QHT, i), TW2, False, "d_down")

            turn(HLE, 2 * TT, h_ready)
            turned()
            pe.wait_ge(on["l1w_loaded"], 48)
            pe.wait_ge(on["x_ready"], 3 * TT)
            hs = [HTE[:, c, :] for c in range(CT)]
            for f in range(CT):
                linear(psum[:, f, :], WQ1, hs, f, "e_q")
            pe.wait_ge(on["e_q_copied"], CT)
            for c in range(CT):
                linear(psum[:, 2 + c, :], WK1, [QE[:, k, :] for k in range(CT)], c, "e_qc")
            for i in range(TT):
                for k in range(CT):
                    last = nc.tensor.matmul(psum[:, 4, i:i + 1], QE[:, k, i * P:(i + 1) * P], col("bk1", k),
                                            start=(k == 0), stop=(k == CT - 1))
            last.then_inc(on["e_cq"], 1)
            pe.wait_ge(on["e_qc_copied"], CT)

            def key_scores(w):
                pe.wait_ge(on[f"ctxt_loaded{w // 2}"], 16)
                for n in range(8):
                    if 8 * w + n >= 4:
                        pe.wait_ge(on["e_masked"], 8 * w + n - 3)
                    for c in range(CT):
                        last = nc.tensor.matmul(psum[:, n % 4, :], QC[:, c, w * P:(w + 1) * P],
                                                CTXT[w // 2][:, c, n * 512:(n + 1) * 512],
                                                start=(c == 0), stop=(c == CT - 1))
                    last.then_inc(on["e_scores"], 1)

            def turn_exps(w):
                pe.wait_ge(on["e_exp"], w + 1)
                if w == 0:
                    pe.wait_ge(on["e_cq_copied"], 1)
                for n in range(8):
                    m = 4 * w + n // 2
                    if m:
                        pe.wait_ge(on["e_turned_a" if n % 2 == 0 else "e_turned_v"], m)
                    for j in range(4):
                        k = 4 * n + j
                        last = nc.tensor.transpose(psum[:, 4 + n % 2, j * P:(j + 1) * P],
                                                   PE1[w % 2][:, k * P:(k + 1) * P], IDENT)
                    last.then_inc(on["e_turned"], 1)

            def weigh_context(w):
                pe.wait_ge(on[f"ctxk_loaded{w // 2}"], 16)
                if w:
                    pe.wait_ge(on["e_normed"], w)
                for k in range(KC):
                    if k % 8 == 0:
                        pe.wait_ge(on["e_turned_a"], 4 * w + k // 8 + 1)
                        pe.wait_ge(on["e_turned_v"], 4 * w + k // 8 + 1)
                    last = nc.tensor.matmul(psum[:, 6, 0:256], PT1[:, k * P:(k + 1) * P], CTXK[w // 2][:, k, :],
                                            start=(k == 0), stop=(k == KC - 1))
                last.then_inc(on["e_att"], 1)

            key_scores(0)
            for w in range(4):
                if w < 3:
                    key_scores(w + 1)
                turn_exps(w)
                weigh_context(w)
            pe.wait_ge(on["bv1_loaded"], 16)
            pe.wait_ge(on["e_masked"], 32)
            bias_rows([psum[:, i, 0:256] for i in range(TT)], BV[0:1, :])
            pe.wait_ge(on["e_normed"], 4)
            turn(AO, 0)
            turned()
            for i in range(TT):
                linear_rows(psum[:, i, 0:256], tok(HTE, i), WV1, True, "e_out")

            turn(HLE, 3 * TT, h_ready)
            turned()
            pe.wait_ge(on["qkv_loaded"], 48)

            def project(which, first_wait):
                for n in range(8):
                    i, half = n // 2, n % 2
                    first_wait(n)
                    bank = VALUE_BANKS[n % 5] if which == 2 else n
                    for c in range(CT):
                        last = nc.tensor.matmul(psum[:, bank, :], HTF[:, c, i * P:(i + 1) * P],
                                                WQKV[which][:, c, half * HALF:(half + 1) * HALF],
                                                start=(c == 0), stop=(c == CT - 1))
                    last.then_inc(on["f_qkv"], 1)

            def turn_heads(src, roped, free):
                for k in range(8):
                    free(k)
                    if k == 0:
                        pe.wait_ge(on["f_roped"], roped)
                    for i in range(TT):
                        last = nc.tensor.transpose(psum[:, k, i * P:(i + 1) * P], src[:, i, k * P:(k + 1) * P],
                                                   IDENT)
                    last.then_inc(on["f_turned"], 1)

            pe.wait_ge(on["x_ready"], 4 * TT)
            project(0, lambda n: None)
            project(1, lambda n: pe.wait_ge(on["f_rope_part"], 3 * (n + 1)))
            turn_heads(QTM, 8, lambda k: pe.wait_ge(on["f_rope_part"], 24 + 3 * (k + 1)))
            turn_heads(KTM, 16, lambda k: pe.wait_ge(on["f_turned_copied"], k + 1))

            def unit(n):
                b, h = n // HM, n % HM
                return b, h, 64 * (h % 2), h // 2

            def head_scores(n):
                b, h, p0, k = unit(n)
                if n >= 4:
                    pe.wait_ge(on["f_exp"], 2 * (n - 3))
                for qt in range(2):
                    last = nc.tensor.matmul(HEAD_SCORES[n % 4][:, qt * S:qt * S + keys(n, qt)],
                                            QT[p0:p0 + DM, k, b * S + qt * P:b * S + (qt + 1) * P],
                                            KT[p0:p0 + DM, k, b * S:b * S + keys(n, qt)], start=True, stop=True)
                last.then_inc(on["f_scores"], 1)

            def turn_weights(n):
                pe.wait_ge(on["f_scaled"], 2 * (n + 1))
                if n >= 2:
                    pe.wait_ge(on["f_pt_copied"], n - 1)
                at = 0
                for k in range(2):
                    for qt in range(2):
                        if k * P < keys(n, qt):
                            last = nc.tensor.transpose(psum[:, 2 + n % 2, at:at + P],
                                                       PM[n % 4][:, qt, k * P:(k + 1) * P], IDENT)
                            at += P
                last.then_inc(on["f_pt"], 1)

            def weigh_heads(pair):
                if pair >= 2:
                    pe.wait_ge(on["f_pv_copied"], pair - 1)
                pe.wait_ge(on["f_pt_copied"], 2 * pair + 2)
                for k in range(2):
                    for j in range(2):
                        n = 2 * pair + j
                        b, h, p0, _ = unit(n)
                        q0 = P if k and causal_head(n) else 0
                        last = nc.tensor.matmul(psum[p0:p0 + DM, 4 + pair % 2, q0:S],
                                                VTM[:, 2 * b + k, h * DM:(h + 1) * DM],
                                                PTM[n % 4][:, k * S:(k + 1) * S - q0], start=(k == 0), stop=(k == 1),
                                                skip_group_check=True)
                last.then_inc(on["f_pv"], 1)

            pe.wait_ge(on["f_turned_copied"], 16)
            for n in range(3):
                head_scores(n)

            def value_bank_copied(n):
                if n >= 5:
                    pe.wait_ge(on["f_v_copied"], n - 4)
            project(2, value_bank_copied)
            pe.wait_ge(on["f_v_copied"], 8)
            for n in range(32):
                if n + 3 < 32:
                    head_scores(n + 3)
                turn_weights(n)
                if n % 2 and n > 2:
                    weigh_heads((n - 3) // 2)
            weigh_heads(15)
            pe.wait_ge(on["wom_loaded"], 16)
            pe.wait_ge(on["f_pv_copied"], 16)
            for i in range(TT):
                linear_rows(psum[:, i, 0:256], tok(OT, i), WOM, False, "f_out")

            turn(HLE, 4 * TT, h_ready)
            turned()
            pe.wait_ge(on["emb_loaded"], 16)
            pe.wait_ge(on["x_ready"], 5 * TT)
            for i in range(TT):
                for c in range(CT):
                    last = nc.tensor.matmul(psum[:, 0, i * E:(i + 1) * E], HTF[:, c, i * P:(i + 1) * P], EMB[:, c, :],
                                            start=(c == 0), stop=(c == CT - 1))
            last.then_inc(on["g_logits"], 1)
            pe.wait_ge(on["g_chosen"], 1)
            pe.wait_ge(on["g_counters"], 2)
            for i in range(TT):
                for j in range(i + 1):
                    last = nc.tensor.matmul(psum[:, 1, i * E:(i + 1) * E], UPPER if j == i else ONESB,
                                            CHOSENB[:, j, :], start=(j == 0), stop=(j == i))
            last.then_inc(on["g_cum"], 1)
            for i in range(TT):
                pe.wait_ge(on["g_sel"], i + 1)
                for c in range(CT):
                    last = nc.tensor.matmul(psum[:, 2 + c, :], HLE[:, i, c * P:(c + 1) * P],
                                            SEL[:, i].rearrange("p e s -> p (e s)"), start=(i == 0),
                                            stop=(i == TT - 1), skip_group_check=True)
                    if i == TT - 1:
                        last.then_inc(on["g_xg"], 1)
            pe.wait_ge(on["g_selw"], TT)
            for k in range(4):
                bank = k % 2
                if k >= 2:
                    pe.wait_ge(on["g_selt_copied"], k - 1)
                for i in range(TT):
                    last = nc.tensor.transpose(psum[:, bank, i * P:(i + 1) * P],
                                               SELW[:, i, 2 * k:2 * k + 2, :].rearrange("p e s -> p (e s)"), IDENT)
                last.then_inc(on["g_selt"], 1)
            pe.wait_ge(on["g_xg_copied"], CT)
            pe.wait_ge(on["w1e_loaded"], 16 * CT)
            for m in range(IT):
                for e in range(E):
                    for c in range(CT):
                        last = nc.tensor.matmul(psum[:, 4 + m, e * CAP:(e + 1) * CAP],
                                                W1E[:, c, e, m * P:(m + 1) * P], XG[:, c, e * CAP:(e + 1) * CAP],
                                                start=(c == 0), stop=(c == CT - 1))
                last.then_inc(on["g_up"], 1)
            pe.wait_ge(on["g_up_copied"], IT)
            pe.wait_ge(on["w2e_loaded"], 16 * IT)
            for k in range(4):
                pe.wait_ge(on["g_selt_copied"], 4)
                for m in range(IT):
                    for e in (2 * k, 2 * k + 1):
                        half = e % 2
                        last = nc.tensor.matmul(psum[CAP * half:CAP * (half + 1), k, 0:256],
                                                INTER[:, m, e * CAP:(e + 1) * CAP], W2E[:, m, e, :],
                                                start=(m == 0), stop=(m == IT - 1), skip_group_check=True)
                last.then_inc(on["g_down"], 1)
            pe.wait_ge(on["g_down_copied"], 4)
            for i in range(TT):
                for k in range(4):
                    last = nc.tensor.matmul(psum[:, 4 + i, 0:256], SELT[:, k, i * P:(i + 1) * P], OE[:, k, :],
                                            start=(k == 0), stop=(k == 3))
                last.then_inc(on["g_out"], 1)


def constants():
    n = np.arange(P)
    freq = (1.0 / np.float32(10000.0) ** (np.arange(0, DM, 2, dtype=np.float32) / np.float32(DM))).astype(np.float32)
    angle = np.arange(S, dtype=np.float32)[:, None] * freq[None, :]
    sign = np.concatenate([-np.ones(DM // 2), np.ones(DM // 2)])
    cos = np.cos(np.concatenate([angle, angle], axis=1).astype(np.float64))
    sin = np.sin(np.concatenate([angle, angle], axis=1).astype(np.float64)) * sign
    later = np.arange(S)[None, :] > np.arange(S)[:, None]
    tables = {"upper": n[:, None] <= n[None, :], "slots": np.tile(np.arange(1, CAP + 1), (P, 1)),
              "experts": np.tile(np.arange(E) - E, (P, 1)),
              "cos": cos.reshape(2, P, DM).transpose(1, 0, 2).reshape(P, -1),
              "sin": sin.reshape(2, P, DM).transpose(1, 0, 2).reshape(P, -1),
              "causal": (later * -1e30).reshape(2, P, S).transpose(1, 0, 2).reshape(P, -1)}
    return np.ascontiguousarray(np.concatenate([tables[k].astype(np.float32) for k in CONSTS], axis=1))


def layout(inputs):
    a = {k: np.asarray(v) for k, v in inputs.items()}
    cols = {"bq": a["L0_xattn_bq"], "bk": a["L0_xattn_bk"], "in_b": a["L0_attn_in_b"],
            "dwa_b": a["L0_attn_dwa_b"], "sym_b": a["L0_attn_sym_b"], "pw_b": a["L0_attn_pw_b"],
            "ha_b": a["L0_attn_ha_b"], "hb_b": a["L0_attn_hb_b"], "fuse_b": a["L0_attn_fuse_b"],
            "norm_w": a["L0_attn_norm_w"],
            "dwa_k": a["L0_attn_dwa_k"].reshape(IT, P, TAPS_A).transpose(0, 2, 1),
            "sym_k": a["L0_attn_sym_k"].reshape(IT, P, TAPS_B).transpose(0, 2, 1),
            "bq1": a["L1_xattn_bq"], "bk1": a["L1_xattn_bk"]}
    rows = {"bo": a["L0_xattn_bo"], "out_b": a["L0_attn_out_b"], "g1": a["L0_ffn_ln1_g"],
            "b1": a["L0_ffn_ln1_b"], "w1b": a["L0_ffn_b1"], "g2": a["L0_ffn_ln2_g"], "b2": a["L0_ffn_ln2_b"],
            "w2b": a["L0_ffn_b2"], "bv": a["L0_xattn_bv"], "bv1": a["L1_xattn_bv"]}
    c = np.ascontiguousarray
    return {
        "x": c(a["x"].reshape(T, D)),
        "cols": c(np.concatenate([cols[n].reshape(COLS[n], P).T for n in COLS], axis=1)),
        "rows": c(np.concatenate([rows[n].reshape(1, -1) for n in ROW_NAMES], axis=1)),
        "wqT": c(a["L0_xattn_Wq"].T), "wkT": c(a["L0_xattn_Wk"].T), "wvT": c(a["L0_xattn_Wv"].T),
        "ctxT": c(a["ctx_1024"].transpose(0, 2, 1)),
        "mask": c(a["mask_1x1xSxS2_if1"].reshape(S, S2)),
        "A": c(a["L0_attn_A"]), "BmT": c(a["L0_attn_Bm"].T), "woT": c(a["L0_xattn_Wo"].T),
        "winT": c(a["L0_attn_in_w"].T), "wpw": c(a["L0_attn_pw_w"]), "whaT": c(a["L0_attn_ha_w"].T),
        "whbT": c(a["L0_attn_hb_w"].T), "wfuT": c(a["L0_attn_fuse_w"].T), "woutT": c(a["L0_attn_out_w"].T),
        "w1T": c(a["L0_ffn_w1"].T), "w2T": c(a["L0_ffn_w2"].T),
        "wq1T": c(a["L1_xattn_Wq"].T), "wk1": c(a["L1_xattn_Wk"]), "wv1T": c(a["L1_xattn_Wv"].T),
        "ctx": c(a["ctx_1024"]), "mask1": c(a["mask_SxS2_ff0"]),
        "wqm": c(a["L1_attn_Wq"]), "wkm": c(a["L1_attn_Wk"]), "wvm": c(a["L1_attn_Wv"]), "wom": c(a["L1_attn_Wo"]),
        "embT": c(a["L1_ffn_expert_embeddings"].T), "w1e": c(a["L1_ffn_first_linear"].transpose(0, 2, 1)),
        "w2e": c(a["L1_ffn_second_linear"].transpose(0, 2, 1)), "consts": constants(),
    }


def kernel(**inputs):
    import concourse.bacc as bacc
    from concourse.bass_utils import run_bass_kernel_spmd

    nc = bacc.Bacc("TRN2", target_bir_lowering=False, num_devices=1)
    arrays = layout(inputs)
    tensors = {name: nc.dram_tensor(name, a.shape, mybir.dt.from_np(a.dtype), kind="ExternalInput").ap()
               for name, a in arrays.items()}
    tensors["out"] = nc.dram_tensor("out", (T, D), F32, kind="ExternalOutput").ap()
    build(nc, tensors)
    got = run_bass_kernel_spmd(nc, [arrays], core_ids=[0])
    return got.results[0]["out"].reshape(B, S, D)
```
